# Optimizing a Trainium2 kernel written in Bass

```python
import numpy as np
import jax
import jax.numpy as jnp

def _softmax(x, axis=-1):
    return jax.nn.softmax(x, axis=axis)

def _gelu(x):
    return jax.nn.gelu(x, approximate=True)

def _silu(x):
    return jax.nn.silu(x)

def _sigmoid(x):
    return jax.nn.sigmoid(x)

def _layernorm(x, axis=-1, eps=1e-05):
    m = jnp.mean(x, axis=axis, keepdims=True)
    v = jnp.var(x, axis=axis, keepdims=True)
    return (x - m) / jnp.sqrt(v + eps)

def _scatter_add(tgt, idx, src, axis=0):
    return tgt.at[idx].add(src)

def _segment_sum(src, seg, n):
    return jax.ops.segment_sum(src, seg, n)
kernel_name = 'mk_adaln_d2_jaxref_r8_20d611'

def setup_inputs(seed: int=0):
    np.random.seed(seed)
    _w = jnp.asarray

    def _L0_attn_setup():
        import jax, jax.numpy as jnp
        import numpy as np
        B, T, D_IN, D_OUT = (2, 256, 256, 256)
        N_HEADS, N_KV_HEADS = (32, 8)
        HEAD_DIM = D_OUT // N_HEADS
        N_REP = N_HEADS // N_KV_HEADS
        ROPE_BASE = 10000.0

        def _rope_freqs(head_dim, length, base=ROPE_BASE):
            theta = 1.0 / base ** (jnp.arange(0, head_dim, 2, dtype=jnp.float32) / head_dim)
            pos = jnp.arange(length, dtype=jnp.float32)
            freqs = jnp.outer(pos, theta)
            return (jnp.cos(freqs), jnp.sin(freqs))

        def _apply_rope(x, cos, sin):
            half = x.shape[-1] // 2
            x1, x2 = (x[..., :half], x[..., half:])
            c = cos[None, None, :, :]
            s = sin[None, None, :, :]
            return jnp.concatenate([x1 * c - x2 * s, x2 * c + x1 * s], axis=-1)
        key = jax.random.key(seed)
        ks = jax.random.split(key, 5)
        scale = 1.0 / np.sqrt(D_IN)
        return {'x': jax.random.normal(ks[0], (B, T, D_IN), dtype=jnp.float32), 'Wq': jax.random.normal(ks[1], (D_IN, D_OUT), dtype=jnp.float32) * scale, 'Wk': jax.random.normal(ks[2], (D_IN, N_KV_HEADS * HEAD_DIM), dtype=jnp.float32) * scale, 'Wv': jax.random.normal(ks[3], (D_IN, N_KV_HEADS * HEAD_DIM), dtype=jnp.float32) * scale, 'Wo': jax.random.normal(ks[4], (D_OUT, D_OUT), dtype=jnp.float32) * scale}
    _L0_attn_in = _L0_attn_setup()

    def _L0_ffn_setup():
        import jax, jax.numpy as jnp
        import numpy as np
        B, S, D, H = (4, 256, 256, 1024)

        def fwht(x):
            orig_shape = x.shape
            n = orig_shape[-1]
            x = x.reshape(-1, n)
            h = 1
            while h < n:
                xb = x.reshape(-1, n // (2 * h), 2, h)
                a = xb[:, :, 0, :]
                b = xb[:, :, 1, :]
                x = jnp.stack([a + b, a - b], axis=2).reshape(-1, n)
                h *= 2
            scale = jnp.asarray(1.0 / np.sqrt(n), dtype=x.dtype)
            return (x * scale).reshape(orig_shape)
        key = jax.random.key(seed)
        kx, k1, k2, k3 = jax.random.split(key, 4)
        x = jax.random.normal(kx, (B, S, D), dtype=jnp.float32)
        W1 = jax.random.normal(k1, (H, D), dtype=jnp.float32) * (1.0 / np.sqrt(D))
        W2 = jax.random.normal(k2, (D, H), dtype=jnp.float32) * (1.0 / np.sqrt(H))
        W3 = jax.random.normal(k3, (H, D), dtype=jnp.float32) * (1.0 / np.sqrt(D))
        return {'x': x, 'W1': W1, 'W2': W2, 'W3': W3}
    _L0_ffn_in = _L0_ffn_setup()
    _L0_c = _w((lambda *s: np.random.randn(*s).astype(np.float32) * 0.05)(8, 256))
    _L0_wmod = _w((lambda *s: np.random.randn(*s).astype(np.float32) * 0.05)(256, 6 * 256) * 256 ** (-0.5))

    def _L1_attn_setup():
        import jax, jax.numpy as jnp
        import numpy as np
        B, S, DIN = (2, 256, 256)
        HQ, HKV, DH = (16, 1, 128)
        key = jax.random.key(seed)
        ks = jax.random.split(key, 9)
        sc_in = 1.0 / np.sqrt(DIN)
        sc_o = 1.0 / np.sqrt(HQ * DH)
        return {'q': jax.random.normal(ks[0], (B, S, DIN), dtype=jnp.float32), 'Wq': jax.random.normal(ks[1], (DIN, HQ * DH), dtype=jnp.float32) * sc_in, 'bq': jnp.zeros((HQ * DH,), dtype=jnp.float32), 'Wk': jax.random.normal(ks[2], (DIN, HKV * DH), dtype=jnp.float32) * sc_in, 'bk': jnp.zeros((HKV * DH,), dtype=jnp.float32), 'Wv': jax.random.normal(ks[3], (DIN, HKV * DH), dtype=jnp.float32) * sc_in, 'bv': jnp.zeros((HKV * DH,), dtype=jnp.float32), 'Wo': jax.random.normal(ks[4], (HQ * DH, DIN), dtype=jnp.float32) * sc_o, 'bo': jnp.zeros((DIN,), dtype=jnp.float32)}
    _L1_attn_in = _L1_attn_setup()

    def _L1_ffn_setup():
        import jax, jax.numpy as jnp
        import numpy as np
        from jax import lax
        H = 256
        I = 176
        E = 16
        TOP_K = 6
        IS = 2 * I

        def _swiglu(x, w13_, w2_):
            gu = x @ w13_.T
            g, u = jnp.split(gu, 2, axis=-1)
            return jax.nn.silu(g) * u @ w2_.T
        key = jax.random.key(seed)
        ks = jax.random.split(key, 6)
        return {'hidden_states': jax.random.normal(ks[0], (1, 256, H), jnp.float32), 'gate_w': jax.random.normal(ks[1], (E, H), jnp.float32) * 0.02, 'w13': jax.random.normal(ks[2], (E, 2 * I, H), jnp.float32) * 0.02, 'w2': jax.random.normal(ks[3], (E, H, I), jnp.float32) * 0.02, 'sw13': jax.random.normal(ks[4], (2 * IS, H), jnp.float32) * 0.02, 'sw2': jax.random.normal(ks[5], (H, IS), jnp.float32) * 0.02}
    _L1_ffn_in = _L1_ffn_setup()
    _L1_c = _w((lambda *s: np.random.randn(*s).astype(np.float32) * 0.05)(8, 256))
    _L1_wmod = _w((lambda *s: np.random.randn(*s).astype(np.float32) * 0.05)(256, 6 * 256) * 256 ** (-0.5))
    _d = {'L0_attn_x': _L0_attn_in['x'], 'L0_attn_Wq': _L0_attn_in['Wq'], 'L0_attn_Wk': _L0_attn_in['Wk'], 'L0_attn_Wv': _L0_attn_in['Wv'], 'L0_attn_Wo': _L0_attn_in['Wo'], 'L0_ffn_W1': _L0_ffn_in['W1'], 'L0_ffn_W2': _L0_ffn_in['W2'], 'L0_ffn_W3': _L0_ffn_in['W3'], 'L0_c': _L0_c, 'L0_wmod': _L0_wmod, 'L1_attn_Wq': _L1_attn_in['Wq'], 'L1_attn_bq': _L1_attn_in['bq'], 'L1_attn_Wk': _L1_attn_in['Wk'], 'L1_attn_bk': _L1_attn_in['bk'], 'L1_attn_Wv': _L1_attn_in['Wv'], 'L1_attn_bv': _L1_attn_in['bv'], 'L1_attn_Wo': _L1_attn_in['Wo'], 'L1_attn_bo': _L1_attn_in['bo'], 'L1_ffn_gate_w': _L1_ffn_in['gate_w'], 'L1_ffn_w13': _L1_ffn_in['w13'], 'L1_ffn_w2': _L1_ffn_in['w2'], 'L1_ffn_sw13': _L1_ffn_in['sw13'], 'L1_ffn_sw2': _L1_ffn_in['sw2'], 'L1_c': _L1_c, 'L1_wmod': _L1_wmod}
    _x0 = _d['L0_attn_x']
    _d['L0_attn_x'] = jax.random.normal(jax.random.fold_in(jax.random.key(seed), 1), (8, 256, 256), dtype=_x0.dtype)
    del _x0
    return _d

def reference(L0_attn_x, L0_attn_Wq, L0_attn_Wk, L0_attn_Wv, L0_attn_Wo, L0_ffn_W1, L0_ffn_W2, L0_ffn_W3, L0_c, L0_wmod, L1_attn_Wq, L1_attn_bq, L1_attn_Wk, L1_attn_bk, L1_attn_Wv, L1_attn_bv, L1_attn_Wo, L1_attn_bo, L1_ffn_gate_w, L1_ffn_w13, L1_ffn_w2, L1_ffn_sw13, L1_ffn_sw2, L1_c, L1_wmod):

    def _L0_attn_ref(x, Wq, Wk, Wv, Wo):
        import jax, jax.numpy as jnp
        import numpy as np
        B, T, D_IN, D_OUT = (2, 256, 256, 256)
        N_HEADS, N_KV_HEADS = (32, 8)
        HEAD_DIM = D_OUT // N_HEADS
        N_REP = N_HEADS // N_KV_HEADS
        ROPE_BASE = 10000.0

        def _rope_freqs(head_dim, length, base=ROPE_BASE):
            theta = 1.0 / base ** (jnp.arange(0, head_dim, 2, dtype=jnp.float32) / head_dim)
            pos = jnp.arange(length, dtype=jnp.float32)
            freqs = jnp.outer(pos, theta)
            return (jnp.cos(freqs), jnp.sin(freqs))

        def _apply_rope(x, cos, sin):
            half = x.shape[-1] // 2
            x1, x2 = (x[..., :half], x[..., half:])
            c = cos[None, None, :, :]
            s = sin[None, None, :, :]
            return jnp.concatenate([x1 * c - x2 * s, x2 * c + x1 * s], axis=-1)
        Bx, Tx, _ = x.shape
        cos, sin = _rope_freqs(HEAD_DIM, Tx)
        q = (x @ Wq).reshape(Bx, Tx, N_HEADS, HEAD_DIM).transpose(0, 2, 1, 3)
        k = (x @ Wk).reshape(Bx, Tx, N_KV_HEADS, HEAD_DIM).transpose(0, 2, 1, 3)
        v = (x @ Wv).reshape(Bx, Tx, N_KV_HEADS, HEAD_DIM).transpose(0, 2, 1, 3)
        q = _apply_rope(q, cos, sin)
        k = _apply_rope(k, cos, sin)
        k = jnp.repeat(k, N_REP, axis=1)
        v = jnp.repeat(v, N_REP, axis=1)
        scores = jnp.einsum('bhtd,bhsd->bhts', q, k)
        causal = jnp.triu(jnp.ones((Tx, Tx), dtype=bool), k=1)
        scores = jnp.where(causal[None, None], -jnp.inf, scores)
        attn = jax.nn.softmax(scores / np.sqrt(HEAD_DIM), axis=-1)
        ctx = jnp.einsum('bhts,bhsd->bthd', attn, v).reshape(Bx, Tx, D_OUT)
        return ctx @ Wo

    def _L0_ffn_ref(x, W1, W2, W3):
        import jax, jax.numpy as jnp
        import numpy as np
        B, S, D, H = (4, 256, 256, 1024)

        def fwht(x):
            orig_shape = x.shape
            n = orig_shape[-1]
            x = x.reshape(-1, n)
            h = 1
            while h < n:
                xb = x.reshape(-1, n // (2 * h), 2, h)
                a = xb[:, :, 0, :]
                b = xb[:, :, 1, :]
                x = jnp.stack([a + b, a - b], axis=2).reshape(-1, n)
                h *= 2
            scale = jnp.asarray(1.0 / np.sqrt(n), dtype=x.dtype)
            return (x * scale).reshape(orig_shape)
        up_gate = jnp.einsum('bsd,hd->bsh', x, W1)
        up_lin = jnp.einsum('bsd,hd->bsh', x, W3)
        hidden = jax.nn.silu(up_gate) * up_lin
        hidden = fwht(hidden)
        out = jnp.einsum('bsh,dh->bsd', hidden, W2)
        return out

    def _L1_attn_ref(q, Wq, bq, Wk, bk, Wv, bv, Wo, bo):
        import jax, jax.numpy as jnp
        import numpy as np
        B, S, DIN = (2, 256, 256)
        HQ, HKV, DH = (16, 1, 128)
        r = HQ // HKV
        lead = q.shape[:-1]
        k_lin = (q @ Wk + bk).reshape(*lead, HKV, DH)
        v_lin = (q @ Wv + bv).reshape(*lead, HKV, DH)
        qx = jnp.swapaxes(v_lin, -3, -2)
        kx = jnp.repeat(jnp.swapaxes(k_lin, -3, -2), r, axis=-3)
        vx = jnp.repeat(qx, r, axis=-3)
        scores = jnp.einsum('...jd,...id->...ji', qx, kx) / DH
        attn = jax.nn.softmax(scores, axis=-1)
        out = jnp.einsum('...jk,...kd->...jd', attn, vx)
        out = jnp.swapaxes(out, -3, -2).reshape(*lead, HQ * DH)
        return out @ Wo + bo

    def _L1_ffn_ref(hidden_states, gate_w, w13, w2, sw13, sw2):
        import jax, jax.numpy as jnp
        import numpy as np
        from jax import lax
        H = 256
        I = 176
        E = 16
        TOP_K = 6
        IS = 2 * I

        def _swiglu(x, w13_, w2_):
            gu = x @ w13_.T
            g, u = jnp.split(gu, 2, axis=-1)
            return jax.nn.silu(g) * u @ w2_.T
        B, S, Hd = hidden_states.shape
        x = hidden_states.reshape(-1, Hd)
        T = x.shape[0]
        scores = jax.nn.softmax(x @ gate_w.T, axis=-1)
        topk_w, topk_ids = lax.top_k(scores, TOP_K)
        topk_w = topk_w / (topk_w.sum(-1, keepdims=True) + 1e-20)
        combine = jnp.einsum('tk,tke->te', topk_w, jax.nn.one_hot(topk_ids, E, dtype=topk_w.dtype))

        def body(acc, ew):
            w13_e, w2_e, c_e = ew
            y = _swiglu(x, w13_e, w2_e)
            return (acc + c_e[:, None] * y, None)
        out, _ = lax.scan(body, jnp.zeros_like(x), (w13, w2, combine.T))
        out = out + _swiglu(x, sw13, sw2)
        return out.reshape(B, S, Hd)
    x = L0_attn_x
    mod = (_silu(L0_c) @ L0_wmod).reshape(L0_c.shape[0], 6, 1, -1)
    sa, ca, ga, sb, cb, gb = (mod[:, 0], mod[:, 1], mod[:, 2], mod[:, 3], mod[:, 4], mod[:, 5])
    ga = (2 * (ga >= 0) - 1) * jnp.maximum(jnp.abs(ga), 0.25)
    gb = (2 * (gb >= 0) - 1) * jnp.maximum(jnp.abs(gb), 0.25)
    h = _layernorm(x, axis=-1) * (1 + ca) + sa
    x = x + ga * _L0_attn_ref(h, L0_attn_Wq, L0_attn_Wk, L0_attn_Wv, L0_attn_Wo)
    h = _layernorm(x, axis=-1) * (1 + cb) + sb
    x = x + gb * _L0_ffn_ref(h, L0_ffn_W1, L0_ffn_W2, L0_ffn_W3)
    mod = (_silu(L1_c) @ L1_wmod).reshape(L1_c.shape[0], 6, 1, -1)
    sa, ca, ga, sb, cb, gb = (mod[:, 0], mod[:, 1], mod[:, 2], mod[:, 3], mod[:, 4], mod[:, 5])
    ga = (2 * (ga >= 0) - 1) * jnp.maximum(jnp.abs(ga), 0.25)
    gb = (2 * (gb >= 0) - 1) * jnp.maximum(jnp.abs(gb), 0.25)
    h = _layernorm(x, axis=-1) * (1 + ca) + sa
    x = x + ga * _L1_attn_ref(h, L1_attn_Wq, L1_attn_bq, L1_attn_Wk, L1_attn_bk, L1_attn_Wv, L1_attn_bv, L1_attn_Wo, L1_attn_bo)
    h = _layernorm(x, axis=-1) * (1 + cb) + sb
    x = x + gb * _L1_ffn_ref(h, L1_ffn_gate_w, L1_ffn_w13, L1_ffn_w2, L1_ffn_sw13, L1_ffn_sw2)
    return x

_drawn_inputs = setup_inputs


def setup_inputs(seed=0):
    import zlib

    import numpy as np

    out = dict(_drawn_inputs(seed))
    spreads = {'L1_attn_bq': (0.0, 0.1),
     'L1_attn_bk': (0.0, 0.8),
     'L1_attn_bv': (0.0, 0.295),
     'L1_attn_bo': (0.0, 0.337)}
    factors = {'L1_attn_Wk': 8.0,
     'L1_attn_Wv': 3.378,
     'L1_ffn_gate_w': 8.0,
     'L1_ffn_w13': 8.0,
     'L1_ffn_w2': 8.0,
     'L1_ffn_sw13': 8.0,
     'L1_ffn_sw2': 8.0}
    for name, (base, spread) in spreads.items():
        noise = np.random.default_rng([zlib.crc32(name.encode()), seed]).standard_normal(out[name].shape)
        drawn = base * np.exp(spread * noise) if base else spread * noise
        out[name] = jnp.asarray(drawn.astype(out[name].dtype))
    for name, factor in factors.items():
        out[name] = (out[name] * factor).astype(out[name].dtype)
    return out
```

```python
from contextlib import ExitStack

import concourse.bass as bass
from concourse import mybir
import numpy as np

F32 = mybir.dt.float32
F32R = mybir.dt.float32r
BF16 = mybir.dt.bfloat16
ALU = mybir.AluOpType
ACT = mybir.ActivationFunctionType
AX = mybir.AxisListType

P = 128
NB = 8
T = 256
D = 256
KC = D // P
TT = T // P
KV = 8
REP = 4
DH = 8
HID = 1024
HT = HID // P
EXP = 16
TOPK = 6
INNER = 176
SHARED = 2 * INNER
MOE = EXP * INNER + SHARED
MT = (MOE + P - 1) // P
HEADS1 = 16
SC0 = DH ** -0.5
SC1 = 1.0 / 128
EPS = 1e-5
MASK = -1e38
NC = EXP + 1

C_ID, C_HAD, C_MASK, C_COS, C_SIN = 0, P, 2 * P, 3 * P, 3 * P + T
C_ONES = C_SIN + T
C_ALL = C_ONES + 1
S_Q = C_ALL
S_K = S_Q + REP * 2 * P
S_ALL = S_K + 2 * 2 * P


def shape_constants():
    c = np.zeros((P, S_ALL), np.float32)
    c[:, C_ID:C_ID + P] = np.eye(P)
    had = np.ones((1, 1), np.float32)
    while had.shape[0] < P:
        had = np.block([[had, had], [had, -had]])
    c[:, C_HAD:C_HAD + P] = had
    t = np.arange(P)
    c[:, C_MASK:C_MASK + P] = np.where(t[None, :] > t[:, None], MASK, 0.0)
    theta = (1.0 / np.float32(10000.0) ** (np.arange(0, DH, 2, dtype=np.float32) / DH)).astype(np.float32)
    freqs = np.outer(np.arange(T, dtype=np.float32), theta).astype(np.float32)
    d = np.arange(P) % DH
    c[:, C_COS:C_COS + T] = np.cos(freqs).T[d % (DH // 2)]
    c[:, C_SIN:C_SIN + T] = np.sin(freqs).T[d % (DH // 2)] * np.where(d < DH // 2, -1.0, 1.0)[:, None]
    for g in range(4):
        for d in range(DH):
            for r in range(REP):
                row = 32 * g + DH * r + d
                q = S_Q + r * 2 * P + 32 * g + d
                c[row, q] = c[row, q + DH] = 1.0
                c[row, q + P + 2 * DH] = 1.0
            for h in range(2):
                row = 32 * h + DH * g + d
                k = S_K + h * 2 * P + 32 * g + d
                c[row, k] = c[row, k + 2 * DH] = 1.0
                c[row, k + P + DH] = 1.0
        c[32 * g + 3 * DH:32 * g + 3 * DH + 2, C_ONES] = 1.0
    return c


def expert_rows():
    s = np.zeros((2 * NC, MOE), np.float32)
    for e in range(EXP):
        s[e, e * INNER:(e + 1) * INNER] = s[NC + e, e * INNER:(e + 1) * INNER] = 1.0
    s[EXP, EXP * INNER:] = s[NC + EXP, EXP * INNER:] = 1.0
    return s


def spread(ap, axis, n):
    shape = list(ap.shape)
    shape[axis] = n
    return ap.to_broadcast(shape)


def wait(eng, sem, b, per, n):
    v = b * per + n
    if isinstance(v, int) and v <= 0:
        return
    eng.wait_ge(sem, v)


def stand(eng, turns):
    eng.sem_inc(turns, 1)


class Steps:

    def __init__(self, sem, per):
        self.sem, self.per, self.b, self.n = sem, per, 0, 0

    def start(self, b):
        assert self.n in (0, self.per), (self.sem.name if hasattr(self.sem, "name") else "", self.n, self.per)
        self.b, self.n = b, 0

    def __call__(self, eng, ins, hold=True):
        ins.then_inc(self.sem, 1)
        self.n += 1
        if hold:
            eng.wait_ge(self.sem, self.b * self.per + self.n)


def adaln_two_layers(nc, x, consts, selrows, cT, wmod, wq, wk, wv, wo, w13, w2, wk1, wv1, bcol1, wo1, bo1,
                     gate, gu, wd, wd_last, gate_rows, out):
    ctx = ExitStack()
    with ctx:
        def sb(name, shape, dt=F32):
            return ctx.enter_context(nc.sbuf_tensor(name, shape, dt))

        def sem(name):
            return ctx.enter_context(nc.semaphore(name))

        XA = sb("residual", [P, NB * TT, D])
        CON = sb("constants", [P, C_ALL])
        ident, had = CON[:, C_ID:C_ID + P], CON[:, C_HAD:C_HAD + P]
        cosT, sinT = CON[:, C_COS:C_COS + T], CON[:, C_SIN:C_SIN + T]
        ones24 = CON[:, C_ONES:C_ONES + 1]
        ident_b = sb("ident_bf16", [P, P], BF16)
        mask_b = sb("mask_bf16", [P, P], BF16)
        SELQ = sb("sel_q", [P, REP, 2, P], F32R)
        SELK = sb("sel_k", [P, 2, 2, P], F32R)
        WQ = sb("wq", [P, KC, 2, D])
        WK = sb("wk", [P, KC, 2, 64])
        WV = sb("wv", [P, KC, 64])
        WO = sb("wo", [P, KC, D])
        W2H = sb("w2_hadamard", [P, HT, D])
        GU = sb("moe_gate_up", [P, KC, 2, MOE])
        WD = sb("moe_down", [P, MT, D])
        WK1 = sb("wk1", [P, KC, P])
        WV1 = sb("wv1", [P, KC, P])
        BC1 = sb("bias_kv1", [P, 2])
        WO1 = sb("wo1_summed", [P, D])
        BO1 = sb("bo1", [P, D])
        GW = sb("gate_w", [P, KC, EXP])
        gu_flat = GU[:, :, :, :].rearrange("p k s m -> p (k s m)")
        wd_flat = WD[:, :, :].rearrange("p m d -> p (m d)")
        WMOD = wd_flat[:, 0:KC * 2 * 1536].rearrange("p (l k n) -> p l k n", l=2, k=KC)
        W2RAW = gu_flat[:, 0:HT * D].rearrange("p (a d) -> p a d", a=HT)
        W2PING = gu_flat[:, HT * D:2 * HT * D].rearrange("p (a d) -> p a d", a=HT)
        SELQK = gu_flat[:, 8192:8192 + S_ALL - S_Q]
        WO1RAW = gu_flat[:, 4096:4096 + HEADS1 * D].rearrange("p (h d) -> p h d", h=HEADS1)
        CT = sb("cond_T", [P, 2, KC, NB])
        CS = sb("cond_silu", [P, 2, KC, NB])
        MODC = sb("mod_cols", [P, 2, NB, 8])
        MB_ = [sb("mod_b_attn", [P, 4]), sb("mod_b_ffn", [P, 4])]
        GB_ = [sb("gate_b_attn", [P, D]), sb("gate_b_ffn", [P, D])]
        HALF = sb("minus_half", [P, TT])
        ST = [sb("bn_attn", [P, TT, 6]), sb("bn_ffn", [P, TT, 6])]
        MV = [sb("mv_attn", [P, TT, 2]), sb("mv_ffn", [P, TT, 2])]
        VE = [sb("ve_attn", [P, TT]), sb("ve_ffn", [P, TT])]
        RS = [sb("rstd_attn", [P, TT]), sb("rstd_ffn", [P, TT])]
        XN = [sb("xn_attn", [P, TT, D]), sb("xn_ffn", [P, TT, D])]
        HTT = [sb("hT_attn", [P, KC, T]), sb("hT_ffn", [P, KC, T])]
        RT = sb("rope_tmp", [P, 2, T])
        QR = sb("qk_rot", [P, 3, T])
        QH = sb("qk_high", [P, 3, T], F32R)
        QL = sb("qk_low", [P, 3, T], F32R)
        QST = sb("q_stack", [P, 2, REP, T], F32R)
        KST = sb("k_stack", [P, 2, T], F32R)
        VA = sb("v_aug", [P, TT, KV, 32])
        NM = sb("minus_max", [P, TT, 2, 4, REP])
        NMS = sb("minus_max_split", [P, TT, 4, 2, 2, REP], F32R)
        NMT = sb("minus_max_T", [64, T], F32)
        PR = [sb("probs0", [P, 6 * T]), sb("probs1", [P, 6 * T])]
        MODR = PR[0][0:NB, :]
        GR = PR[1][0:NB, 0:2 * D].rearrange("b (s d) -> b s d", s=2)
        GT = PR[1][0:NB, 2 * D:4 * D].rearrange("b (s d) -> b s d", s=2)
        OS = sb("ctx_raw", [P, KV, T])
        RD = sb("recip_den", [P, TT, KV, REP])
        CX = sb("ctx", [P, TT, D])
        CXT = sb("ctx_T", [P, KC, T])
        TH = [sb("tanh0", [P, T]), sb("tanh1", [P, T])]
        AG = [sb("act0", [P, T]), sb("act1", [P, T])]
        HB = [sb("hid0", [P, T]), sb("hid1", [P, T])]
        KT1, VT1 = OS[:, 0, :], OS[:, 1, :]
        V1 = OS[:, 2, :].rearrange("p (i d) -> p i d", i=TT)
        P1 = OS[:, 4:6, :]
        PT1 = OS[:, 6:8, :]
        OT1 = OS[:, 3, :]
        NM1 = RD[:, 0, 0, 0:2]
        NMB1 = RD[:, 0, 1, 0:2]
        DEN1 = sb("den1", [P, 2])
        RDN1 = RD[:, 0, 2, 0:2]
        LMX = sb("r_max", [P, TT])
        SE = sb("r_exp", [P, TT, EXP])
        ZZ = sb("r_sum", [P, TT])
        RZ = sb("r_rsum", [P, TT])
        S18 = sb("r_scores", [P, TT, EXP + 2])
        M8 = sb("r_top8", [P, TT, 8])
        RP = sb("r_replaced", [P, TT, EXP + 2])
        CW = sb("r_combine", [P, TT, NC])
        WS = sb("r_wsum", [P, TT])
        CSP = sb("r_split", [P, TT, 2, NC], F32R)
        CTT = sb("r_split_T", [2 * NC, T], F32R)

        with nc.sbuf_tensor("w13", [P, KC, 2, HID], F32) as W13:
            pass
        SELC = sb("sel_expert", [2 * NC, MOE], F32R)
        SELRAW = [(0, PR[0][0:2 * NC, :]), (6 * T, PR[1][0:2 * NC, :]), (12 * T, OS[0:2 * NC, 0, 0:MOE - 12 * T])]

        PS = ctx.enter_context(nc.psum_tensor("psum", [P, 8, 512], F32))
        SPA = PS[:, 0:2, :].rearrange("p b n -> p (b n)")
        SPB = PS[:, 2, :]
        ring = [PS[:, i, :] for i in range(4)]
        OP = PS[:, 4, :]
        GUP = [PS[:, 5, :], PS[:, 6, :]]
        FO = PS[:, 7, :]
        CTX = [OP, ring[3]]
        CB = [OP, ring[0]]

        d_x, d_con, d_w0, d_ffn, d_w2, d_mod, d_wo1, d_sel, d_gu, d_wd, d_l1 = (
            sem(n) for n in ("ld_x", "ld_constants", "ld_attn0", "ld_w13", "ld_w2raw", "ld_wmod", "ld_wo1raw",
                             "ld_selraw", "ld_moe_gu", "ld_moe_down", "ld_attn1"))
        gates_stored, out_stored = sem("gates_stored"), sem("out_stored")
        dve_setup, pool_setup, act_setup = sem("dve_setup"), sem("pool_setup"), sem("act_setup")
        cs_ready, mod_ps, mod_sb, modT_ps, modc_ready = (sem(n) for n in (
            "cond_ready", "mod_in_psum", "mod_in_sbuf", "modT_in_psum", "mod_cols_ready"))
        gr_ready, w2_ps, w2_ping, w2_done, wo1_done, selraw_used, consts_ready, selc_ready = (sem(n) for n in (
            "gate_rows_ready", "w2_in_psum", "w2_evacuated", "w2_ready", "wo1_ready", "selraw_used",
            "consts_ready", "selc_ready"))

        def names(layer, which):
            return {n: sem(f"{n}_{layer}{which}") for n in (
                "dve", "pool", "act", "gate_in", "mv", "rstd", "xn", "xnT", "hT", "x_done")}

        turns = {e: sem("turns_" + e) for e in ("dve", "pe", "pool")}
        block = ctx.enter_context(nc.Block())

        L = [dict(attn=names(0, "a"), ffn=names(0, "f")), dict(attn=names(1, "a"), ffn=names(1, "f"))]
        s = {n: sem(n) for n in (
            "q_ps", "k_ps", "v_ps", "rope_done", "qk_split", "v_done", "kst_ps", "kst_done", "qst_ps",
            "qst_act", "qst_dve", "s_ps", "max_done", "nm_split", "nmT_ps", "nmT_done", "rows_in",
            "st_ps", "exp_done", "masked", "pv_ps", "o_done", "oT_ps", "ctx_done", "ctxT_ps", "ctxT_done",
            "wo_ps", "wo_read",
            "gu0_ps", "tanh0", "hid0", "down0_used", "ffn0_read",
            "kv1_ps", "kv1_done", "v1T_ps", "v1_done", "s1_ps", "nmb1", "exp1", "p1_norm", "pT1_ps", "pT1_done",
            "o1_ps", "o1_done", "wo1_ps", "wo1_read",
            "lg_ps", "lmax", "lexp", "csplit", "cT_ps", "cT_done", "gu1_ps", "cb_ps", "tanh1", "hid1",
            "down1_used", "ffn1_read")}
        ch = {k: sem("steps_" + k) for k in ("dve_a0", "dve_f0", "dve_a1", "dve_f1", "pool_0a", "pool_0f",
                                             "pool_1a", "pool_1f")}

        def xtile(b, tt):
            return XA[:, b * TT + tt, :] if isinstance(b, int) else XA[:, bass.ds(b * TT + tt, 1), :].rearrange("p a d -> p (a d)")

        def xboth(b):
            return XA[:, b * TT:(b + 1) * TT, :] if isinstance(b, int) else XA[:, bass.ds(b * TT, TT), :]

        def wide(eng, loop, layer):
            loop(0, None)
            loop(1, 0)
            with eng.Fori(2, NB) as i:
                loop(i, i - 1)
            loop(None, NB - 1)

        @block.sync
        def _(sp):
            sp.dma_start(CON[:, :], consts[:, 0:C_ALL]).then_inc(d_con, 16)
            sp.dma_start(CT[:, :, :, :], cT).then_inc(d_mod, 16)
            sp.dma_start(WMOD, wmod).then_inc(d_mod, 16)
            sp.dma_start(SELQK, consts[:, S_Q:S_ALL]).then_inc(d_con, 16)
            sp.dma_start(XA[:, :, :], x.rearrange("(n p) d -> p n d", p=P)).then_inc(d_x, 16)
            sp.dma_start(WQ[:, :, :, :], wq).then_inc(d_w0, 16)
            sp.dma_start(WK[:, :, :, :], wk).then_inc(d_w0, 16)
            sp.dma_start(WV[:, :, :], wv).then_inc(d_w0, 16)
            sp.dma_start(WO[:, :, :], wo).then_inc(d_w0, 16)
            sp.dma_start(W2RAW, w2).then_inc(d_w2, 16)
            for k in range(KC):
                sp.dma_start(W13[:, k, :, :], w13[:, k, :, :]).then_inc(d_ffn, 16)
            sp.dma_start(WO1RAW, wo1).then_inc(d_wo1, 16)
            sp.dma_start(WK1[:, :, :], wk1).then_inc(d_l1, 16)
            sp.dma_start(WV1[:, :, :], wv1).then_inc(d_l1, 16)
            sp.dma_start(BC1[:, :], bcol1).then_inc(d_l1, 16)
            sp.dma_start(BO1[:, :], spread(bo1.rearrange("(a d) -> a d", a=1), 0, P)).then_inc(d_l1, 16)
            sp.dma_start(GW[:, :, :], gate).then_inc(d_l1, 16)
            for l in range(2):
                sp.wait_ge(gr_ready, l + 1)
                sp.dma_start(gate_rows[l], GR[:, :, :]).then_inc(gates_stored, 16)
                sp.wait_ge(gates_stored, 16 * (l + 1))
            sp.wait_ge(wo1_done, 1)
            sp.wait_ge(w2_done, 1)
            sp.wait_ge(consts_ready, 1)
            for k in range(KC):
                for h in range(2):
                    sp.dma_start(GU[:, k, h, :], gu[:, k, h, :]).then_inc(d_gu, 16)
            sp.wait_ge(mod_ps, 6)
            full = MT - 1
            sp.dma_start(WD[:, 0:full, :], wd[:, :, :]).then_inc(d_wd, 16)
            sp.dma_start(WD[0:MOE - full * P, full, :], wd_last).then_inc(d_wd, 16)

            def gate_row(layer, side, b):
                n = L[layer]["attn" if side == 0 else "ffn"]
                wait(sp, n["x_done"], b, 1, 0)
                if isinstance(b, int):
                    src = gate_rows[layer, b:b + 1, side, :]
                else:
                    src = gate_rows[layer, bass.ds(b, 1), side, :]
                sp.dma_start(GB_[side][:, :], spread(src, 0, P)).then_inc(n["gate_in"], 16)

            def turn0(ia, jf):
                if jf is not None:
                    gate_row(0, 1, jf)
                if ia is not None:
                    gate_row(0, 0, ia)
                    wait(sp, s["nmT_done"], ia, 1, 1)
                    for g in range(4):
                        for hl in range(2):
                            row = 32 * g + 3 * DH + hl
                            sp.dma_start(
                                QST[row:row + 1, :, :, :].rearrange("p c r t -> p (c r) t").bitcast(F32),
                                NMT[16 * g + 8 * hl:16 * g + 8 * hl + 8, :]).then_inc(s["rows_in"], 16)

            def turn1(ia, jf):
                if jf is not None:
                    gate_row(1, 1, jf)
                if ia is not None:
                    gate_row(1, 0, ia)
                if jf is not None:
                    wait(sp, L[1]["ffn"]["x_done"], jf, 1, 1)
                    lo = jf * T
                    dst = out[lo:lo + T, :] if isinstance(jf, int) else out[bass.ds(lo, T), :]
                    sp.dma_start(dst.rearrange("(n p) d -> p n d", p=P), xboth(jf)).then_inc(out_stored, 16)

            wide(sp, turn0, 0)
            sp.wait_ge(L[0]["attn"]["x_done"], NB)
            sp.wait_ge(L[0]["ffn"]["x_done"], NB)
            for lo, buf in SELRAW:
                sp.dma_start(buf, selrows[:, lo:lo + buf.shape[1]]).then_inc(d_sel, 16)
            wide(sp, turn1, 1)
            sp.wait_ge(out_stored, 16 * NB)

        @block.gpsimd
        def _(po):
            n = [0]

            def step(ins):
                n[0] += 1
                ins.then_inc(pool_setup, 1)
                po.wait_ge(pool_setup, n[0])

            step(po.memset(HALF[:, :], -0.5))
            po.wait_ge(d_wo1, 16)
            h = HEADS1 // 2
            while h > 1:
                step(po.tensor_tensor(WO1RAW[:, 0:h, :], WO1RAW[:, 0:h, :], WO1RAW[:, h:2 * h, :], ALU.add))
                h //= 2
            po.tensor_tensor(WO1[:, :], WO1RAW[:, 0, :], WO1RAW[:, 1, :], ALU.add).then_inc(wo1_done, 1)

            def norm(layer, which, b):
                side = 0 if which == "attn" else 1
                m = L[layer][which]
                st = Steps(ch[f"pool_{layer}{which[0]}"], 1)
                st.start(b)
                wait(po, m["mv"], b, 1, 1)
                wait(po, m["xn"], b, 1, 0)
                stand(po, turns["pool"])
                st(po, po.tensor_scalar(VE[side][:, :], MV[side][:, :, 1], EPS, None, ALU.add))
                po.tensor_tensor(RS[side][:, :], VE[side][:, :], HALF[:, :], ALU.pow).then_inc(m["rstd"], 1)

            def turn0(ia, jf):
                if jf is not None:
                    norm(0, "ffn", jf)
                if ia is not None:
                    norm(0, "attn", ia)
                    for g in range(KV):
                        wait(po, s["exp_done"], ia, 2 * KV, 2 * g + 2)
                        stand(po, turns["pool"])
                        pa = PR[g % 2][:, 0:4 * T].rearrange("p (r t) -> p r t", r=REP)[:, :, 0:P]
                        pb = PR[g % 2][:, 4 * T:6 * T].rearrange("p (r t) -> p r t", r=REP)
                        po.affine_select(out=pa, in_=pa, compare_op=ALU.is_ge, fill=0.0, base=0,
                                         pattern=[[0, REP], [1, P]], channel_multiplier=-1).then_inc(s["masked"], 1)
                        po.affine_select(out=pb, in_=pb, compare_op=ALU.is_ge, fill=0.0, base=0,
                                         pattern=[[0, REP], [1, P]], channel_multiplier=-1).then_inc(s["masked"], 1)

            def turn1(ia, jf):
                if jf is not None:
                    norm(1, "ffn", jf)
                if ia is not None:
                    norm(1, "attn", ia)

            wide(po, turn0, 0)
            wide(po, turn1, 1)

        @block.scalar
        def _(act):
            act.wait_ge(d_mod, 32)
            nc.scalar.activation(CS[:, :, :, :], CT[:, :, :, :], ACT.Tanh, scale=0.5).then_inc(act_setup, 1)
            act.wait_ge(w2_ps, 1)
            nc.scalar.activation(W2PING.rearrange("p a d -> p (a d)"), PS[:, 4:8, :].rearrange("p b n -> p (b n)"),
                                 ACT.Copy, scale=1.0 / 64).then_inc(w2_ping, 1)

            def turn0(ia, jf):
                if jf is not None:
                    tanh0(jf, 0)
                if ia is not None:
                    b = ia
                    if isinstance(b, int) and b == 0:
                        act.wait_ge(gates_stored, 32)
                        act.wait_ge(consts_ready, 1)
                    wait(act, s["v_ps"], b, 1, 1)
                    wait(act, s["pv_ps"], b, KV, 0)
                    nc.scalar.activation(VA[:, :, :, 0:DH], ring[3][:, 0:2 * 64].rearrange("p (t g d) -> p t g d", t=TT, g=KV),
                                         ACT.Copy).then_inc(s["v_done"], 1)
                    wait(act, s["kst_ps"], b, 1, 1)
                    nc.scalar.activation(KST[:, :, :].rearrange("p c t -> p (c t)"), ring[2], ACT.Identity,
                                         bias=ones24).then_inc(s["kst_done"], 1)
                    for m, bank in ((0, 0), (2, 3)):
                        wait(act, s["qst_ps"], b, 4, m + 1)
                        nc.scalar.activation(QST[:, m // 2, 0:2, :].rearrange("p r t -> p (r t)"), ring[bank],
                                             ACT.Copy).then_inc(s["qst_act"], 1)
                    for j in range(1, HT // 2 + 1):
                        if jf is not None:
                            tanh0(jf, j)
                    wait(act, s["nmT_ps"], b, 1, 1)
                    wait(act, s["rows_in"], b, 128, 0)
                    nc.scalar.activation(NMT[:, :], ring[3][0:64, 0:T], ACT.Copy).then_inc(s["nmT_done"], 1)
                    for g in range(KV):
                        wait(act, s["pv_ps"], b, KV, g - 1)
                        wait(act, s["st_ps"], b, 2 * KV, 2 * g + 1)
                        nc.scalar.activation(PR[g % 2][:, 0:4 * T], SPA, ACT.Exp, scale=SC0).then_inc(s["exp_done"], 1)
                        wait(act, s["st_ps"], b, 2 * KV, 2 * g + 2)
                        nc.scalar.activation(PR[g % 2][:, 4 * T:6 * T], SPB, ACT.Exp, scale=SC0).then_inc(s["exp_done"], 1)
                        if jf is not None and g % 2 == 1 and g < KV - 1:
                            tanh0(jf, HT // 2 + 1 + g // 2)
                    wait(act, s["ctxT_ps"], b, 1, 1)
                    nc.scalar.activation(CXT[:, :, :].rearrange("p k t -> p (k t)"), ring[0], ACT.Copy).then_inc(s["ctxT_done"], 1)
                elif jf is not None:
                    for j in range(1, HT):
                        tanh0(jf, j)

            def tanh0(b, j):
                wait(act, s["gu0_ps"], b, HT, j + 1)
                wait(act, s["hid0"], b, HT, j - 1)
                nc.scalar.activation(TH[j % 2][:, :], GUP[j % 2][:, 0:T], ACT.Tanh, scale=0.5).then_inc(s["tanh0"], 1)

            wide(act, turn0, 0)

            def tanh1(b, j):
                rows = min(P, MOE - j * P)
                wait(act, s["gu1_ps"], b, MT, j + 1)
                wait(act, s["hid1"], b, MT, j - 1)
                nc.scalar.activation(TH[j % 2][0:rows, :], GUP[j % 2][0:rows, 0:T], ACT.Tanh, scale=0.5).then_inc(s["tanh1"], 1)

            def router(b):
                wait(act, s["lmax"], b, 1, 1)
                for tt in range(TT):
                    nc.scalar.activation(SE[:, tt, :], FO[:, tt * EXP:(tt + 1) * EXP], ACT.Exp, bias=LMX[:, tt:tt + 1],
                                         accum_out=ZZ[:, tt:tt + 1]).then_inc(s["lexp"], 1)
                wait(act, s["cT_ps"], b, 1, 1)
                nc.scalar.activation(CTT[:, :], OP[0:2 * NC, 0:T], ACT.Copy).then_inc(s["cT_done"], 1)

            def attn1(b, k):
                if k == 0:
                    wait(act, s["kv1_ps"], b, 1, 1)
                    nc.scalar.activation(KT1, ring[1][:, 0:T], ACT.Identity, bias=BC1[:, 0:1]).then_inc(s["kv1_done"], 1)
                    nc.scalar.activation(VT1, ring[1][:, T:2 * T], ACT.Identity, bias=BC1[:, 1:2]).then_inc(s["kv1_done"], 1)
                if k == 1:
                    wait(act, s["v1T_ps"], b, 1, 1)
                    nc.scalar.activation(V1.rearrange("p i d -> p (i d)"), ring[2][:, 0:T], ACT.Copy).then_inc(s["v1_done"], 1)
                if k == 2:
                    wait(act, s["nmb1"], b, 1, 1)
                    for tt in range(TT):
                        nc.scalar.activation(P1[:, tt, :], ring[3][:, tt * T:(tt + 1) * T], ACT.Exp, scale=SC1,
                                             bias=NMB1[:, tt:tt + 1], accum_out=DEN1[:, tt:tt + 1]).then_inc(s["exp1"], 1)
                if k == 3:
                    wait(act, s["pT1_ps"], b, 1, 1)
                    nc.scalar.activation(PT1.rearrange("p i t -> p (i t)"), ring[3], ACT.Copy).then_inc(s["pT1_done"], 1)
                if k == 4:
                    wait(act, s["o1_ps"], b, 1, 1)
                    nc.scalar.activation(OT1, ring[1][:, 0:T], ACT.Copy).then_inc(s["o1_done"], 1)

            def turn1(ia, jf):
                if jf is not None:
                    router(jf)
                for j in range(MT):
                    if jf is not None:
                        tanh1(jf, j)
                    if ia is not None and j % 4 == 3 and j // 4 < 5:
                        attn1(ia, j // 4)

            wide(act, turn1, 1)

        @block.vector
        def _(dve):
            n = [0]

            def step(ins, hold=True):
                n[0] += 1
                ins.then_inc(dve_setup, 1)
                if hold:
                    dve.wait_ge(dve_setup, n[0])

            dve.memset(S18[:, :, :], -1.0)
            dve.memset(CW[:, :, :], 0.5)
            step(dve.memset(VA[:, :, :, :], 0.0))
            step(dve.memset(VA[:, :, :, DH:DH + 1], 1.0))
            dve.wait_ge(d_con, 32)
            dve.tensor_copy(ident_b[:, :], ident)
            dve.tensor_copy(mask_b[:, :], CON[:, C_MASK:C_MASK + P])
            dve.tensor_copy(SELQ[:, :, :, :], SELQK[:, 0:S_K - S_Q].rearrange("p (r h n) -> p r h n", r=REP, h=2))
            dve.tensor_copy(SELK[:, :, :, :], SELQK[:, S_K - S_Q:S_ALL - S_Q].rearrange("p (c h n) -> p c h n", c=2, h=2))\
                .then_inc(consts_ready, 1)
            dve.wait_ge(act_setup, 1)
            step(dve.scalar_tensor_tensor(CS[:, :, :, :].rearrange("p l k b -> p (l k b)"),
                                          CS[:, :, :, :].rearrange("p l k b -> p (l k b)"), 1.0,
                                          CT[:, :, :, :].rearrange("p l k b -> p (l k b)"), ALU.add, ALU.mult))
            dve.tensor_scalar(CS[:, :, :, :], CS[:, :, :, :], 0.5, None, ALU.mult).then_inc(cs_ready, 1)
            for l in range(2):
                for c in range(3):
                    dve.wait_ge(mod_ps, 3 * l + c + 1)
                    if l == 1 and c == 0:
                        dve.wait_ge(modT_ps, 1)
                    dve.tensor_copy(MODR[:, c * 512:(c + 1) * 512], ring[c][0:NB, :]).then_inc(mod_sb, 1)
                dve.wait_ge(mod_sb, 3 * l + 3)
                g = MODR[:, :].rearrange("p (a c d) -> p a c d", a=2, c=3)[:, :, 2, :]
                step(dve.scalar_tensor_tensor(GT[:, :, :], g, -1.0, g, ALU.mult, ALU.max))
                step(dve.tensor_scalar(GT[:, :, :], GT[:, :, :], 0.25, None, ALU.max))
                if l == 1:
                    dve.wait_ge(gates_stored, 16)
                step(dve.tensor_scalar(GR[:, :, :], g, 0.0, 2.0, ALU.is_ge, ALU.mult))
                step(dve.tensor_scalar(GR[:, :, :], GR[:, :, :], -1.0, None, ALU.add))
                dve.tensor_tensor(GR[:, :, :], GR[:, :, :], GT[:, :, :], ALU.mult).then_inc(gr_ready, 1)
                dve.wait_ge(modT_ps, l + 1)
                mt = ring[3][:, 0:64].rearrange("p (a s k b) -> p a s k b", a=2, s=2, k=KC)
                mc = MODC[:, l, :, :].rearrange("p b (a s k) -> p a s k b", a=2, s=2)
                for a in range(2):
                    dve.tensor_copy(mc[:, a, 0, :, :], mt[:, a, 0, :, :])
                    ins = dve.tensor_scalar(mc[:, a, 1, :, :], mt[:, a, 1, :, :], 1.0, None, ALU.add)
                ins.then_inc(modc_ready, 1)
            dve.wait_ge(w2_ping, 1)
            src, dst = W2PING, W2H[:, :, :]
            for h in (1, 2, 4):
                v = src.rearrange("p (n s h) d -> p n s (h d)", s=2, h=h)
                o = dst.rearrange("p (n s h) d -> p n s (h d)", s=2, h=h)
                dve.tensor_tensor(o[:, :, 0, :], v[:, :, 0, :], v[:, :, 1, :], ALU.add)
                ins = dve.tensor_tensor(o[:, :, 1, :], v[:, :, 0, :], v[:, :, 1, :], ALU.subtract)
                if h < 4:
                    step(ins)
                else:
                    ins.then_inc(w2_done, 1)
                src, dst = dst, src
            def norm(layer, which, b, st):
                side = 0 if which == "attn" else 1
                m = L[layer][which]
                mc = MODC[:, layer, b:b + 1, 4 * side:4 * side + 4] if isinstance(b, int) else \
                    MODC[:, layer, bass.ds(b, 1), 4 * side:4 * side + 4]
                dve.tensor_copy(MB_[side][:, :], mc.rearrange("p a c -> p (a c)"))
                if which == "ffn":
                    wait(dve, L[layer]["attn"]["x_done"], b, 1, 1)
                elif layer == 1:
                    wait(dve, L[0]["ffn"]["x_done"], b, 1, 1)
                for tt in range(TT):
                    ins = dve.bn_stats(ST[side][:, tt, :], xtile(b, tt))
                st(dve, ins)
                stand(dve, turns["dve"])
                dve.bn_aggr(MV[side][:, 0, :], ST[side][:, 0, :])
                dve.bn_aggr(MV[side][:, 1, :], ST[side][:, 1, :]).then_inc(m["mv"], 1)
                wait(dve, m["mv"], b, 1, 1)
                wait(dve, m["rstd"], b, 1, 1)
                wait(dve, m["xnT"], b, 1, 0)
                for tt in range(TT):
                    ins = dve.tensor_scalar(XN[side][:, tt, :], xtile(b, tt), MV[side][:, tt, 0:1],
                                            RS[side][:, tt:tt + 1], ALU.subtract, ALU.mult)
                ins.then_inc(m["xn"], 1)

            def modulate(layer, which, b):
                side = 0 if which == "attn" else 1
                m = L[layer][which]
                wait(dve, m["xnT"], b, 1, 1)
                bank = (ring[3] if side == 0 else GUP[0])
                for k in range(KC):
                    ins = dve.tensor_scalar(HTT[side][:, k, :], bank[:, k * T:(k + 1) * T], MB_[side][:, 2 + k:3 + k],
                                            MB_[side][:, k:k + 1], ALU.mult, ALU.add)
                ins.then_inc(m["hT"], 1)

            def residual(layer, which, b, ps, st, filled, per, read, bias=None):
                side = 0 if which == "attn" else 1
                m = L[layer][which]
                Y = XN[side]
                g = spread(GB_[side][:, :].rearrange("p (a d) -> p a d", a=1), 1, TT)
                wait(dve, s[filled], b, per, per)
                wait(dve, m["gate_in"], b, 16, 16)
                src = ps.rearrange("p (t d) -> p t d", t=TT)
                if bias is not None:
                    dve.tensor_tensor(Y[:, :, :], src, spread(bias[:, :].rearrange("p (a d) -> p a d", a=1), 1, TT),
                                      ALU.add).then_inc(s[read], 1)
                    wait(dve, s[read], b, 1, 1)
                    st(dve, dve.tensor_tensor(Y[:, :, :], Y[:, :, :], g, ALU.mult))
                else:
                    dve.tensor_tensor(Y[:, :, :], src, g, ALU.mult).then_inc(s[read], 1)
                    wait(dve, s[read], b, 1, 1)
                dve.tensor_tensor(xboth(b), xboth(b), Y[:, :, :], ALU.add).then_inc(m["x_done"], 1)

            f0 = Steps(ch["dve_f0"], 1 + HT)
            a0 = Steps(ch["dve_a0"], 1 + 3 + 3 + 4)

            def hidden0(b, j, st):
                wait(dve, s["tanh0"], b, HT, j + 1)
                wait(dve, s["down0_used"], b, HT, j - 1)
                st(dve, dve.scalar_tensor_tensor(AG[j % 2][:, :], TH[j % 2][:, :], 1.0, GUP[j % 2][:, 0:T],
                                                 ALU.add, ALU.mult))
                dve.tensor_tensor(HB[j % 2][:, :], AG[j % 2][:, :], GUP[j % 2][:, T:2 * T], ALU.mult).then_inc(s["hid0"], 1)

            def turn0(ia, jf):
                if jf is not None:
                    f0.start(jf)
                    norm(0, "ffn", jf, f0)
                    modulate(0, "ffn", jf)
                    hidden0(jf, 0, f0)
                if ia is not None:
                    b = ia
                    a0.start(b)
                    norm(0, "attn", b, a0)
                    modulate(0, "attn", b)
                    for c in range(3):
                        rows = P if c < 2 else 64
                        ps = ring[c][0:rows, :]
                        if c < 2:
                            wait(dve, s["q_ps"], b, 2, c + 1)
                        else:
                            wait(dve, s["k_ps"], b, 1, 1)
                        dve.tensor_tensor(RT[0:rows, 0, :], ps[:, 0:T], cosT[0:rows, :], ALU.mult)
                        dve.tensor_tensor(RT[0:rows, 1, :], ps[:, T:2 * T], sinT[0:rows, :], ALU.mult).then_inc(s["rope_done"], 1)
                        wait(dve, s["rope_done"], b, 3, c + 1)
                        st_ = dve.tensor_tensor(QR[0:rows, c, :], RT[0:rows, 0, :], RT[0:rows, 1, :], ALU.add)
                        a0(dve, st_)
                        a0(dve, dve.tensor_copy(QH[0:rows, c, :], QR[0:rows, c, :]))
                        dve.tensor_tensor(QL[0:rows, c, :], QR[0:rows, c, :], QH[0:rows, c, :].bitcast(F32),
                                          ALU.subtract).then_inc(s["qk_split"], 1)
                    for m, bank in ((1, 1), (3, 2)):
                        wait(dve, s["qst_ps"], b, 4, m + 1)
                        dve.tensor_copy(QST[:, m // 2, 2:4, :].rearrange("p r t -> p (r t)"), ring[bank]).then_inc(s["qst_dve"], 1)
                if jf is not None and ia is None:
                    for j in range(1, HT):
                        hidden0(jf, j, f0)
                if ia is not None:
                    for g in range(KV):
                        c, gg = g // 4, g % 4
                        wait(dve, s["s_ps"], b, 2 * KV, 2 * g + 1)
                        dve.tensor_reduce(NM[:, 0, c, gg, :], SPB.rearrange("p (r t) -> p r t", r=REP), AX.X, ALU.max,
                                          negate=True).then_inc(s["max_done"], 1)
                        wait(dve, s["s_ps"], b, 2 * KV, 2 * g + 2)
                        dve.tensor_reduce(NM[:, 1, c, gg, :], SPA.rearrange("p (r t) -> p r t", r=REP), AX.X, ALU.max,
                                          negate=True).then_inc(s["max_done"], 1)
                        if jf is not None and g % 2 == 1:
                            hidden0(jf, 1 + g // 2, f0)
                    wait(dve, s["max_done"], b, 2 * KV, 2 * KV)
                    for c in range(2):
                        ins = dve.tensor_copy(NMS[:, :, :, 0, c, :], NM[:, :, c, :, :])
                    a0(dve, ins)
                    for c in range(2):
                        ins = dve.tensor_tensor(NMS[:, :, :, 1, c, :], NM[:, :, c, :, :], NMS[:, :, :, 0, c, :].bitcast(F32),
                                                ALU.subtract)
                    ins.then_inc(s["nm_split"], 1)
                    for g in range(KV):
                        wait(dve, s["pv_ps"], b, KV, g + 1)
                        dve.tensor_copy(OS[:, g, :], CTX[g % 2][:, 0:T]).then_inc(s["o_done"], 1)
                        if g % 2 == 0 and g < KV - 2 and jf is not None:
                            hidden0(jf, HT // 2 + 1 + g // 2, f0)
                    for n_ in range(4):
                        tt, q = n_ // 2, n_ % 2
                        wait(dve, s["oT_ps"], b, 4, n_ + 1)
                        v = ring[n_].rearrange("p (g r e) -> p g r e", g=4, r=REP)
                        rd = RD[:, tt, 4 * q:4 * q + 4, :]
                        ins = dve.reciprocal(rd, v[:, :, :, DH])
                        if n_ < 3:
                            a0(dve, ins)
                        else:
                            a0(dve, ins)
                        for g in range(4):
                            ins = dve.tensor_tensor(
                                CX[:, tt, (4 * q + g) * 32:(4 * q + g + 1) * 32].rearrange("p (r d) -> p r d", r=REP),
                                v[:, g, :, 0:DH],
                                spread(rd[:, g, :].rearrange("p (r o) -> p r o", o=1), 2, DH), ALU.mult)
                        ins.then_inc(s["ctx_done"], 1)
                    residual(0, "attn", b, ring[1], a0, "wo_ps", 1, "wo_read")
                if jf is not None:
                    residual(0, "ffn", jf, FO, f0, "down0_used", HT, "ffn0_read")

            a0.per = 1 + 6 + 1 + 4
            wide(dve, turn0, 0)

            dve.wait_ge(d_sel, 48)
            for lo, buf in SELRAW:
                dve.tensor_copy(SELC[:, lo:lo + buf.shape[1]], buf).then_inc(selc_ready, 1)

            f1 = Steps(ch["dve_f1"], 1 + 9 + 2 * MT)
            a1 = Steps(ch["dve_a1"], 1 + 3)

            def router(b, st):
                wait(dve, s["lg_ps"], b, 1, 1)
                dve.tensor_reduce(LMX[:, :], FO[:, 0:TT * EXP].rearrange("p (t e) -> p t e", t=TT), AX.X, ALU.max,
                                  negate=True).then_inc(s["lmax"], 1)
                wait(dve, s["lexp"], b, TT, TT)
                st(dve, dve.reciprocal(RZ[:, :], ZZ[:, :]))
                for tt in range(TT):
                    ins = dve.tensor_scalar(S18[:, tt, 0:EXP], SE[:, tt, :], RZ[:, tt:tt + 1], None, ALU.mult)
                st(dve, ins)
                stand(dve, turns["dve"])
                for tt in range(TT):
                    ins = dve.max(M8[:, tt, :], S18[:, tt, 0:EXP])
                st(dve, ins)
                st(dve, dve.memset(M8[:, :, TOPK:8], -1.0))
                stand(dve, turns["dve"])
                for tt in range(TT):
                    ins = dve.match_replace(RP[:, tt, :], M8[:, tt, :], S18[:, tt, :], 0.0)
                st(dve, ins)
                st(dve, dve.tensor_tensor(CW[:, :, 0:EXP], S18[:, :, 0:EXP], RP[:, :, 0:EXP], ALU.subtract))
                st(dve, dve.tensor_reduce(WS[:, :], CW[:, :, 0:EXP], AX.X, ALU.add))
                st(dve, dve.tensor_scalar(WS[:, :], WS[:, :], 1e-20, None, ALU.add))
                st(dve, dve.reciprocal(WS[:, :], WS[:, :]))
                for tt in range(TT):
                    ins = dve.tensor_scalar(CW[:, tt, 0:EXP], CW[:, tt, 0:EXP], WS[:, tt:tt + 1], 0.5, ALU.mult, ALU.mult)
                st(dve, ins)
                st(dve, dve.tensor_copy(CSP[:, :, 0, :], CW[:, :, :]))
                dve.tensor_tensor(CSP[:, :, 1, :], CW[:, :, :], CSP[:, :, 0, :].bitcast(F32), ALU.subtract)\
                    .then_inc(s["csplit"], 1)

            def hidden1(b, j, st):
                rows = min(P, MOE - j * P)
                wait(dve, s["tanh1"], b, MT, j + 1)
                wait(dve, s["down1_used"], b, MT, j - 1)
                st(dve, dve.scalar_tensor_tensor(AG[j % 2][0:rows, :], TH[j % 2][0:rows, :], 1.0, GUP[j % 2][0:rows, 0:T],
                                                 ALU.add, ALU.mult))
                st(dve, dve.tensor_tensor(AG[j % 2][0:rows, :], AG[j % 2][0:rows, :], GUP[j % 2][0:rows, T:2 * T], ALU.mult))
                wait(dve, s["cb_ps"], b, MT, j + 1)
                dve.tensor_tensor(HB[j % 2][0:rows, :], AG[j % 2][0:rows, :], CB[j % 2][0:rows, 0:T],
                                  ALU.mult).then_inc(s["hid1"], 1)

            def attn1(b, k, st):
                if k == 0:
                    modulate(1, "attn", b)
                if k == 1:
                    wait(dve, s["s1_ps"], b, 1, 1)
                    st(dve, dve.tensor_reduce(NM1, ring[3].rearrange("p (t i) -> p t i", t=TT), AX.X, ALU.max, negate=True))
                    dve.tensor_scalar(NMB1, NM1, SC1, None, ALU.mult).then_inc(s["nmb1"], 1)
                if k == 2:
                    wait(dve, s["exp1"], b, TT, TT)
                    st(dve, dve.reciprocal(RDN1, DEN1[:, :]))
                    for tt in range(TT):
                        ins = dve.tensor_scalar(P1[:, tt, :], P1[:, tt, :], RDN1[:, tt:tt + 1], None, ALU.mult)
                    ins.then_inc(s["p1_norm"], 1)
                if k == 5:
                    residual(1, "attn", b, ring[2], st, "wo1_ps", 1, "wo1_read", bias=BO1)

            f1.per = 1 + 11 + 2 * MT
            a1.per = 1 + 2 + 1

            def turn1(ia, jf):
                if jf is not None:
                    f1.start(jf)
                    norm(1, "ffn", jf, f1)
                    modulate(1, "ffn", jf)
                    router(jf, f1)
                if ia is not None:
                    a1.start(ia)
                    norm(1, "attn", ia, a1)
                for j in range(MT):
                    if jf is not None:
                        hidden1(jf, j, f1)
                    if ia is not None and j % 4 == 3 and j // 4 < 6:
                        attn1(ia, j // 4, a1)
                if jf is not None:
                    residual(1, "ffn", jf, FO, f1, "down1_used", MT, "ffn1_read")

            wide(dve, turn1, 1)

        @block.tensor
        def _(pe):
            mm = nc.tensor.matmul
            pe.wait_ge(cs_ready, 1)
            pe.wait_ge(d_mod, 32)
            pe.wait_ge(d_con, 32)
            for l in range(2):
                if l == 1:
                    pe.wait_ge(mod_sb, 3)
                for c in range(3):
                    for k in range(KC):
                        ins = mm(ring[c][0:NB, :], CS[:, l, k, :], WMOD[:, l, k, c * 512:(c + 1) * 512],
                                 start=(k == 0), stop=(k == KC - 1))
                    ins.then_inc(mod_ps, 1)
                pe.wait_ge(mod_sb, 3 * l + 3)
                if l == 1:
                    pe.wait_ge(modc_ready, 1)
                for a in range(2):
                    for sc in range(2):
                        for k in range(KC):
                            col = (3 * a + sc) * D + k * P
                            ins = nc.tensor.transpose(ring[3][:, ((a * 2 + sc) * KC + k) * NB:((a * 2 + sc) * KC + k + 1) * NB],
                                                      MODR[:, col:col + P], ident[0:NB, 0:NB])
                ins.then_inc(modT_ps, 1)
            pe.wait_ge(d_w2, 16)
            for a in range(HT):
                ins = mm(PS[:, 4 + a // 2, (a % 2) * D:(a % 2 + 1) * D], had, W2RAW[:, a, :], start=True, stop=True)
            ins.then_inc(w2_ps, 1)
            pe.wait_ge(modc_ready, 2)
            pe.wait_ge(w2_ping, 1)
            pe.wait_ge(consts_ready, 1)

            def xnT(layer, which, b):
                side = 0 if which == "attn" else 1
                m = L[layer][which]
                bank = (ring[3] if side == 0 else GUP[0])
                wait(pe, m["xn"], b, 1, 1)
                for k in range(KC):
                    for tt in range(TT):
                        ins = nc.tensor.transpose(bank[:, k * T + tt * P:k * T + (tt + 1) * P],
                                                  XN[side][:, tt, k * P:(k + 1) * P], ident)
                ins.then_inc(m["xnT"], 1)

            def gu0(b, j):
                if j == 0:
                    wait(pe, L[0]["ffn"]["hT"], b, 1, 1)
                wait(pe, s["hid0"], b, HT, j - 1)
                for h in range(2):
                    for k in range(KC):
                        ins = mm(GUP[j % 2][:, h * T:(h + 1) * T], W13[:, k, h, j * P:(j + 1) * P], HTT[1][:, k, :],
                                 start=(k == 0), stop=(k == KC - 1))
                ins.then_inc(s["gu0_ps"], 1)

            def down(b, j, hid, used, read, per, W, rows):
                wait(pe, s[hid], b, per, j + 1)
                if j == 0:
                    wait(pe, s[read], b, 1, 0)
                for tt in range(TT):
                    ins = mm(FO[:, tt * D:(tt + 1) * D], HB[j % 2][0:rows, tt * P:(tt + 1) * P], W[0:rows, j, :],
                             start=(j == 0 and tt == 0), stop=(j == per - 1), skip_group_check=True)
                ins.then_inc(s[used], 1)

            def down0(b, j):
                down(b, j, "hid0", "down0_used", "ffn0_read", HT, W2H, P)

            def turn0(ia, jf):
                tiles = []
                if jf is not None:
                    xnT(0, "ffn", jf)
                    gu0(jf, 0)

                def ffn(k):
                    if jf is not None:
                        if k + 1 < HT:
                            gu0(jf, k + 1)
                        down0(jf, k)

                if ia is not None:
                    b = ia
                    xnT(0, "attn", b)
                    H = HTT[0]
                    wait(pe, L[0]["attn"]["hT"], b, 1, 1)
                    if isinstance(b, int) and b == 0:
                        pe.wait_ge(d_w0, 64)
                    wait(pe, s["wo_read"], b, 1, 0)
                    for c in range(2):
                        for h in range(2):
                            for k in range(KC):
                                ins = mm(ring[c][:, h * T:(h + 1) * T], WQ[:, k, h, c * P:(c + 1) * P], H[:, k, :],
                                         start=(k == 0), stop=(k == KC - 1))
                        ins.then_inc(s["q_ps"], 1)
                    for h in range(2):
                        for k in range(KC):
                            ins = mm(ring[2][0:64, h * T:(h + 1) * T], WK[:, k, h, :], H[:, k, :],
                                     start=(k == 0), stop=(k == KC - 1))
                    ins.then_inc(s["k_ps"], 1)
                    for tt in range(TT):
                        for k in range(KC):
                            ins = mm(ring[3][:, tt * 64:(tt + 1) * 64], H[:, k, tt * P:(tt + 1) * P], WV[:, k, :],
                                     start=(k == 0), stop=(k == KC - 1))
                    ins.then_inc(s["v_ps"], 1)
                    wait(pe, s["qk_split"], b, 3, 3)
                    for c in range(2):
                        for hl, src in enumerate((QH, QL)):
                            ins = mm(ring[2][:, c * T:(c + 1) * T], SELK[0:64, c, hl, :], src[0:64, 2, :],
                                     start=(hl == 0), stop=(hl == 1))
                    ins.then_inc(s["kst_ps"], 1)
                    for m, bank in enumerate((0, 1, 3, 2)):
                        if bank == 3:
                            wait(pe, s["v_done"], b, 1, 1)
                        if bank == 2:
                            wait(pe, s["kst_done"], b, 1, 1)
                        for r2 in range(2):
                            for hl, src in enumerate((QH, QL)):
                                ins = mm(ring[bank][:, r2 * T:(r2 + 1) * T], SELQ[:, 2 * (m % 2) + r2, hl, :],
                                         src[:, m // 2, :], start=(hl == 0), stop=(hl == 1))
                        ins.then_inc(s["qst_ps"], 1)
                    wait(pe, s["kst_done"], b, 1, 1)
                    wait(pe, s["qst_act"], b, 2, 2)
                    wait(pe, s["qst_dve"], b, 2, 2)
                    for g in range(KV):
                        c, R = g // 4, slice(32 * (g % 4), 32 * (g % 4) + 3 * DH)
                        wait(pe, s["max_done"], b, 2 * KV, 2 * g - 1 if g else 0)
                        mk = mask_b[:, :].rearrange("p (a s) -> p a s", a=1)
                        mm(SPB.rearrange("p (r t) -> p r t", r=REP), ident_b[:, :], spread(mk, 1, REP), start=True,
                           stop=False, skip_group_check=True)
                        for r in range(REP):
                            ins = mm(SPB[:, r * P:(r + 1) * P], QST[R, c, r, 0:P], KST[R, c, 0:P], start=False, stop=True,
                                     skip_group_check=True)
                        ins.then_inc(s["s_ps"], 1)
                        wait(pe, s["max_done"], b, 2 * KV, 2 * g)
                        for i in range(2):
                            mm(SPA[:, i * 512:(i + 1) * 512].rearrange("p (r t) -> p r t", r=2)[:, :, P:T], ident_b[:, :],
                               spread(mk, 1, 2), start=True, stop=False, skip_group_check=True)
                        for r in range(REP):
                            ins = mm(SPA[:, r * T:(r + 1) * T], QST[R, c, r, P:T], KST[R, c, :], start=False, stop=True,
                                     skip_group_check=True)
                        ins.then_inc(s["s_ps"], 1)
                        if g % 2 == 1:
                            ffn(g // 2)
                    wait(pe, s["nm_split"], b, 1, 1)
                    stand(pe, turns["pe"])
                    for tt in range(TT):
                        ins = nc.tensor.transpose(ring[3][0:64, tt * P:(tt + 1) * P],
                                                  NMS[:, tt, :, :, :, :].rearrange("p g h c r -> p (g h c r)").bitcast(F32), ident)
                    ins.then_inc(s["nmT_ps"], 1)
                    wait(pe, s["rows_in"], b, 128, 128)

                    def pv(g):
                        wait(pe, s["masked"], b, 2 * KV, 2 * g + 2)
                        wait(pe, s["o_done"], b, KV, g - 1)
                        o, pr = CTX[g % 2][:, 0:T], PR[g % 2]
                        for r in range(REP):
                            mm(o[32 * r:32 * r + 32, :], VA[:, 0, g, :], pr[:, r * T:(r + 1) * T], start=True, stop=False,
                               skip_group_check=True)
                        for r in range(REP):
                            ins = mm(o[32 * r:32 * r + 32, P:T], VA[:, 1, g, :], pr[:, 4 * T + r * P:4 * T + (r + 1) * P],
                                     start=False, stop=True, skip_group_check=True)
                        ins.then_inc(s["pv_ps"], 1)

                    for g in range(KV):
                        c, R = g // 4, slice(32 * (g % 4), 32 * (g % 4) + 3 * DH + 2)
                        wait(pe, s["exp_done"], b, 2 * KV, 2 * g - 1 if g else 0)
                        for i in range(2):
                            ins = mm(SPA[:, i * 512:(i + 1) * 512], KST[R, c, 0:P], QST[R, c, 2 * i:2 * i + 2, :],
                                     start=True, stop=True)
                        ins.then_inc(s["st_ps"], 1)
                        wait(pe, s["exp_done"], b, 2 * KV, 2 * g)
                        mm(SPB, KST[R, c, P:T], QST[R, c, :, P:T], start=True, stop=True).then_inc(s["st_ps"], 1)
                        if g % 2 == 1:
                            ffn(HT // 2 + g // 2)
                        if g:
                            pv(g - 1)
                    pv(KV - 1)
                    for n_ in range(4):
                        tt, q = n_ // 2, n_ % 2
                        wait(pe, s["o_done"], b, KV, KV)
                        for g in range(4):
                            ins = nc.tensor.transpose(ring[n_][:, g * P:(g + 1) * P], OS[:, 4 * q + g, tt * P:(tt + 1) * P], ident)
                        ins.then_inc(s["oT_ps"], 1)
                    wait(pe, s["ctx_done"], b, 4, 4)
                    for k in range(KC):
                        for tt in range(TT):
                            ins = nc.tensor.transpose(ring[0][:, k * T + tt * P:k * T + (tt + 1) * P],
                                                      CX[:, tt, k * P:(k + 1) * P], ident)
                    ins.then_inc(s["ctxT_ps"], 1)
                    wait(pe, s["ctxT_done"], b, 1, 1)
                    for tt in range(TT):
                        for k in range(KC):
                            ins = mm(ring[1][:, tt * D:(tt + 1) * D], CXT[:, k, tt * P:(tt + 1) * P], WO[:, k, :],
                                     start=(k == 0), stop=(k == KC - 1))
                    ins.then_inc(s["wo_ps"], 1)
                else:
                    for k in range(HT):
                        ffn(k)

            pe.wait_ge(d_ffn, 32)
            pe.wait_ge(w2_done, 1)
            wide(pe, turn0, 0)

            pe.wait_ge(d_l1, 80)
            pe.wait_ge(wo1_done, 1)
            pe.wait_ge(d_gu, 64)
            pe.wait_ge(d_wd, 32)
            pe.wait_ge(selc_ready, 3)

            def gu1(b, j):
                rows = min(P, MOE - j * P)
                wait(pe, s["hid1"], b, MT, j - 1 if j else 0)
                for h in range(2):
                    for k in range(KC):
                        ins = mm(GUP[j % 2][0:rows, h * T:(h + 1) * T], GU[:, k, h, j * P:j * P + rows], HTT[1][:, k, :],
                                 start=(k == 0), stop=(k == KC - 1))
                ins.then_inc(s["gu1_ps"], 1)
                mm(CB[j % 2][0:rows, 0:T], SELC[:, j * P:j * P + rows], CTT[:, :], start=True,
                   stop=True).then_inc(s["cb_ps"], 1)

            def router(b):
                wait(pe, L[1]["ffn"]["hT"], b, 1, 1)
                wait(pe, s["ffn1_read"], b, 1, 0)
                for tt in range(TT):
                    for k in range(KC):
                        ins = mm(FO[:, tt * EXP:(tt + 1) * EXP], HTT[1][:, k, tt * P:(tt + 1) * P], GW[:, k, :],
                                 start=(k == 0), stop=(k == KC - 1))
                ins.then_inc(s["lg_ps"], 1)
                wait(pe, s["csplit"], b, 1, 1)
                stand(pe, turns["pe"])
                for tt in range(TT):
                    ins = nc.tensor.transpose(OP[0:2 * NC, tt * P:(tt + 1) * P],
                                              CSP[:, tt, :, :].rearrange("p h e -> p (h e)").bitcast(F32), ident)
                ins.then_inc(s["cT_ps"], 1)
                wait(pe, s["cT_done"], b, 1, 1)

            def attn1(b, k_):
                H = HTT[0]
                if k_ == 0:
                    xnT(1, "attn", b)
                    wait(pe, L[1]["attn"]["hT"], b, 1, 1)
                    for w, W in enumerate((WK1, WV1)):
                        for k in range(KC):
                            ins = mm(ring[1][:, w * T:(w + 1) * T], W[:, k, :], H[:, k, :], start=(k == 0), stop=(k == KC - 1))
                    ins.then_inc(s["kv1_ps"], 1)
                if k_ == 1:
                    wait(pe, s["kv1_done"], b, 2, 2)
                    wait(pe, s["wo1_read"], b, 1, 0)
                    for i in range(TT):
                        ins = nc.tensor.transpose(ring[2][:, i * P:(i + 1) * P], VT1[:, i * P:(i + 1) * P], ident)
                    ins.then_inc(s["v1T_ps"], 1)
                    for tt in range(TT):
                        ins = mm(ring[3][:, tt * T:(tt + 1) * T], VT1[:, tt * P:(tt + 1) * P], KT1, start=True, stop=True)
                    ins.then_inc(s["s1_ps"], 1)
                if k_ == 3:
                    wait(pe, s["p1_norm"], b, 1, 1)
                    for i in range(TT):
                        for tt in range(TT):
                            ins = nc.tensor.transpose(ring[3][:, i * T + tt * P:i * T + (tt + 1) * P],
                                                      P1[:, tt, i * P:(i + 1) * P], ident)
                    ins.then_inc(s["pT1_ps"], 1)
                if k_ == 4:
                    wait(pe, s["pT1_done"], b, 1, 1)
                    wait(pe, s["v1_done"], b, 1, 1)
                    for i in range(TT):
                        ins = mm(ring[1][:, 0:T], V1[:, i, :], PT1[:, i, :], start=(i == 0), stop=(i == TT - 1))
                    ins.then_inc(s["o1_ps"], 1)
                if k_ == 5:
                    wait(pe, s["o1_done"], b, 1, 1)
                    for tt in range(TT):
                        ins = mm(ring[2][:, tt * D:(tt + 1) * D], OT1[:, tt * P:(tt + 1) * P], WO1[:, :], start=True, stop=True)
                    ins.then_inc(s["wo1_ps"], 1)

            def turn1(ia, jf):
                if jf is not None:
                    xnT(1, "ffn", jf)
                    router(jf)
                    gu1(jf, 0)
                for j in range(MT):
                    if jf is not None:
                        if j + 1 < MT:
                            gu1(jf, j + 1)
                        down(jf, j, "hid1", "down1_used", "ffn1_read", MT, WD, min(P, MOE - j * P))
                    if ia is not None and j % 4 == 3 and j // 4 < 6:
                        attn1(ia, j // 4)

            wide(pe, turn1, 1)


def kernel(**inputs):
    import concourse.bacc as bacc
    from concourse.bass_utils import run_bass_kernel_spmd

    nc = bacc.Bacc("TRN2", target_bir_lowering=False, num_devices=1)
    a = {k: np.asarray(v) for k, v in inputs.items()}

    def swapped(w):
        w = w.reshape(D, -1, 2, DH // 2)
        return w[:, :, ::-1, :].reshape(D, -1)

    def half(which):
        rows = a["L1_ffn_w13"][:, which * INNER:(which + 1) * INNER, :].reshape(EXP * INNER, D)
        return np.concatenate([rows, a["L1_ffn_sw13"][which * SHARED:(which + 1) * SHARED]]).T

    def rows(*parts):
        w = np.stack(parts)
        return w.reshape(len(parts), -1, P, w.shape[-1]).transpose(2, 1, 0, 3)

    def one(w):
        return rows(w)[:, :, 0, :]

    down = np.concatenate([a["L1_ffn_w2"].transpose(0, 2, 1).reshape(EXP * INNER, D), a["L1_ffn_sw2"].T])
    last = (MT - 1) * P
    arrays = {
        "x": a["L0_attn_x"].reshape(NB * T, D),
        "consts": shape_constants(),
        "selrows": expert_rows(),
        "cT": rows(a["L0_c"].T, a["L1_c"].T).transpose(0, 2, 1, 3),
        "wmod": rows(a["L0_wmod"], a["L1_wmod"]).transpose(0, 2, 1, 3),
        "wq": rows(a["L0_attn_Wq"], swapped(a["L0_attn_Wq"])),
        "wk": rows(a["L0_attn_Wk"], swapped(a["L0_attn_Wk"])),
        "wv": one(a["L0_attn_Wv"]),
        "wo": one(a["L0_attn_Wo"]),
        "w13": rows(a["L0_ffn_W1"].T, a["L0_ffn_W3"].T),
        "w2": one(a["L0_ffn_W2"].T),
        "wk1": one(a["L1_attn_Wk"]),
        "wv1": one(a["L1_attn_Wv"]),
        "bcol1": np.stack([a["L1_attn_bk"], a["L1_attn_bv"]], axis=1),
        "wo1": one(a["L1_attn_Wo"]),
        "bo1": a["L1_attn_bo"],
        "gate": one(a["L1_ffn_gate_w"].T),
        "gu": rows(half(0), half(1)),
        "wd": one(down[:last]),
        "wd_last": down[last:],
    }
    arrays = {f"in_{k}": np.ascontiguousarray(v) for k, v in arrays.items()}
    args = [nc.dram_tensor(k, v.shape, mybir.dt.from_np(v.dtype), kind="ExternalInput").ap() for k, v in arrays.items()]
    gate_rows = nc.dram_tensor("gate_rows", (2, NB, 2, D), F32, kind="Internal").ap()
    out = nc.dram_tensor("out_x", (NB * T, D), F32, kind="ExternalOutput").ap()
    adaln_two_layers(nc, *args, gate_rows, out)
    r = run_bass_kernel_spmd(nc, [arrays], core_ids=[0])
    return r.results[0]["out_x"].reshape(NB, T, D)
```

```python
from contextlib import ExitStack

import concourse.bass as bass
from concourse import mybir
import numpy as np

F32 = mybir.dt.float32
F32R = mybir.dt.float32r
BF16 = mybir.dt.bfloat16
ALU = mybir.AluOpType
ACT = mybir.ActivationFunctionType
AX = mybir.AxisListType

P = 128
NB = 8
T = 256
D = 256
KC = D // P
TT = T // P
KV = 8
REP = 4
DH = 8
HID = 1024
HT = HID // P
EXP = 16
TOPK = 6
INNER = 176
SHARED = 2 * INNER
MOE = EXP * INNER + SHARED
MT = (MOE + P - 1) // P
HEADS1 = 16
SC0 = DH ** -0.5
SC1 = 1.0 / 128
EPS = 1e-5
MASK = -1e38
EARLY = 8
BF16_ONE = 0x3f80
NC = EXP + 1

C_ID, C_HAD, C_MASK, C_COS, C_SIN = 0, P, 2 * P, 3 * P, 3 * P + T
C_ONES = C_SIN + T
C_ALL = C_ONES + 1
S_Q = C_ALL
S_K = S_Q + REP * 2 * P
S_ALL = S_K + 2 * 2 * P


def shape_constants():
    c = np.zeros((P, S_ALL), np.float32)
    c[:, C_ID:C_ID + P] = np.eye(P)
    had = np.ones((1, 1), np.float32)
    while had.shape[0] < P:
        had = np.block([[had, had], [had, -had]])
    c[:, C_HAD:C_HAD + P] = had
    t = np.arange(P)
    c[:, C_MASK:C_MASK + P] = np.where(t[None, :] > t[:, None], MASK, 0.0)
    theta = (1.0 / np.float32(10000.0) ** (np.arange(0, DH, 2, dtype=np.float32) / DH)).astype(np.float32)
    freqs = np.outer(np.arange(T, dtype=np.float32), theta).astype(np.float32)
    d = np.arange(P) % DH
    c[:, C_COS:C_COS + T] = np.cos(freqs).T[d % (DH // 2)]
    c[:, C_SIN:C_SIN + T] = np.sin(freqs).T[d % (DH // 2)] * np.where(d < DH // 2, -1.0, 1.0)[:, None]
    for g in range(4):
        for d in range(DH):
            for r in range(REP):
                row = 32 * g + DH * r + d
                q = S_Q + r * 2 * P + 32 * g + d
                c[row, q] = c[row, q + DH] = 1.0
                c[row, q + P + 2 * DH] = 1.0
            for h in range(2):
                row = 32 * h + DH * g + d
                k = S_K + h * 2 * P + 32 * g + d
                c[row, k] = c[row, k + 2 * DH] = 1.0
                c[row, k + P + DH] = 1.0
        c[32 * g + 3 * DH:32 * g + 3 * DH + 2, C_ONES] = 1.0
    return c


def expert_rows():
    s = np.zeros((3 * NC, MT * P), np.uint16)
    for p in range(3):
        for e in range(EXP):
            s[p * NC + e, e * INNER:(e + 1) * INNER] = BF16_ONE
        s[p * NC + EXP, EXP * INNER:MOE] = BF16_ONE
    return s


def spread(ap, axis, n):
    shape = list(ap.shape)
    shape[axis] = n
    return ap.to_broadcast(shape)


def wait(eng, sem, b, per, n):
    v = b * per + n
    if isinstance(v, int) and v <= 0:
        return
    eng.wait_ge(sem, v)


def stand(eng, turns):
    eng.sem_inc(turns, 1)


class Steps:

    def __init__(self, sem, per):
        self.sem, self.per, self.b, self.n = sem, per, 0, 0

    def start(self, b):
        assert self.n in (0, self.per), (self.sem.name if hasattr(self.sem, "name") else "", self.n, self.per)
        self.b, self.n = b, 0

    def __call__(self, eng, ins, hold=True):
        ins.then_inc(self.sem, 1)
        self.n += 1
        if hold:
            eng.wait_ge(self.sem, self.b * self.per + self.n)


def adaln_two_layers(nc, x, consts, selrows, cT, wmod, wq, wk, wv, wo, w13, w2, wk1, wv1, bcol1, wo1, bo1,
                     gate, moe, gate_rows, out):
    ctx = ExitStack()
    with ctx:
        def sb(name, shape, dt=F32):
            return ctx.enter_context(nc.sbuf_tensor(name, shape, dt))

        def sem(name):
            return ctx.enter_context(nc.semaphore(name))

        XA = sb("residual", [P, NB * TT, D])
        IDT = sb("ident", [P, P])
        ident = IDT[:, :]
        WK1 = sb("wk1", [P, KC, P])
        WV1 = sb("wv1", [P, KC, P])
        BC1 = sb("bias_kv1", [P, 2])
        WO1 = sb("wo1_summed", [P, D])
        BO1 = sb("bo1", [P, D])
        GW = sb("gate_w", [P, KC, EXP])
        CT = sb("cond_T", [P, 2, KC, NB])
        CS = sb("cond_silu", [P, 2, KC, NB])
        MODC = sb("mod_cols", [P, 2, NB, 8])
        MB_ = [sb("mod_b_attn", [P, 4]), sb("mod_b_ffn", [P, 4])]
        GB_ = [sb("gate_b_attn", [P, D]), sb("gate_b_ffn", [P, D])]
        IDB = sb("ident_bf16", [P, P], BF16)
        HALF = sb("minus_half", [P, TT])
        ST = [sb("bn_attn", [P, TT, 6]), sb("bn_ffn", [P, TT, 6])]
        MV = [sb("mv_attn", [P, TT, 2]), sb("mv_ffn", [P, TT, 2])]
        VE = [sb("ve_attn", [P, TT]), sb("ve_ffn", [P, TT])]
        RS = [sb("rstd_attn", [P, TT]), sb("rstd_ffn", [P, TT])]
        XN = [sb("xn_attn", [P, TT, D]), sb("xn_ffn", [P, TT, D])]
        HTT = [sb("hT_attn", [P, KC, T]), sb("hT_ffn", [P, KC, T])]
        HFH = sb("hT_ffn_high", [P, KC, T], F32R)
        HFL = sb("hT_ffn_low", [P, KC, T], F32R)
        HB = [sb(f"hid{i}", [P, T]) for i in range(3)]
        HH = [sb(f"hid_high{i}", [P, T], F32R) for i in range(3)]
        HL = [sb(f"hid_low{i}", [P, T], F32R) for i in range(3)]

        def slot(j, per):
            def of(j):
                return 1 if j % 3 == 0 and j == per - 1 else j % 3
            before = j - 1
            while of(before % per) != of(j):
                before -= 1
            return of(j), before

        def aliased(name, shape, *names):
            with nc.sbuf_tensor(name, shape, F32) as t:
                return t

        TW = 4 * P + D
        SETUP = aliased("setup_area", [P, EARLY * 2 * TW])
        WHI_A = sb("moe_high_a", [P, EARLY, TW], F32R)
        RAW_A = aliased("moe_raw_a", [P, EARLY, TW])
        WLO_A = sb("moe_low_a", [P, EARLY, TW], F32R)
        WMOD = SETUP[:, 0:6144].rearrange("p (l k n) -> p l k n", l=2, k=KC)
        WO1RAW = SETUP[:, 0:4096].rearrange("p (h d) -> p h d", h=HEADS1)
        W2RAW = SETUP[:, 6144:8192].rearrange("p (a d) -> p a d", a=HT)
        W2PING = SETUP[:, 8192:10240].rearrange("p (a d) -> p a d", a=HT)
        SELQK = SETUP[:, 10240:10240 + S_ALL - S_Q]

        layer0 = ExitStack()

        def s0(name, shape, dt=F32):
            return layer0.enter_context(nc.sbuf_tensor(name, shape, dt))

        CON = s0("constants", [P, C_ALL])
        had = CON[:, C_HAD:C_HAD + P]
        cosT, sinT = CON[:, C_COS:C_COS + T], CON[:, C_SIN:C_SIN + T]
        ones24 = CON[:, C_ONES:C_ONES + 1]
        mask_b = s0("mask_bf16", [P, P], BF16)
        SELQ = s0("sel_q", [P, REP, 2, P], F32R)
        SELK = s0("sel_k", [P, 2, 2, P], F32R)
        WQ = s0("wq", [P, KC, 2, D])
        WK = s0("wk", [P, KC, 2, 64])
        WV = s0("wv", [P, KC, 64])
        WO = s0("wo", [P, KC, D])
        W13H = s0("w13_high", [P, KC, 2, HID], F32R)
        W13RAW = aliased("w13_raw", [P, KC, 2, HID])
        W13L = s0("w13_low", [P, KC, 2, HID], F32R)
        W2HI = s0("w2_hadamard_high", [P, HT, D], F32R)
        W2LO = s0("w2_hadamard_low", [P, HT, D], F32R)
        RT = s0("rope_tmp", [P, 2, T])
        QR = s0("qk_rot", [P, 3, T])
        QH = s0("qk_high", [P, 3, T], F32R)
        QL = s0("qk_low", [P, 3, T], F32R)
        QST = s0("q_stack", [P, 2, REP, T], F32R)
        KST = s0("k_stack", [P, 2, T], F32R)
        VA = s0("v_aug", [P, TT, KV, 32])
        NM = s0("minus_max", [P, TT, 2, 4, REP])
        NMS = s0("minus_max_split", [P, TT, 4, 2, 2, REP], F32R)
        NMT = s0("minus_max_T", [64, T], F32)
        PR = [s0("probs0", [P, 6 * T]), s0("probs1", [P, 6 * T])]
        MODR = PR[0][0:NB, :]
        GR = PR[1][0:NB, 0:2 * D].rearrange("b (s d) -> b s d", s=2)
        GT = PR[1][0:NB, 2 * D:4 * D].rearrange("b (s d) -> b s d", s=2)
        OS = s0("ctx_raw", [P, KV, T])
        W2F = OS
        RD = s0("recip_den", [P, TT, KV, REP])
        CX = RT
        CXT = QR[:, 0:2, :]
        layer0.close()

        LATE = MT - EARLY
        LOTS = [0, 1, 3, 6, 10, 14, LATE]
        WHI_B = sb("moe_high_b", [P, LATE, TW], F32R)
        RAW_B = aliased("moe_raw_b", [P, LATE, TW])
        WLO_B = sb("moe_low_b", [P, LATE, TW], F32R)
        SELC = sb("sel_expert", [3 * NC, MT * P], BF16)
        L1B = sb("attn1", [P, 3, T])
        KT1, VT1, OT1 = L1B[:, 0, :], L1B[:, 1, :], L1B[:, 0, :]
        V1 = L1B[:, 2, :].rearrange("p (i d) -> p i d", i=TT)
        PT1 = HTT[0]
        P1 = XN[0]
        SM = sb("softmax1", [P, 8])
        NM1, NMB1, DEN1, RDN1 = SM[:, 0:2], SM[:, 2:4], SM[:, 4:6], SM[:, 6:8]
        LMX = sb("r_max", [P, TT])
        SE = sb("r_exp", [P, TT, EXP])
        ZZ = sb("r_sum", [P, TT])
        RZ = sb("r_rsum", [P, TT])
        S18 = sb("r_scores", [P, TT, EXP + 2])
        M8 = sb("r_top8", [P, TT, 8])
        RP = sb("r_replaced", [P, TT, EXP + 2])
        CW = sb("r_combine", [P, TT, NC])
        CW2 = sb("r_rest", [P, TT, NC])
        WS = sb("r_wsum", [P, TT])
        CSP = sb("r_split", [P, TT, 3, NC], BF16)
        CTT = sb("r_split_T", [3 * NC, T], BF16)

        def moe_tile(j, k, h, rows):
            hi, lo, n = (WHI_A, WLO_A, j) if j < EARLY else (WHI_B, WLO_B, j - EARLY)
            at = (2 * h + k) * P
            return hi[:, n, at:at + rows], lo[:, n, at:at + rows]

        def moe_down(j, rows):
            hi, lo, n = (WHI_A, WLO_A, j) if j < EARLY else (WHI_B, WLO_B, j - EARLY)
            return hi[0:rows, n, 4 * P:TW], lo[0:rows, n, 4 * P:TW]

        PS = ctx.enter_context(nc.psum_tensor("psum", [P, 8, 512], F32))
        SPA = PS[:, 0:2, :].rearrange("p b n -> p (b n)")
        SPB = PS[:, 2, :]
        ring = [PS[:, i, :] for i in range(4)]
        OP = PS[:, 4, :]
        GUP = [PS[:, 5, :], PS[:, 6, :]]
        FO = PS[:, 7, :]
        CTX = [OP, ring[3]]
        CB = OP
        GUP1 = [PS[:, 5, :], PS[:, 6, :], PS[:, 3, :]]

        def bank1(j):
            last = MT - 1
            if j == last:
                return GUP1[1], j - 2
            return GUP1[j % 3], (j - 3 if j >= 3 else {0: last - 3, 1: last, 2: last - 1}[j] - MT)

        (ld_x, ld_consts, ld_w0, ld_w13, ld_w2, ld_mod, ld_wo1, ld_l1, ld_early, ld_sel) = (
            sem(n) for n in ("ld_x", "ld_constants", "ld_attn0", "ld_w13", "ld_w2raw", "ld_mod", "ld_wo1raw",
                             "ld_attn1", "ld_moe_early", "ld_sel"))
        ld_late = [sem(f"ld_moe_late{i}") for i in range(len(LOTS) - 1)]
        gates_stored, out_stored = sem("gates_stored"), sem("out_stored")
        dve_setup, pool_setup, act_setup = sem("dve_setup"), sem("pool_setup"), sem("act_setup")
        (cs_ready, mod_ps, mod_sb, modT_ps, modc_ready, gr_ready, w2_ps, w2_ping, w2_done, w2_split, w13_split,
         wo1_done, consts_ready, late_high, late_done, early_done) = (sem(n) for n in (
            "cond_ready", "mod_in_psum", "mod_in_sbuf", "modT_in_psum", "mod_cols_ready", "gate_rows_ready",
            "w2_in_psum", "w2_evacuated", "w2_ready", "w2_split", "w13_split", "wo1_ready", "consts_ready",
            "late_high", "late_done", "early_done"))

        def names(layer, which):
            return {n: sem(f"{n}_{layer}{which}") for n in (
                "gate_in", "mv", "rstd", "xn", "xnT", "hT", "hT_split", "x_done")}

        L = [dict(attn=names(0, "a"), ffn=names(0, "f")), dict(attn=names(1, "a"), ffn=names(1, "f"))]
        s = {n: sem(n) for n in (
            "q_ps", "k_ps", "v_ps", "rope_done", "qk_split", "v_done", "kst_ps", "kst_done", "qst_ps",
            "qst_act", "qst_dve", "s_ps", "max_done", "nm_split", "nmT_ps", "nmT_done", "rows_in",
            "st_ps", "exp_done", "masked", "pv_ps", "o_done", "oT_ps", "ctx_done", "ctxT_ps", "ctxT_done",
            "wo_ps", "wo_read",
            "gu0_ps", "tanh0", "hid0", "high0", "low0", "down0_used", "ffn0_read",
            "gu1_ps", "cb_ps", "tanh1", "act1", "gated1", "hid1", "high1", "low1", "down1_used", "ffn1_read",
            "kv1_ps", "kv1_done", "v1T_ps", "v1_done", "s1_ps", "nmb1", "exp1", "p1_norm", "pT1_ps", "pT1_done",
            "o1_ps", "o1_done", "wo1_ps", "wo1_read",
            "lg_ps", "lmax", "lexp", "csplit", "cT_ps", "cT_done")}
        ch = {k: sem("steps_" + k) for k in ("dve_a0", "dve_f0", "dve_a1", "dve_r1", "dve_n0a", "dve_n0f",
                                             "dve_n1a", "dve_n1f", "pool_0a", "pool_0f", "pool_1a", "pool_1f")}
        mod_cols_in = [[sem(f"mod_cols_in_{l}{w}") for w in "af"] for l in range(2)]
        turns = {e: sem("turns_" + e) for e in ("dve", "pe", "pool")}

        def xtile(b, tt):
            if isinstance(b, int):
                return XA[:, b * TT + tt, :]
            return XA[:, bass.ds(b * TT + tt, 1), :].rearrange("p a d -> p (a d)")

        def xboth(b):
            return XA[:, b * TT:(b + 1) * TT, :] if isinstance(b, int) else XA[:, bass.ds(b * TT, TT), :]

        def layer0_turns(eng, turn):
            turn(0, None, 1)
            turn(1, 0, 2)
            with eng.Fori(2, NB - 1) as i:
                turn(i, i - 1, i + 1)
            turn(NB - 1, NB - 2, None)
            turn(None, NB - 1, None)

        def layer1_turns(eng, turn):
            turn(0, None, None)
            turn(1, 0, None)
            with eng.Fori(2, NB) as i:
                turn(i, i - 1, i - 2)
            turn(None, NB - 1, NB - 2)

        STEPS_PE = {2: "xnT", 4: "kv", 6: "scores", 10: "probsT", 12: "ctx", 14: "wo", 17: "xnT2", 19: "logits"}
        STEPS_ACT = {5: "kv", 7: "v", 8: "exp", 11: "probsT", 13: "ctx", 20: "route"}
        STEPS_DVE = {0: "mean", 1: "norm", 3: "modulate", 7: "max", 9: "softmax", 15: "wo", 16: "norm2",
                     18: "modulate2", 20: "max2", 21: "route"}
        STEPS_POOL = {0: "rstd", 15: "rstd2"}

        def late_at(ia, jf, j):
            n = None
            if isinstance(ia, int) and ia == 0:
                n = j // 3 if j % 3 == 2 else None
            if isinstance(jf, int) and jf == 0:
                n = 8 + j
            return n if n is not None and n < LATE else None

        block = ctx.enter_context(nc.Block())

        @block.sync
        def _(sp):
            sp.dma_start(CT[:, :, :, :], cT).then_inc(ld_mod, 16)
            sp.dma_start(CON[:, :], consts[:, 0:C_ALL]).then_inc(ld_consts, 16)
            sp.dma_start(IDT[:, :], consts[:, C_ID:C_ID + P]).then_inc(ld_consts, 16)
            sp.dma_start(SELQK, consts[:, S_Q:S_ALL]).then_inc(ld_consts, 16)
            sp.dma_start(XA[:, 0:TT, :], x[0:T, :].rearrange("(n p) d -> p n d", p=P)).then_inc(ld_x, 16)
            sp.dma_start(WMOD, wmod).then_inc(ld_mod, 16)
            sp.dma_start(WQ[:, :, :, :], wq).then_inc(ld_w0, 16)
            sp.dma_start(WK[:, :, :, :], wk).then_inc(ld_w0, 16)
            sp.dma_start(WV[:, :, :], wv).then_inc(ld_w0, 16)
            sp.dma_start(W2RAW, w2).then_inc(ld_w2, 16)
            sp.dma_start(WO[:, :, :], wo).then_inc(ld_w0, 16)
            sp.dma_start(W13RAW[:, :, :, :], w13).then_inc(ld_w13, 16)
            sp.dma_start(XA[:, TT:NB * TT, :], x[T:NB * T, :].rearrange("(n p) d -> p n d", p=P)).then_inc(ld_x, 16)
            sp.dma_start(WK1[:, :, :], wk1).then_inc(ld_l1, 16)
            sp.dma_start(WV1[:, :, :], wv1).then_inc(ld_l1, 16)
            sp.dma_start(BC1[:, :], bcol1).then_inc(ld_l1, 16)
            sp.dma_start(BO1[:, :], spread(bo1.rearrange("(a d) -> a d", a=1), 0, P)).then_inc(ld_l1, 16)
            sp.dma_start(GW[:, :, :], gate).then_inc(ld_l1, 16)
            for l in range(2):
                sp.wait_ge(gr_ready, l + 1)
                sp.dma_start(gate_rows[l], GR[:, :, :]).then_inc(gates_stored, 16)
                sp.wait_ge(gates_stored, 16 * (l + 1))
            sp.wait_ge(mod_ps, 6)
            sp.dma_start(WO1RAW, wo1).then_inc(ld_wo1, 16)
            sp.wait_ge(wo1_done, 1)
            sp.wait_ge(w2_done, 1)
            sp.wait_ge(consts_ready, 1)
            sp.dma_start(RAW_A[:, :, :], moe[:, 0:EARLY, :]).then_inc(ld_early, 16)

            def gate_row(layer, side, b):
                n = L[layer]["attn" if side == 0 else "ffn"]
                wait(sp, n["x_done"], b, 1, 0)
                src = gate_rows[layer, b:b + 1, side, :] if isinstance(b, int) else \
                    gate_rows[layer, bass.ds(b, 1), side, :]
                sp.dma_start(GB_[side][:, :], spread(src, 0, P)).then_inc(n["gate_in"], 16)

            def turn0(ia, jf, nxt):
                if jf is not None:
                    gate_row(0, 1, jf)
                if ia is not None:
                    gate_row(0, 0, ia)
                    wait(sp, s["nmT_done"], ia, 1, 1)
                    for g in range(4):
                        for hl in range(2):
                            row = 32 * g + 3 * DH + hl
                            sp.dma_start(
                                QST[row:row + 1, :, :, :].rearrange("p c r t -> p (c r) t").bitcast(F32),
                                NMT[16 * g + 8 * hl:16 * g + 8 * hl + 8, :]).then_inc(s["rows_in"], 16)

            def turn1(ia, jf, prev):
                if ia is not None:
                    gate_row(1, 0, ia)
                if prev is not None:
                    store(prev)
                if jf is not None:
                    gate_row(1, 1, jf)

            def store(b):
                wait(sp, L[1]["ffn"]["x_done"], b, 1, 1)
                dst = out[b * T:(b + 1) * T, :] if isinstance(b, int) else out[bass.ds(b * T, T), :]
                sp.dma_start(dst.rearrange("(n p) d -> p n d", p=P), xboth(b)).then_inc(out_stored, 16)

            layer0_turns(sp, turn0)
            sp.wait_ge(L[0]["attn"]["x_done"], NB)
            sp.wait_ge(L[0]["ffn"]["x_done"], NB)
            for n, lot in enumerate(ld_late):
                lo, hi = LOTS[n], LOTS[n + 1]
                sp.dma_start(RAW_B[:, lo:hi, :], moe[:, EARLY + lo:EARLY + hi, :]).then_inc(lot, 16)
                if n == 1:
                    sp.dma_start(SELC[:, :], selrows.bitcast(BF16)).then_inc(ld_sel, 16)
            layer1_turns(sp, turn1)
            store(NB - 1)
            sp.wait_ge(out_stored, 16 * NB)

        @block.gpsimd
        def _(po):
            n_ = [0]

            def step(ins):
                n_[0] += 1
                ins.then_inc(pool_setup, 1)
                po.wait_ge(pool_setup, n_[0])

            step(po.memset(HALF[:, :], -0.5))

            norm_steps = {(l, w): Steps(ch[f"pool_{l}{w[0]}"], 1) for l in (0, 1) for w in ("attn", "ffn")}

            def norm(layer, which, b):
                side = 0 if which == "attn" else 1
                m = L[layer][which]
                st = norm_steps[layer, which]
                st.start(b)
                wait(po, m["mv"], b, 1, 1)
                wait(po, m["xn"], b, 1, 0)
                stand(po, turns["pool"])
                st(po, po.tensor_scalar(VE[side][:, :], MV[side][:, :, 1], EPS, None, ALU.add))
                po.tensor_tensor(RS[side][:, :], VE[side][:, :], HALF[:, :], ALU.pow).then_inc(m["rstd"], 1)

            def low_tile(j, b, per, high, low):
                i, _ = slot(j, per)
                wait(po, s[high], b, per, j + 1)
                po.tensor_tensor(HL[i][:, :], HB[i][:, :], HH[i][:, :].bitcast(F32), ALU.subtract)\
                    .then_inc(s[low], 1)

            def setup_splits():
                po.wait_ge(ld_wo1, 16)
                h = HEADS1 // 2
                while h > 1:
                    step(po.tensor_tensor(WO1RAW[:, 0:h, :], WO1RAW[:, 0:h, :], WO1RAW[:, h:2 * h, :], ALU.add))
                    h //= 2
                po.tensor_tensor(WO1[:, :], WO1RAW[:, 0, :], WO1RAW[:, 1, :], ALU.add).then_inc(wo1_done, 1)
                po.wait_ge(w2_done, 1)
                step(po.tensor_copy(W2HI[:, :, :], W2F[:, :, :]))
                po.tensor_tensor(W2LO[:, :, :], W2F[:, :, :], W2HI[:, :, :].bitcast(F32), ALU.subtract)\
                    .then_inc(w2_split, 1)
                po.wait_ge(ld_w13, 16)
                step(po.tensor_copy(W13H[:, :, :, :], W13RAW[:, :, :, :]))
                po.tensor_tensor(W13L[:, :, :, :], W13RAW[:, :, :, :], W13H[:, :, :, :].bitcast(F32), ALU.subtract)\
                    .then_inc(w13_split, 1)

            def early(b):
                hi, raw, lo = (w[:, b, :] if isinstance(b, int) else
                               w[:, bass.ds(b, 1), :].rearrange("p a n -> p (a n)") for w in (WHI_A, RAW_A, WLO_A))
                if isinstance(b, int) and b == 0:
                    po.wait_ge(ld_early, 16)
                po.tensor_copy(hi, raw).then_inc(early_done, 1)
                wait(po, early_done, b, 2, 1)
                stand(po, turns["pool"])
                po.tensor_tensor(lo, raw, hi.bitcast(F32), ALU.subtract).then_inc(early_done, 1)

            def turn0(ia, jf, nxt):
                def tile(j):
                    if jf is not None:
                        low_tile(j, jf, HT, "high0", "low0")

                if jf is not None:
                    norm(0, "ffn", jf)
                tile(0)
                if ia is not None:
                    if isinstance(ia, int) and ia == 0:
                        setup_splits()
                    for j in range(1, 6):
                        tile(j)
                    for g in range(KV):
                        wait(po, s["exp_done"], ia, 2 * KV, 2 * g + 2)
                        stand(po, turns["pool"])
                        pa = PR[g % 2][:, 0:4 * T].rearrange("p (r t) -> p r t", r=REP)[:, :, 0:P]
                        pb = PR[g % 2][:, 4 * T:6 * T].rearrange("p (r t) -> p r t", r=REP)
                        for pr in (pa, pb):
                            po.affine_select(out=pr, in_=pr, compare_op=ALU.is_ge, fill=0.0, base=0,
                                             pattern=[[0, REP], [1, P]], channel_multiplier=-1).then_inc(s["masked"], 1)
                        if g == 3:
                            tile(6)
                    if nxt is not None:
                        norm(0, "attn", nxt)
                    tile(7)
                    early(ia)
                else:
                    for j in range(1, HT):
                        tile(j)

            norm(0, "attn", 0)
            layer0_turns(po, turn0)

            def turn1(ia, jf, prev):
                for j in range(MT - 1):
                    if jf is not None:
                        low_tile(j, jf, MT, "high1", "low1")
                    if ia is not None and STEPS_POOL.get(j) == "rstd":
                        norm(1, "attn", ia)
                    if ia is not None and STEPS_POOL.get(j) == "rstd2":
                        norm(1, "ffn", ia)
                    n = late_at(ia, jf, j)
                    if n is not None:
                        po.wait_ge(late_high, n + 1)
                        po.tensor_tensor(WLO_B[:, n, :], RAW_B[:, n, :], WHI_B[:, n, :].bitcast(F32), ALU.subtract)\
                            .then_inc(late_done, 1)
                if jf is not None:
                    low_tile(MT - 1, jf, MT, "high1", "low1")

            layer1_turns(po, turn1)

        @block.scalar
        def _(act):
            act.wait_ge(ld_mod, 32)
            nc.scalar.activation(CS[:, :, :, :], CT[:, :, :, :], ACT.Tanh, scale=0.5).then_inc(act_setup, 1)
            act.wait_ge(w2_ps, 1)
            nc.scalar.activation(W2PING.rearrange("p a d -> p (a d)"), PS[:, 4:8, :].rearrange("p b n -> p (b n)"),
                                 ACT.Copy, scale=1.0 / 64).then_inc(w2_ping, 1)

            def split_hT(layer, b):
                m = L[layer]["ffn"]
                wait(act, m["hT"], b, 1, 1)
                nc.scalar.activation(HFH[:, :, :], HTT[1][:, :, :], ACT.Copy).then_inc(m["hT_split"], 1)

            def tanh0(b, j):
                wait(act, s["gu0_ps"], b, HT, j + 1)
                i, before = slot(j, HT)
                wait(act, s["low0"], b, HT, before + 1)
                nc.scalar.activation(HB[i][:, :], GUP[j % 2][:, 0:T], ACT.Tanh, scale=0.5).then_inc(s["tanh0"], 1)

            def high_tile(j, b, per, hid, used, high):
                wait(act, s[hid], b, per, j + 1)
                i, before = slot(j, per)
                wait(act, s[used], b, per, before + 1)
                nc.scalar.activation(HH[i][:, :], HB[i][:, :], ACT.Copy).then_inc(s[high], 1)

            def turn0(ia, jf, nxt):
                def tile(j):
                    if jf is not None:
                        tanh0(jf, j)
                        high_tile(j, jf, HT, "hid0", "down0_used", "high0")

                def evac_qst(m, bank):
                    wait(act, s["qst_ps"], ia, 4, m + 1)
                    nc.scalar.activation(QST[:, m // 2, 0:2, :].rearrange("p r t -> p (r t)"), ring[bank],
                                         ACT.Copy).then_inc(s["qst_act"], 1)

                if ia is not None:
                    b = ia
                    if isinstance(b, int) and b == 0:
                        act.wait_ge(gates_stored, 32)
                        act.wait_ge(consts_ready, 1)
                    wait(act, s["v_ps"], b, 1, 1)
                    wait(act, s["pv_ps"], b, KV, 0)
                    nc.scalar.activation(VA[:, :, :, 0:DH], ring[3][:, 0:2 * 64].rearrange("p (t g d) -> p t g d", t=TT, g=KV),
                                         ACT.Copy).then_inc(s["v_done"], 1)
                if jf is not None:
                    split_hT(0, jf)
                tile(0)
                if ia is not None:
                    wait(act, s["kst_ps"], b, 1, 1)
                    nc.scalar.activation(KST[:, :, :].rearrange("p c t -> p (c t)"), ring[2], ACT.Identity,
                                         bias=ones24).then_inc(s["kst_done"], 1)
                    evac_qst(0, 0)
                    tile(1)
                    evac_qst(2, 3)
                    for j in (2, 3):
                        tile(j)
                    wait(act, s["nmT_ps"], b, 1, 1)
                    wait(act, s["rows_in"], b, 128, 0)
                    nc.scalar.activation(NMT[:, :], ring[3][0:64, 0:T], ACT.Copy).then_inc(s["nmT_done"], 1)
                    for j in (4, 5):
                        tile(j)
                    for g in range(KV):
                        wait(act, s["pv_ps"], b, KV, g - 1)
                        wait(act, s["st_ps"], b, 2 * KV, 2 * g + 1)
                        nc.scalar.activation(PR[g % 2][:, 0:4 * T], SPA, ACT.Exp, scale=SC0).then_inc(s["exp_done"], 1)
                        wait(act, s["st_ps"], b, 2 * KV, 2 * g + 2)
                        nc.scalar.activation(PR[g % 2][:, 4 * T:6 * T], SPB, ACT.Exp, scale=SC0).then_inc(s["exp_done"], 1)
                        if g == 3:
                            tile(6)
                    tile(7)
                    wait(act, s["ctxT_ps"], b, 1, 1)
                    nc.scalar.activation(CXT.rearrange("p k t -> p (k t)"), ring[0], ACT.Copy)\
                        .then_inc(s["ctxT_done"], 1)
                else:
                    for j in range(1, HT):
                        tile(j)

            layer0_turns(act, turn0)

            def tanh1(b, j):
                bank, _ = bank1(j)
                wait(act, s["gu1_ps"], b, MT, j + 1)
                i, before = slot(j, MT)
                wait(act, s["low1"], b, MT, before + 1)
                nc.scalar.activation(HB[i][:, :], bank[:, 0:T], ACT.Tanh, scale=0.5).then_inc(s["tanh1"], 1)

            def chain(what, b):
                if what == "kv":
                    wait(act, s["kv1_ps"], b, 1, 1)
                    nc.scalar.activation(KT1, ring[1][:, 0:T], ACT.Identity, bias=BC1[:, 0:1]).then_inc(s["kv1_done"], 1)
                    nc.scalar.activation(VT1, ring[1][:, T:2 * T], ACT.Identity, bias=BC1[:, 1:2]).then_inc(s["kv1_done"], 1)
                if what == "v":
                    wait(act, s["v1T_ps"], b, 1, 1)
                    nc.scalar.activation(V1.rearrange("p i d -> p (i d)"), ring[2][:, 0:T], ACT.Copy).then_inc(s["v1_done"], 1)
                if what == "exp":
                    wait(act, s["nmb1"], b, 1, 1)
                    for tt in range(TT):
                        nc.scalar.activation(P1[:, tt, :], ring[0][:, tt * T:(tt + 1) * T], ACT.Exp, scale=SC1,
                                             bias=NMB1[:, tt:tt + 1], accum_out=DEN1[:, tt:tt + 1]).then_inc(s["exp1"], 1)
                if what == "probsT":
                    wait(act, s["pT1_ps"], b, 1, 1)
                    nc.scalar.activation(PT1[:, :, :].rearrange("p i t -> p (i t)"), ring[2], ACT.Copy).then_inc(s["pT1_done"], 1)
                if what == "ctx":
                    wait(act, s["o1_ps"], b, 1, 1)
                    nc.scalar.activation(OT1, ring[1][:, 0:T], ACT.Copy).then_inc(s["o1_done"], 1)
                if what == "route":
                    wait(act, s["lmax"], b, 1, 1)
                    for tt in range(TT):
                        nc.scalar.activation(SE[:, tt, :], ring[2][:, tt * EXP:(tt + 1) * EXP], ACT.Exp, bias=LMX[:, tt:tt + 1],
                                             accum_out=ZZ[:, tt:tt + 1]).then_inc(s["lexp"], 1)

            def turn1(ia, jf, prev):
                if jf is not None:
                    wait(act, s["cT_ps"], jf, 1, 1)
                    if prev is not None:
                        wait(act, s["cb_ps"], prev, MT, MT)
                    nc.scalar.activation(CTT[:, :], ring[0].bitcast(BF16)[0:3 * NC, 0:T], ACT.Copy).then_inc(s["cT_done"], 1)
                    tanh1(jf, 0)
                for j in range(MT - 1):
                    if jf is not None:
                        tanh1(jf, j + 1)
                        high_tile(j, jf, MT, "hid1", "down1_used", "high1")
                    if ia is not None:
                        chain(STEPS_ACT.get(j), ia)
                    n = late_at(ia, jf, j)
                    if n is not None:
                        act.wait_ge(ld_late[max(i for i in range(len(ld_late)) if LOTS[i] <= n)], 16)
                        nc.scalar.activation(WHI_B[:, n, :], RAW_B[:, n, :], ACT.Copy).then_inc(late_high, 1)
                if ia is not None:
                    if jf is not None:
                        wait(act, s["gu1_ps"], jf, MT, MT)
                    split_hT(1, ia)
                if jf is not None:
                    high_tile(MT - 1, jf, MT, "hid1", "down1_used", "high1")

            layer1_turns(act, turn1)

        @block.vector
        def _(dve):
            n_ = [0]

            def step(ins):
                n_[0] += 1
                ins.then_inc(dve_setup, 1)
                dve.wait_ge(dve_setup, n_[0])

            dve.wait_ge(ld_consts, 48)
            dve.tensor_copy(SELQ[:, :, :, :], SELQK[:, 0:S_K - S_Q].rearrange("p (r h n) -> p r h n", r=REP, h=2))
            dve.tensor_copy(SELK[:, :, :, :], SELQK[:, S_K - S_Q:S_ALL - S_Q].rearrange("p (c h n) -> p c h n", c=2, h=2))
            dve.tensor_copy(mask_b[:, :], CON[:, C_MASK:C_MASK + P])
            dve.tensor_copy(IDB[:, :], ident)
            step(dve.memset(VA[:, :, :, :], 0.0))
            dve.memset(VA[:, :, :, DH:DH + 1], 1.0).then_inc(consts_ready, 1)
            dve.wait_ge(act_setup, 1)
            step(dve.scalar_tensor_tensor(CS[:, :, :, :].rearrange("p l k b -> p (l k b)"),
                                          CS[:, :, :, :].rearrange("p l k b -> p (l k b)"), 1.0,
                                          CT[:, :, :, :].rearrange("p l k b -> p (l k b)"), ALU.add, ALU.mult))
            dve.tensor_scalar(CS[:, :, :, :], CS[:, :, :, :], 0.5, None, ALU.mult).then_inc(cs_ready, 1)

            norm_steps = {(l, w): Steps(ch[f"dve_n{l}{w[0]}"], 1) for l in (0, 1) for w in ("attn", "ffn")}

            def mean(layer, which, b):
                side = 0 if which == "attn" else 1
                m = L[layer][which]
                st = norm_steps[layer, which]
                st.start(b)
                if which == "ffn":
                    wait(dve, L[layer]["attn"]["x_done"], b, 1, 1)
                elif layer == 1:
                    wait(dve, L[0]["ffn"]["x_done"], b, 1, 1)
                stand(dve, turns["dve"])
                for tt in range(TT):
                    ins = dve.bn_stats(ST[side][:, tt, :], xtile(b, tt))
                st(dve, ins)
                stand(dve, turns["dve"])
                dve.bn_aggr(MV[side][:, 0, :], ST[side][:, 0, :])
                dve.bn_aggr(MV[side][:, 1, :], ST[side][:, 1, :]).then_inc(m["mv"], 1)

            def norm(layer, which, b):
                side = 0 if which == "attn" else 1
                m = L[layer][which]
                wait(dve, m["mv"], b, 1, 1)
                wait(dve, m["rstd"], b, 1, 1)
                wait(dve, m["xnT"], b, 1, 0)
                for tt in range(TT):
                    ins = dve.tensor_scalar(XN[side][:, tt, :], xtile(b, tt), MV[side][:, tt, 0:1],
                                            RS[side][:, tt:tt + 1], ALU.subtract, ALU.mult)
                ins.then_inc(m["xn"], 1)

            def low_hT(layer, b):
                m = L[layer]["ffn"]
                wait(dve, m["hT_split"], b, 2, 1)
                dve.tensor_tensor(HFL[:, :, :], HTT[1][:, :, :], HFH[:, :, :].bitcast(F32), ALU.subtract)\
                    .then_inc(m["hT_split"], 1)

            def modulate(layer, which, b, bank):
                side = 0 if which == "attn" else 1
                m = L[layer][which]
                mc = MODC[:, layer, b:b + 1, 4 * side:4 * side + 4] if isinstance(b, int) else \
                    MODC[:, layer, bass.ds(b, 1), 4 * side:4 * side + 4]
                dve.tensor_copy(MB_[side][:, :], mc.rearrange("p a c -> p (a c)")).then_inc(mod_cols_in[layer][side], 1)
                wait(dve, mod_cols_in[layer][side], b, 1, 1)
                wait(dve, m["xnT"], b, 1, 1)
                if which == "ffn":
                    wait(dve, m["hT_split"], b, 2, 0)
                for k in range(KC):
                    ins = dve.tensor_scalar(HTT[side][:, k, :], bank[:, k * T:(k + 1) * T], MB_[side][:, 2 + k:3 + k],
                                            MB_[side][:, k:k + 1], ALU.mult, ALU.add)
                ins.then_inc(m["hT"], 1)

            def residual(layer, which, b, ps, Y, st, filled, per, read, bias=None):
                m = L[layer][which]
                g = spread(GB_[0 if which == "attn" else 1][:, :].rearrange("p (a d) -> p a d", a=1), 1, TT)
                wait(dve, s[filled], b, per, per)
                wait(dve, m["gate_in"], b, 16, 16)
                src = ps.rearrange("p (t d) -> p t d", t=TT)
                if bias is not None:
                    dve.tensor_tensor(Y, src, spread(bias[:, :].rearrange("p (a d) -> p a d", a=1), 1, TT),
                                      ALU.add).then_inc(s[read], 1)
                    wait(dve, s[read], b, 1, 1)
                    st(dve, dve.tensor_tensor(Y, Y, g, ALU.mult))
                else:
                    dve.tensor_tensor(Y, src, g, ALU.mult).then_inc(s[read], 1)
                    wait(dve, s[read], b, 1, 1)
                dve.tensor_tensor(xboth(b), xboth(b), Y, ALU.add).then_inc(m["x_done"], 1)

            dve.wait_ge(ld_x, 16)
            mean(0, "attn", 0)
            norm(0, "attn", 0)
            for l in range(2):
                for c in range(3):
                    dve.wait_ge(mod_ps, 3 * l + c + 1)
                    if l == 1 and c == 0:
                        dve.wait_ge(modT_ps, 1)
                    dve.tensor_copy(MODR[:, c * 512:(c + 1) * 512], ring[c][0:NB, :]).then_inc(mod_sb, 1)
                dve.wait_ge(mod_sb, 3 * l + 3)
                dve.wait_ge(modT_ps, l + 1)
                mt = ring[3][:, 0:64].rearrange("p (a s k b) -> p a s k b", a=2, s=2, k=KC)
                mc = MODC[:, l, :, :].rearrange("p b (a s k) -> p a s k b", a=2, s=2)
                for a in range(2):
                    dve.tensor_copy(mc[:, a, 0, :, :], mt[:, a, 0, :, :])
                    ins = dve.tensor_scalar(mc[:, a, 1, :, :], mt[:, a, 1, :, :], 1.0, None, ALU.add)
                ins.then_inc(modc_ready, 1)
                g = MODR[:, :].rearrange("p (a c d) -> p a c d", a=2, c=3)[:, :, 2, :]
                step(dve.scalar_tensor_tensor(GT[:, :, :], g, -1.0, g, ALU.mult, ALU.max))
                step(dve.tensor_scalar(GT[:, :, :], GT[:, :, :], 0.25, None, ALU.max))
                if l == 1:
                    dve.wait_ge(gates_stored, 16)
                step(dve.tensor_scalar(GR[:, :, :], g, 0.0, 2.0, ALU.is_ge, ALU.mult))
                step(dve.tensor_scalar(GR[:, :, :], GR[:, :, :], -1.0, None, ALU.add))
                dve.tensor_tensor(GR[:, :, :], GR[:, :, :], GT[:, :, :], ALU.mult).then_inc(gr_ready, 1)
            dve.wait_ge(w2_ping, 1)
            for h, src, dst in ((1, W2PING, W2RAW), (2, W2RAW, W2PING), (4, W2PING, W2F[:, :, :])):
                v = src.rearrange("p (n s h) d -> p n s (h d)", s=2, h=h)
                o = dst.rearrange("p (n s h) d -> p n s (h d)", s=2, h=h)
                dve.tensor_tensor(o[:, :, 0, :], v[:, :, 0, :], v[:, :, 1, :], ALU.add)
                ins = dve.tensor_tensor(o[:, :, 1, :], v[:, :, 0, :], v[:, :, 1, :], ALU.subtract)
                if h < 4:
                    step(ins)
                else:
                    ins.then_inc(w2_done, 1)

            a0 = Steps(ch["dve_a0"], 6 + 1 + 4)
            f0 = Steps(ch["dve_f0"], HT)

            def rope(b, c):
                rows = P if c < 2 else 64
                ps = ring[c][0:rows, :]
                if c < 2:
                    wait(dve, s["q_ps"], b, 2, c + 1)
                else:
                    wait(dve, s["k_ps"], b, 1, 1)
                dve.tensor_tensor(RT[0:rows, 0, :], ps[:, 0:T], cosT[0:rows, :], ALU.mult)
                dve.tensor_tensor(RT[0:rows, 1, :], ps[:, T:2 * T], sinT[0:rows, :], ALU.mult).then_inc(s["rope_done"], 1)
                wait(dve, s["rope_done"], b, 3, {0: 1, 2: 2, 1: 3}[c])
                a0(dve, dve.tensor_tensor(QR[0:rows, c, :], RT[0:rows, 0, :], RT[0:rows, 1, :], ALU.add))
                a0(dve, dve.tensor_copy(QH[0:rows, c, :], QR[0:rows, c, :]))
                dve.tensor_tensor(QL[0:rows, c, :], QR[0:rows, c, :], QH[0:rows, c, :].bitcast(F32),
                                  ALU.subtract).then_inc(s["qk_split"], 1)

            def hidden0(b, j):
                wait(dve, s["tanh0"], b, HT, j + 1)
                hid = HB[slot(j, HT)[0]][:, :]
                f0(dve, dve.scalar_tensor_tensor(hid, hid, 1.0, GUP[j % 2][:, 0:T], ALU.add, ALU.mult))
                dve.tensor_tensor(hid, hid, GUP[j % 2][:, T:2 * T], ALU.mult).then_inc(s["hid0"], 1)

            def turn0(ia, jf, nxt):
                def tile(j):
                    if jf is not None:
                        hidden0(jf, j)

                def evac_qst(m, bank):
                    wait(dve, s["qst_ps"], ia, 4, m + 1)
                    dve.tensor_copy(QST[:, m // 2, 2:4, :].rearrange("p r t -> p (r t)"), ring[bank]).then_inc(s["qst_dve"], 1)

                if jf is not None:
                    f0.start(jf)
                    mean(0, "ffn", jf)
                    norm(0, "ffn", jf)
                if ia is not None:
                    b = ia
                    a0.start(b)
                    rope(b, 0)
                    rope(b, 2)
                if jf is not None:
                    modulate(0, "ffn", jf, GUP[0])
                    low_hT(0, jf)
                if ia is not None:
                    rope(b, 1)
                    tile(0)
                    evac_qst(1, 1)
                    tile(1)
                    evac_qst(3, 2)
                    for g in range(KV):
                        c, gg = g // 4, g % 4
                        wait(dve, s["s_ps"], b, 2 * KV, 2 * g + 1)
                        dve.tensor_reduce(NM[:, 0, c, gg, :], SPB.rearrange("p (r t) -> p r t", r=REP), AX.X, ALU.max,
                                          negate=True).then_inc(s["max_done"], 1)
                        wait(dve, s["s_ps"], b, 2 * KV, 2 * g + 2)
                        dve.tensor_reduce(NM[:, 1, c, gg, :], SPA.rearrange("p (r t) -> p r t", r=REP), AX.X, ALU.max,
                                          negate=True).then_inc(s["max_done"], 1)
                        if g == 1:
                            tile(2)
                        if g == 5:
                            tile(3)
                    wait(dve, s["max_done"], b, 2 * KV, 2 * KV)
                    for c in range(2):
                        ins = dve.tensor_copy(NMS[:, :, :, 0, c, :], NM[:, :, c, :, :])
                    a0(dve, ins)
                    for c in range(2):
                        ins = dve.tensor_tensor(NMS[:, :, :, 1, c, :], NM[:, :, c, :, :], NMS[:, :, :, 0, c, :].bitcast(F32),
                                                ALU.subtract)
                    ins.then_inc(s["nm_split"], 1)
                    for j in (4, 5):
                        tile(j)
                    if isinstance(b, int) and b == 0:
                        dve.wait_ge(w2_split, 1)
                    for g in range(KV):
                        wait(dve, s["pv_ps"], b, KV, g + 1)
                        dve.tensor_copy(OS[:, g, :], CTX[g % 2][:, 0:T]).then_inc(s["o_done"], 1)
                        if g == 2:
                            tile(6)
                        if g == 5 and nxt is not None:
                            if isinstance(nxt, int) and nxt == 1:
                                dve.wait_ge(ld_x, 32)
                            mean(0, "attn", nxt)
                            norm(0, "attn", nxt)
                    tile(7)
                    for n in range(4):
                        tt, q = n // 2, n % 2
                        wait(dve, s["oT_ps"], b, 4, n + 1)
                        v = ring[n].rearrange("p (g r e) -> p g r e", g=4, r=REP)
                        rd = RD[:, tt, 4 * q:4 * q + 4, :]
                        a0(dve, dve.reciprocal(rd, v[:, :, :, DH]))
                        for g in range(4):
                            ins = dve.tensor_tensor(
                                CX[:, tt, (4 * q + g) * 32:(4 * q + g + 1) * 32].rearrange("p (r d) -> p r d", r=REP),
                                v[:, g, :, 0:DH],
                                spread(rd[:, g, :].rearrange("p (r o) -> p r o", o=1), 2, DH), ALU.mult)
                        ins.then_inc(s["ctx_done"], 1)
                    if nxt is not None:
                        modulate(0, "attn", nxt, ring[3])
                    residual(0, "attn", b, ring[1], RT[:, :, :], a0, "wo_ps", 1, "wo_read")
                else:
                    for j in range(HT):
                        tile(j)
                if jf is not None:
                    residual(0, "ffn", jf, FO, XN[1][:, :, :], f0, "down0_used", HT, "ffn0_read")

            modulate(0, "attn", 0, ring[3])
            layer0_turns(dve, turn0)

            a1 = Steps(ch["dve_a1"], 3)
            r1 = Steps(ch["dve_r1"], 14)
            step(dve.memset(S18[:, :, :], -1.0))
            step(dve.memset(CW[:, :, :], 0.5))

            def gated1(b, j):
                if j < MT:
                    bank, _ = bank1(j)
                    wait(dve, s["tanh1"], b, MT, j + 1)
                    hid = HB[slot(j, MT)[0]][:, :]
                    dve.scalar_tensor_tensor(hid, hid, 1.0, bank[:, 0:T], ALU.add, ALU.mult)\
                        .then_inc(s["act1"], 1)
                if j > 0:
                    wait(dve, s["gated1"], b, MT, j)
                    wait(dve, s["cb_ps"], b, MT, j)
                    last = HB[slot(j - 1, MT)[0]][:, :]
                    dve.tensor_tensor(last, last, CB[:, 0:T], ALU.mult)\
                        .then_inc(s["hid1"], 1)
                if j < MT:
                    wait(dve, s["act1"], b, MT, j + 1)
                    dve.tensor_tensor(hid, hid, bank[:, T:2 * T], ALU.mult)\
                        .then_inc(s["gated1"], 1)

            def max2(b):
                wait(dve, s["lg_ps"], b, 1, 1)
                dve.tensor_reduce(LMX[:, :], ring[2][:, 0:TT * EXP].rearrange("p (t e) -> p t e", t=TT), AX.X, ALU.max,
                                  negate=True).then_inc(s["lmax"], 1)

            def route(b, st):
                st.start(b)
                wait(dve, s["lexp"], b, TT, TT)
                st(dve, dve.reciprocal(RZ[:, :], ZZ[:, :]))
                for tt in range(TT):
                    ins = dve.tensor_scalar(S18[:, tt, 0:EXP], SE[:, tt, :], RZ[:, tt:tt + 1], None, ALU.mult)
                st(dve, ins)
                stand(dve, turns["dve"])
                for tt in range(TT):
                    ins = dve.max(M8[:, tt, :], S18[:, tt, 0:EXP])
                st(dve, ins)
                st(dve, dve.memset(M8[:, :, TOPK:8], -1.0))
                stand(dve, turns["dve"])
                for tt in range(TT):
                    ins = dve.match_replace(RP[:, tt, :], M8[:, tt, :], S18[:, tt, :], 0.0)
                st(dve, ins)
                st(dve, dve.tensor_tensor(CW[:, :, 0:EXP], S18[:, :, 0:EXP], RP[:, :, 0:EXP], ALU.subtract))
                st(dve, dve.tensor_reduce(WS[:, :], CW[:, :, 0:EXP], AX.X, ALU.add))
                st(dve, dve.tensor_scalar(WS[:, :], WS[:, :], 1e-20, None, ALU.add))
                st(dve, dve.reciprocal(WS[:, :], WS[:, :]))
                for tt in range(TT):
                    ins = dve.tensor_scalar(CW[:, tt, 0:EXP], CW[:, tt, 0:EXP], WS[:, tt:tt + 1], 0.5, ALU.mult, ALU.mult)
                st(dve, ins)
                wait(dve, s["cT_ps"], b, 1, 0)
                st(dve, dve.tensor_copy(CSP[:, :, 0, :], CW[:, :, :]))
                st(dve, dve.tensor_tensor(CW2[:, :, :], CW[:, :, :], CSP[:, :, 0, :], ALU.subtract))
                st(dve, dve.tensor_copy(CSP[:, :, 1, :], CW2[:, :, :]))
                st(dve, dve.tensor_tensor(CW2[:, :, :], CW2[:, :, :], CSP[:, :, 1, :], ALU.subtract))
                dve.tensor_copy(CSP[:, :, 2, :], CW2[:, :, :]).then_inc(s["csplit"], 1)

            def chain(what, b):
                if what == "mean":
                    a1.start(b)
                    mean(1, "attn", b)
                if what == "norm":
                    norm(1, "attn", b)
                if what == "modulate":
                    modulate(1, "attn", b, ring[0])
                if what == "max":
                    wait(dve, s["s1_ps"], b, 1, 1)
                    a1(dve, dve.tensor_reduce(NM1, ring[0].rearrange("p (t i) -> p t i", t=TT), AX.X, ALU.max, negate=True))
                    dve.tensor_scalar(NMB1, NM1, SC1, None, ALU.mult).then_inc(s["nmb1"], 1)
                if what == "softmax":
                    wait(dve, s["exp1"], b, TT, TT)
                    a1(dve, dve.reciprocal(RDN1, DEN1))
                    for tt in range(TT):
                        ins = dve.tensor_scalar(P1[:, tt, :], P1[:, tt, :], RDN1[:, tt:tt + 1], None, ALU.mult)
                    ins.then_inc(s["p1_norm"], 1)
                if what == "wo":
                    residual(1, "attn", b, ring[0], XN[0][:, :, :], a1, "wo1_ps", 1, "wo1_read", bias=BO1)
                    mean(1, "ffn", b)
                if what == "norm2":
                    norm(1, "ffn", b)
                if what == "modulate2":
                    modulate(1, "ffn", b, ring[1])
                if what == "max2":
                    max2(b)
                if what == "route":
                    route(b, r1)

            def turn1(ia, jf, prev):
                if jf is not None:
                    gated1(jf, 0)
                if prev is not None:
                    residual(1, "ffn", prev, FO, XN[1][:, :, :], None, "down1_used", MT, "ffn1_read")
                for j in range(MT - 1):
                    if jf is not None:
                        gated1(jf, j + 1)
                    if ia is not None:
                        chain(STEPS_DVE.get(j), ia)
                if ia is not None:
                    low_hT(1, ia)
                if jf is not None:
                    gated1(jf, MT)

            layer1_turns(dve, turn1)
            residual(1, "ffn", NB - 1, FO, XN[1][:, :, :], None, "down1_used", MT, "ffn1_read")

        @block.tensor
        def _(pe):
            mm = nc.tensor.matmul

            def xnT(layer, which, b, bank):
                side = 0 if which == "attn" else 1
                m = L[layer][which]
                wait(pe, m["xn"], b, 1, 1)
                for k in range(KC):
                    for tt in range(TT):
                        ins = nc.tensor.transpose(bank[:, k * T + tt * P:k * T + (tt + 1) * P],
                                                  XN[side][:, tt, k * P:(k + 1) * P], ident)
                ins.then_inc(m["xnT"], 1)

            def product3(out, terms, low_ready=None):
                first = True
                for mi, wi in ((0, 0), (0, 1), (1, 0)):
                    if mi == 1 and low_ready is not None:
                        low_ready()
                    for n, (w, m) in enumerate(terms):
                        last = mi == 1 and n == len(terms) - 1
                        ins = mm(out, w[wi], m[mi], start=first, stop=last)
                        first = False
                return ins

            pe.wait_ge(ld_consts, 48)
            pe.wait_ge(cs_ready, 1)
            pe.wait_ge(ld_mod, 32)
            for l in range(2):
                if l == 1:
                    pe.wait_ge(mod_sb, 3)
                for c in range(3):
                    for k in range(KC):
                        ins = mm(ring[c][0:NB, :], CS[:, l, k, :], WMOD[:, l, k, c * 512:(c + 1) * 512],
                                 start=(k == 0), stop=(k == KC - 1))
                    ins.then_inc(mod_ps, 1)
                if l == 1:
                    pe.wait_ge(modc_ready, 1)
                pe.wait_ge(mod_sb, 3 * l + 3)
                for a in range(2):
                    for sc in range(2):
                        for k in range(KC):
                            col = (3 * a + sc) * D + k * P
                            at = ((a * 2 + sc) * KC + k) * NB
                            ins = nc.tensor.transpose(ring[3][:, at:at + NB], MODR[:, col:col + P], ident[0:NB, 0:NB])
                ins.then_inc(modT_ps, 1)
            pe.wait_ge(ld_w2, 16)
            for a in range(HT):
                ins = mm(PS[:, 4 + a // 2, (a % 2) * D:(a % 2 + 1) * D], had, W2RAW[:, a, :], start=True, stop=True)
            ins.then_inc(w2_ps, 1)
            pe.wait_ge(modc_ready, 2)
            xnT(0, "attn", 0, ring[3])
            pe.wait_ge(w2_ping, 1)
            pe.wait_ge(consts_ready, 1)
            pe.wait_ge(ld_w0, 64)

            def gu0(b, j):
                if j == 0:
                    wait(pe, L[0]["ffn"]["hT_split"], b, 2, 1)
                    low = lambda: wait(pe, L[0]["ffn"]["hT_split"], b, 2, 2)
                else:
                    low = None
                wait(pe, s["hid0"], b, HT, j - 1)
                for h in range(2):
                    ins = product3(GUP[j % 2][:, h * T:(h + 1) * T],
                                   [((W13H[:, k, h, j * P:(j + 1) * P], W13L[:, k, h, j * P:(j + 1) * P]),
                                     (HFH[:, k, :], HFL[:, k, :])) for k in range(KC)], low)
                ins.then_inc(s["gu0_ps"], 1)

            def down(b, j, low, used, read, per, W):
                wait(pe, s[low], b, per, j + 1)
                if j == 0:
                    wait(pe, s[read], b, 1, 0)
                for tt in range(TT):
                    for n, (hid, w) in enumerate(((HH, W[0]), (HH, W[1]), (HL, W[0]))):
                        ins = mm(FO[:, tt * D:(tt + 1) * D], hid[slot(j, per)[0]][:, tt * P:(tt + 1) * P], w,
                                 start=(j == 0 and tt == 0 and n == 0), stop=(j == per - 1 and n == 2),
                                 skip_group_check=True)
                ins.then_inc(s[used], 1)

            def turn0(ia, jf, nxt):
                def ffn(k):
                    if jf is not None:
                        if k + 1 < HT:
                            gu0(jf, k + 1)
                        k -= 1
                        if k >= 0:
                            down(jf, k, "low0", "down0_used", "ffn0_read", HT,
                                 (W2HI[:, k, :], W2LO[:, k, :]))

                if isinstance(jf, int) and jf == 0:
                    pe.wait_ge(w13_split, 1)
                    pe.wait_ge(w2_split, 1)
                if ia is not None:
                    b = ia
                    H = HTT[0]
                    wait(pe, L[0]["attn"]["hT"], b, 1, 1)
                    wait(pe, s["wo_read"], b, 1, 0)

                    def proj_q(c):
                        for h in range(2):
                            for k in range(KC):
                                ins = mm(ring[c][:, h * T:(h + 1) * T], WQ[:, k, h, c * P:(c + 1) * P], H[:, k, :],
                                         start=(k == 0), stop=(k == KC - 1))
                        ins.then_inc(s["q_ps"], 1)

                    proj_q(0)
                    for h in range(2):
                        for k in range(KC):
                            ins = mm(ring[2][0:64, h * T:(h + 1) * T], WK[:, k, h, :], H[:, k, :],
                                     start=(k == 0), stop=(k == KC - 1))
                    ins.then_inc(s["k_ps"], 1)
                    proj_q(1)
                    for tt in range(TT):
                        for k in range(KC):
                            ins = mm(ring[3][:, tt * 64:(tt + 1) * 64], H[:, k, tt * P:(tt + 1) * P], WV[:, k, :],
                                     start=(k == 0), stop=(k == KC - 1))
                    ins.then_inc(s["v_ps"], 1)
                if jf is not None:
                    wait(pe, s["hid0"], jf, HT, 0)
                    xnT(0, "ffn", jf, GUP[0])
                    gu0(jf, 0)
                if ia is not None:
                    wait(pe, s["qk_split"], b, 3, 2)
                    for c in range(2):
                        for hl, src in enumerate((QH, QL)):
                            ins = mm(ring[2][:, c * T:(c + 1) * T], SELK[0:64, c, hl, :], src[0:64, 2, :],
                                     start=(hl == 0), stop=(hl == 1))
                    ins.then_inc(s["kst_ps"], 1)
                    wait(pe, s["qk_split"], b, 3, 3)

                    def q_stack(m, bank):
                        if bank == 3:
                            wait(pe, s["v_done"], b, 1, 1)
                        if bank == 2:
                            wait(pe, s["kst_done"], b, 1, 1)
                        for r2 in range(2):
                            for hl, src in enumerate((QH, QL)):
                                ins = mm(ring[bank][:, r2 * T:(r2 + 1) * T], SELQ[:, 2 * (m % 2) + r2, hl, :],
                                         src[:, m // 2, :], start=(hl == 0), stop=(hl == 1))
                        ins.then_inc(s["qst_ps"], 1)

                    q_stack(0, 0)
                    q_stack(1, 1)
                    ffn(0)
                    q_stack(2, 3)
                    q_stack(3, 2)
                    wait(pe, s["qst_act"], b, 2, 2)
                    wait(pe, s["qst_dve"], b, 2, 2)
                    mk = mask_b[:, :].rearrange("p (a s) -> p a s", a=1)
                    for g in range(KV):
                        c, R = g // 4, slice(32 * (g % 4), 32 * (g % 4) + 3 * DH)
                        wait(pe, s["max_done"], b, 2 * KV, 2 * g - 1 if g else 0)
                        mm(SPB.rearrange("p (r t) -> p r t", r=REP), IDB[:, :], spread(mk, 1, REP), start=True,
                           stop=False, skip_group_check=True)
                        for r in range(REP):
                            ins = mm(SPB[:, r * P:(r + 1) * P], QST[R, c, r, 0:P], KST[R, c, 0:P], start=False, stop=True,
                                     skip_group_check=True)
                        ins.then_inc(s["s_ps"], 1)
                        wait(pe, s["max_done"], b, 2 * KV, 2 * g)
                        for i in range(2):
                            mm(SPA[:, i * 512:(i + 1) * 512].rearrange("p (r t) -> p r t", r=2)[:, :, P:T], IDB[:, :],
                               spread(mk, 1, 2), start=True, stop=False, skip_group_check=True)
                        for r in range(REP):
                            ins = mm(SPA[:, r * T:(r + 1) * T], QST[R, c, r, P:T], KST[R, c, :], start=False, stop=True,
                                     skip_group_check=True)
                        ins.then_inc(s["s_ps"], 1)
                        if g == 1:
                            ffn(1)
                        if g == 5:
                            ffn(2)
                    ffn(3)
                    wait(pe, s["nm_split"], b, 1, 1)
                    stand(pe, turns["pe"])
                    for tt in range(TT):
                        ins = nc.tensor.transpose(ring[3][0:64, tt * P:(tt + 1) * P],
                                                  NMS[:, tt, :, :, :, :].rearrange("p g h c r -> p (g h c r)").bitcast(F32), ident)
                    ins.then_inc(s["nmT_ps"], 1)
                    ffn(4)
                    wait(pe, s["rows_in"], b, 128, 128)

                    def pv(g):
                        wait(pe, s["masked"], b, 2 * KV, 2 * g + 2)
                        wait(pe, s["o_done"], b, KV, g - 1)
                        o, pr = CTX[g % 2][:, 0:T], PR[g % 2]
                        for r in range(REP):
                            mm(o[32 * r:32 * r + 32, :], VA[:, 0, g, :], pr[:, r * T:(r + 1) * T], start=True, stop=False,
                               skip_group_check=True)
                        for r in range(REP):
                            ins = mm(o[32 * r:32 * r + 32, P:T], VA[:, 1, g, :], pr[:, 4 * T + r * P:4 * T + (r + 1) * P],
                                     start=False, stop=True, skip_group_check=True)
                        ins.then_inc(s["pv_ps"], 1)

                    for g in range(KV):
                        c, R = g // 4, slice(32 * (g % 4), 32 * (g % 4) + 3 * DH + 2)
                        wait(pe, s["exp_done"], b, 2 * KV, 2 * g - 1 if g else 0)
                        for i in range(2):
                            ins = mm(SPA[:, i * 512:(i + 1) * 512], KST[R, c, 0:P], QST[R, c, 2 * i:2 * i + 2, :],
                                     start=True, stop=True)
                        ins.then_inc(s["st_ps"], 1)
                        wait(pe, s["exp_done"], b, 2 * KV, 2 * g)
                        mm(SPB, KST[R, c, P:T], QST[R, c, :, P:T], start=True, stop=True).then_inc(s["st_ps"], 1)
                        if g:
                            pv(g - 1)
                        if g == 3:
                            ffn(5)
                    ffn(6)
                    pv(KV - 1)
                    for n in range(4):
                        tt, q = n // 2, n % 2
                        wait(pe, s["o_done"], b, KV, KV)
                        for g in range(4):
                            ins = nc.tensor.transpose(ring[n][:, g * P:(g + 1) * P], OS[:, 4 * q + g, tt * P:(tt + 1) * P], ident)
                        ins.then_inc(s["oT_ps"], 1)
                    ffn(7)
                    wait(pe, s["ctx_done"], b, 4, 4)
                    if nxt is not None:
                        xnT(0, "attn", nxt, ring[3])
                    for k in range(KC):
                        for tt in range(TT):
                            ins = nc.tensor.transpose(ring[0][:, k * T + tt * P:k * T + (tt + 1) * P],
                                                      CX[:, tt, k * P:(k + 1) * P], ident)
                    ins.then_inc(s["ctxT_ps"], 1)
                    ffn(HT)
                    wait(pe, s["ctxT_done"], b, 1, 1)
                    for tt in range(TT):
                        for k in range(KC):
                            ins = mm(ring[1][:, tt * D:(tt + 1) * D], CXT[:, k, tt * P:(tt + 1) * P], WO[:, k, :],
                                     start=(k == 0), stop=(k == KC - 1))
                    ins.then_inc(s["wo_ps"], 1)
                else:
                    for k in range(HT + 1):
                        ffn(k)

            layer0_turns(pe, turn0)

            def gu1(b, j):
                bank, before = bank1(j)
                wait(pe, s["gated1"], b, MT, before + 1)
                low = None
                if j == 0:
                    wait(pe, L[1]["ffn"]["hT_split"], b, 2, 1)
                    low = lambda: wait(pe, L[1]["ffn"]["hT_split"], b, 2, 2)
                if isinstance(b, int) and b == 0:
                    if j >= EARLY:
                        pe.wait_ge(late_done, j - EARLY + 1)
                    elif j == 0:
                        pe.wait_ge(early_done, 2 * EARLY)
                for h in range(2):
                    ins = product3(bank[:, h * T:(h + 1) * T],
                                   [(moe_tile(j, k, h, P), (HFH[:, k, :], HFL[:, k, :])) for k in range(KC)], low)
                ins.then_inc(s["gu1_ps"], 1)

            def cb(b, j):
                wait(pe, s["hid1"], b, MT, j)
                mm(CB[:, 0:T], SELC[:, j * P:(j + 1) * P], CTT[:, :], start=True, stop=True).then_inc(s["cb_ps"], 1)

            def down1(b, j):
                down(b, j, "low1", "down1_used", "ffn1_read", MT, moe_down(j, P))

            def chain(what, b):
                H = HTT[0]
                if what == "xnT":
                    wait(pe, s["wo1_read"], b, 1, 0)
                    xnT(1, "attn", b, ring[0])
                if what == "kv":
                    wait(pe, L[1]["attn"]["hT"], b, 1, 1)
                    wait(pe, L[1]["ffn"]["hT"], b, 1, 0)
                    for w, W in enumerate((WK1, WV1)):
                        for k in range(KC):
                            ins = mm(ring[1][:, w * T:(w + 1) * T], W[:, k, :], H[:, k, :], start=(k == 0), stop=(k == KC - 1))
                    ins.then_inc(s["kv1_ps"], 1)
                if what == "scores":
                    wait(pe, s["kv1_done"], b, 2, 2)
                    wait(pe, s["lexp"], b, TT, 0)
                    for i in range(TT):
                        ins = nc.tensor.transpose(ring[2][:, i * P:(i + 1) * P], VT1[:, i * P:(i + 1) * P], ident)
                    ins.then_inc(s["v1T_ps"], 1)
                    for tt in range(TT):
                        ins = mm(ring[0][:, tt * T:(tt + 1) * T], VT1[:, tt * P:(tt + 1) * P], KT1, start=True, stop=True)
                    ins.then_inc(s["s1_ps"], 1)
                if what == "probsT":
                    wait(pe, s["p1_norm"], b, 1, 1)
                    wait(pe, s["v1_done"], b, 1, 1)
                    for i in range(TT):
                        for tt in range(TT):
                            ins = nc.tensor.transpose(ring[2][:, i * T + tt * P:i * T + (tt + 1) * P],
                                                      P1[:, tt, i * P:(i + 1) * P], ident)
                    ins.then_inc(s["pT1_ps"], 1)
                if what == "ctx":
                    wait(pe, s["pT1_done"], b, 1, 1)
                    for i in range(TT):
                        ins = mm(ring[1][:, 0:T], V1[:, i, :], PT1[:, i, :], start=(i == 0), stop=(i == TT - 1))
                    ins.then_inc(s["o1_ps"], 1)
                if what == "wo":
                    wait(pe, s["o1_done"], b, 1, 1)
                    for tt in range(TT):
                        ins = mm(ring[0][:, tt * D:(tt + 1) * D], OT1[:, tt * P:(tt + 1) * P], WO1[:, :], start=True, stop=True)
                    ins.then_inc(s["wo1_ps"], 1)
                if what == "xnT2":
                    xnT(1, "ffn", b, ring[1])
                if what == "logits":
                    wait(pe, L[1]["ffn"]["hT"], b, 1, 1)
                    for tt in range(TT):
                        for k in range(KC):
                            ins = mm(ring[2][:, tt * EXP:(tt + 1) * EXP], HTT[1][:, k, tt * P:(tt + 1) * P], GW[:, k, :],
                                     start=(k == 0), stop=(k == KC - 1))
                    ins.then_inc(s["lg_ps"], 1)

            def turn1(ia, jf, prev):
                if jf is not None:
                    gu1(jf, 0)
                if prev is not None:
                    down1(prev, MT - 2)
                    down1(prev, MT - 1)
                if jf is not None:
                    wait(pe, s["csplit"], jf, 1, 1)
                    wait(pe, s["wo1_read"], jf, 1, 1)
                    stand(pe, turns["pe"])
                    for tt in range(TT):
                        ins = nc.tensor.transpose(ring[0].bitcast(BF16)[0:3 * NC, tt * P:(tt + 1) * P],
                                                  CSP[:, tt, :, :].rearrange("p h e -> p (h e)"), IDB[:, :])
                    ins.then_inc(s["cT_ps"], 1)
                    gu1(jf, 1)
                    wait(pe, s["cT_done"], jf, 1, 1)
                    cb(jf, 0)
                for j in range(MT - 1):
                    if jf is not None:
                        if j + 2 < MT:
                            gu1(jf, j + 2)
                        if j > 0:
                            down1(jf, j - 1)
                        cb(jf, j + 1)
                    if ia is not None:
                        chain(STEPS_PE.get(j), ia)

            pe.wait_ge(ld_l1, 80)
            pe.wait_ge(wo1_done, 1)
            pe.wait_ge(ld_sel, 16)
            layer1_turns(pe, turn1)
            down1(NB - 1, MT - 2)
            down1(NB - 1, MT - 1)


def kernel(**inputs):
    import concourse.bacc as bacc
    from concourse.bass_utils import run_bass_kernel_spmd

    nc = bacc.Bacc("TRN2", target_bir_lowering=False, num_devices=1)
    a = {k: np.asarray(v) for k, v in inputs.items()}

    def swapped(w):
        w = w.reshape(D, -1, 2, DH // 2)
        return w[:, :, ::-1, :].reshape(D, -1)

    def half(which):
        rows = a["L1_ffn_w13"][:, which * INNER:(which + 1) * INNER, :].reshape(EXP * INNER, D)
        return np.concatenate([rows, a["L1_ffn_sw13"][which * SHARED:(which + 1) * SHARED]])

    def rows(*parts):
        w = np.stack(parts)
        return w.reshape(len(parts), -1, P, w.shape[-1]).transpose(2, 1, 0, 3)

    def one(w):
        return rows(w)[:, :, 0, :]

    def tiles(w):
        return np.concatenate([w, np.zeros((MT * P - MOE, D), w.dtype)]).reshape(MT, P, D)

    def halves(which):
        return tiles(half(which)).transpose(0, 2, 1).reshape(MT, KC, P, P).transpose(2, 0, 1, 3)

    down = tiles(np.concatenate([a["L1_ffn_w2"].transpose(0, 2, 1).reshape(EXP * INNER, D), a["L1_ffn_sw2"].T]))
    arrays = {
        "x": a["L0_attn_x"].reshape(NB * T, D),
        "consts": shape_constants(),
        "selrows": expert_rows(),
        "cT": rows(a["L0_c"].T, a["L1_c"].T).transpose(0, 2, 1, 3),
        "wmod": rows(a["L0_wmod"], a["L1_wmod"]).transpose(0, 2, 1, 3),
        "wq": rows(a["L0_attn_Wq"], swapped(a["L0_attn_Wq"])),
        "wk": rows(a["L0_attn_Wk"], swapped(a["L0_attn_Wk"])),
        "wv": one(a["L0_attn_Wv"]),
        "wo": one(a["L0_attn_Wo"]),
        "w13": rows(a["L0_ffn_W1"].T, a["L0_ffn_W3"].T),
        "w2": one(a["L0_ffn_W2"].T),
        "wk1": one(a["L1_attn_Wk"]),
        "wv1": one(a["L1_attn_Wv"]),
        "bcol1": np.stack([a["L1_attn_bk"], a["L1_attn_bv"]], axis=1),
        "wo1": one(a["L1_attn_Wo"]),
        "bo1": a["L1_attn_bo"],
        "gate": one(a["L1_ffn_gate_w"].T),
        "moe": np.concatenate([halves(0).reshape(P, MT, KC * P), halves(1).reshape(P, MT, KC * P),
                               down.transpose(1, 0, 2)], axis=2),
    }
    arrays = {f"in_{k}": np.ascontiguousarray(v) for k, v in arrays.items()}
    args = [nc.dram_tensor(k, v.shape, mybir.dt.from_np(v.dtype), kind="ExternalInput").ap() for k, v in arrays.items()]
    gate_rows = nc.dram_tensor("gate_rows", (2, NB, 2, D), F32, kind="Internal").ap()
    out = nc.dram_tensor("out_x", (NB * T, D), F32, kind="ExternalOutput").ap()
    adaln_two_layers(nc, *args, gate_rows, out)
    r = run_bass_kernel_spmd(nc, [arrays], core_ids=[0])
    return r.results[0]["out_x"].reshape(NB, T, D)
```

```python
from contextlib import ExitStack

import concourse.bass as bass
from concourse import mybir
import numpy as np

F32 = mybir.dt.float32
F32R = mybir.dt.float32r
BF16 = mybir.dt.bfloat16
ALU = mybir.AluOpType
ACT = mybir.ActivationFunctionType
AX = mybir.AxisListType

P = 128
NB = 8
T = 256
D = 256
KC = D // P
TT = T // P
KV = 8
REP = 4
DH = 8
HID = 1024
HT = HID // P
EXP = 16
TOPK = 6
INNER = 176
SHARED = 2 * INNER
MOE = EXP * INNER + SHARED
MT = (MOE + P - 1) // P
HEADS1 = 16
SC0 = DH ** -0.5
SC1 = 1.0 / 128
EPS = 1e-5
MASK = -1e38
EARLY = 8
BF16_ONE = 0x3f80
NC = EXP + 1

C_ID, C_HAD, C_MASK, C_COS, C_SIN = 0, P, 2 * P, 3 * P, 3 * P + T
C_ONES = C_SIN + T
C_ALL = C_ONES + 1
S_Q = C_ALL
S_K = S_Q + REP * 2 * P
S_ALL = S_K + 2 * 2 * P


def shape_constants():
    c = np.zeros((P, S_ALL), np.float32)
    c[:, C_ID:C_ID + P] = np.eye(P)
    had = np.ones((1, 1), np.float32)
    while had.shape[0] < P:
        had = np.block([[had, had], [had, -had]])
    c[:, C_HAD:C_HAD + P] = had
    t = np.arange(P)
    c[:, C_MASK:C_MASK + P] = np.where(t[None, :] > t[:, None], MASK, 0.0)
    theta = (1.0 / np.float32(10000.0) ** (np.arange(0, DH, 2, dtype=np.float32) / DH)).astype(np.float32)
    freqs = np.outer(np.arange(T, dtype=np.float32), theta).astype(np.float32)
    d = np.arange(P) % DH
    c[:, C_COS:C_COS + T] = np.cos(freqs).T[d % (DH // 2)]
    c[:, C_SIN:C_SIN + T] = np.sin(freqs).T[d % (DH // 2)] * np.where(d < DH // 2, -1.0, 1.0)[:, None]
    for g in range(4):
        for d in range(DH):
            for r in range(REP):
                row = 32 * g + DH * r + d
                q = S_Q + r * 2 * P + 32 * g + d
                c[row, q] = c[row, q + DH] = 1.0
                c[row, q + P + 2 * DH] = 1.0
            for h in range(2):
                row = 32 * h + DH * g + d
                k = S_K + h * 2 * P + 32 * g + d
                c[row, k] = c[row, k + 2 * DH] = 1.0
                c[row, k + P + DH] = 1.0
        c[32 * g + 3 * DH:32 * g + 3 * DH + 2, C_ONES] = 1.0
    return c


def expert_rows():
    s = np.zeros((3 * NC, MT * P), np.uint16)
    for p in range(3):
        for e in range(EXP):
            s[p * NC + e, e * INNER:(e + 1) * INNER] = BF16_ONE
        s[p * NC + EXP, EXP * INNER:MOE] = BF16_ONE
    return s


def spread(ap, axis, n):
    shape = list(ap.shape)
    shape[axis] = n
    return ap.to_broadcast(shape)


def wait(eng, sem, b, per, n):
    v = b * per + n
    if isinstance(v, int) and v <= 0:
        return
    eng.wait_ge(sem, v)


def stand(eng, turns):
    eng.sem_inc(turns, 1)


class Steps:

    def __init__(self, sem, per, base=0):
        self.sem, self.per, self.base, self.b, self.n = sem, per, base, 0, 0

    def start(self, b):
        assert self.n in (0, self.per), (self.sem.name if hasattr(self.sem, "name") else "", self.n, self.per)
        self.b, self.n = b, 0

    def __call__(self, eng, ins, hold=True):
        ins.then_inc(self.sem, 1)
        self.n += 1
        if hold:
            eng.wait_ge(self.sem, self.base + self.b * self.per + self.n)


def adaln_two_layers(nc, x, consts, selrows, cT, wmod, wq, wk, wv, wo, w13, w2, wk1, wv1, bcol1, wo1, bo1,
                     gate, moe, gate_rows, out):
    ctx = ExitStack()
    with ctx:
        def sb(name, shape, dt=F32):
            return ctx.enter_context(nc.sbuf_tensor(name, shape, dt))

        def sem(name):
            return ctx.enter_context(nc.semaphore(name))

        XA = sb("residual", [P, NB * TT, D])
        IDT = sb("ident", [P, P])
        ident = IDT[:, :]
        WK1 = sb("wk1", [P, KC, P])
        WV1 = sb("wv1", [P, KC, P])
        BC1 = sb("bias_kv1", [P, 2])
        WO1 = sb("wo1_summed", [P, D])
        BO1 = sb("bo1", [P, D])
        GW = sb("gate_w", [P, KC, EXP])
        CT = sb("cond_T", [P, 2, KC, NB])
        CS = sb("cond_silu", [P, 2, KC, NB])
        MODC = sb("mod_cols", [P, 2, NB, 8])
        MB_ = [sb("mod_b_attn", [P, 4]), sb("mod_b_ffn", [P, 4])]
        GB_ = [sb("gate_b_attn", [P, D]), sb("gate_b_ffn", [P, D])]
        IDB = sb("ident_bf16", [P, P], BF16)
        HALF = sb("minus_half", [P, TT])
        ST = [sb("bn_attn", [P, TT, 6]), sb("bn_ffn", [P, TT, 6])]
        MV = [sb("mv_attn", [P, TT, 2]), sb("mv_ffn", [P, TT, 2])]
        VE = [sb("ve_attn", [P, TT]), sb("ve_ffn", [P, TT])]
        RS = [sb("rstd_attn", [P, TT]), sb("rstd_ffn", [P, TT])]
        XN = [sb("xn_attn", [P, TT, D]), sb("xn_ffn", [P, TT, D])]
        HTT = [sb("hT_attn", [P, KC, T]), sb("hT_ffn", [P, KC, T])]
        HFH = sb("hT_ffn_high", [P, KC, T], F32R)
        HFL = sb("hT_ffn_low", [P, KC, T], F32R)
        HB = [sb(f"hid{i}", [P, T]) for i in range(3)]
        HH = [sb(f"hid_high{i}", [P, T], F32R) for i in range(3)]
        HL = [sb(f"hid_low{i}", [P, T], F32R) for i in range(3)]

        def slot(j, per):
            def of(j):
                return 1 if j % 3 == 0 and j == per - 1 else j % 3
            before = j - 1
            while of(before % per) != of(j):
                before -= 1
            return of(j), before

        def aliased(name, shape, *names):
            with nc.sbuf_tensor(name, shape, F32) as t:
                return t

        TW = 4 * P + D
        SETUP = aliased("setup_area", [P, EARLY * 2 * TW])
        WHI_A = sb("moe_high_a", [P, EARLY, TW], F32R)
        RAW_A = aliased("moe_raw_a", [P, EARLY, TW])
        WLO_A = sb("moe_low_a", [P, EARLY, TW], F32R)
        WMOD = SETUP[:, 0:6144].rearrange("p (l k n) -> p l k n", l=2, k=KC)
        WO1RAW = SETUP[:, 0:4096].rearrange("p (h d) -> p h d", h=HEADS1)
        W2RAW = SETUP[:, 6144:8192].rearrange("p (a d) -> p a d", a=HT)
        W2PING = SETUP[:, 8192:10240].rearrange("p (a d) -> p a d", a=HT)
        SELQK = SETUP[:, 10240:10240 + S_ALL - S_Q]

        layer0 = ExitStack()

        def s0(name, shape, dt=F32):
            return layer0.enter_context(nc.sbuf_tensor(name, shape, dt))

        W13H = s0("w13_high", [P, KC, 2, HID], F32R)
        W13RAW = aliased("w13_raw", [P, KC, 2, HID])
        W13L = s0("w13_low", [P, KC, 2, HID], F32R)
        W2HI = s0("w2_hadamard_high", [P, HT, D], F32R)
        W2LO = s0("w2_hadamard_low", [P, HT, D], F32R)
        RT = s0("rope_tmp", [P, 2, T])
        CON = s0("constants", [P, C_ALL])
        had = CON[:, C_HAD:C_HAD + P]
        cosT, sinT = CON[:, C_COS:C_COS + T], CON[:, C_SIN:C_SIN + T]
        ones24 = CON[:, C_ONES:C_ONES + 1]
        mask_b = s0("mask_bf16", [P, P], BF16)
        SELQ = s0("sel_q", [P, REP, 2, P], F32R)
        SELK = s0("sel_k", [P, 2, 2, P], F32R)
        WQ = s0("wq", [P, KC, 2, D])
        WK = s0("wk", [P, KC, 2, 64])
        WV = s0("wv", [P, KC, 64])
        WO = s0("wo", [P, KC, D])
        QR = s0("qk_rot", [P, 3, T])
        QH = s0("qk_high", [P, 3, T], F32R)
        QL = s0("qk_low", [P, 3, T], F32R)
        QST = s0("q_stack", [P, 2, REP, T], F32R)
        KST = s0("k_stack", [P, 2, T], F32R)
        VA = s0("v_aug", [P, TT, KV, 32])
        NM = s0("minus_max", [P, TT, 2, 4, REP])
        NMS = s0("minus_max_split", [P, TT, 2, 2, 4, REP], F32R)
        NMT = s0("minus_max_T", [32, 2, T], F32)
        PR = [s0("probs0", [P, 6 * T]), s0("probs1", [P, 6 * T])]
        MODR = PR[0][0:NB, :]
        GR = PR[1][0:NB, 0:2 * D].rearrange("b (s d) -> b s d", s=2)
        GT = PR[1][0:NB, 2 * D:4 * D].rearrange("b (s d) -> b s d", s=2)
        OS = s0("ctx_raw", [P, KV, T])
        W2F = OS
        RD = s0("recip_den", [P, TT, KV, REP])
        CX = XN[0]
        CXT = XN[1][:, :, :]
        layer0.close()

        LATE = MT - EARLY
        LOTS = [0, 1, 3, 6, 10, 14, LATE]
        WHI_B = sb("moe_high_b", [P, LATE, TW], F32R)
        RAW_B = aliased("moe_raw_b", [P, LATE, TW])
        WLO_B = sb("moe_low_b", [P, LATE, TW], F32R)
        SELC = sb("sel_expert", [3 * NC, MT * P], BF16)
        L1B = sb("attn1", [P, 3, T])
        KT1, VT1, OT1 = L1B[:, 0, :], L1B[:, 1, :], L1B[:, 0, :]
        V1 = L1B[:, 2, :].rearrange("p (i d) -> p i d", i=TT)
        PT1 = HTT[0]
        P1 = XN[0]
        SM = sb("softmax1", [P, 8])
        NM1, NMB1, DEN1, RDN1 = SM[:, 0:2], SM[:, 2:4], SM[:, 4:6], SM[:, 6:8]
        LMX = sb("r_max", [P, TT])
        SE = sb("r_exp", [P, TT, EXP])
        ZZ = sb("r_sum", [P, TT])
        RZ = sb("r_rsum", [P, TT])
        S18 = sb("r_scores", [P, TT, EXP + 2])
        M8 = sb("r_top8", [P, TT, 8])
        RP = sb("r_replaced", [P, TT, EXP + 2])
        CW = sb("r_combine", [P, TT, NC])
        CW2 = sb("r_rest", [P, TT, NC])
        WS = sb("r_wsum", [P, TT])
        CSP = sb("r_split", [P, TT, 3, NC], BF16)
        CTT = sb("r_split_T", [3 * NC, T], BF16)

        def moe_tile(j, k, h, rows):
            hi, lo, n = (WHI_A, WLO_A, j) if j < EARLY else (WHI_B, WLO_B, j - EARLY)
            at = (2 * h + k) * P
            return hi[:, n, at:at + rows], lo[:, n, at:at + rows]

        def moe_down(j, rows):
            hi, lo, n = (WHI_A, WLO_A, j) if j < EARLY else (WHI_B, WLO_B, j - EARLY)
            return hi[0:rows, n, 4 * P:TW], lo[0:rows, n, 4 * P:TW]

        PS = ctx.enter_context(nc.psum_tensor("psum", [P, 8, 512], F32))
        SPA = PS[:, 0:2, :].rearrange("p b n -> p (b n)")
        SPB = PS[:, 2, :]
        ring = [PS[:, i, :] for i in range(4)]
        OP = PS[:, 4, :]
        GUP = [PS[:, 5, :], PS[:, 6, :]]
        FO = PS[:, 7, :]
        CTX = [OP, ring[3]]
        B_MOD = [(ring[0], ring[1], ring[2]), (GUP[0], GUP[1], FO)]
        B_MODT = [ring[3], GUP[0]]
        B_Q, B_K, B_V = (ring[0], OP), GUP[0], ring[3]
        B_KST, B_QST = ring[1], (ring[3], ring[0], ring[3], ring[3])
        B_MAX = (ring[1], ring[0], ring[2], OP)
        B_NMT = ring[3]
        B_OT = (ring[1], ring[2], ring[3], OP)
        B_XNT, B_CTXT, B_WO = ring[0], ring[1], ring[2]
        CB = OP
        GUP1 = [PS[:, 5, :], PS[:, 6, :], PS[:, 3, :]]

        def bank1(j):
            last = MT - 1
            if j == last:
                return GUP1[1], j - 2
            return GUP1[j % 3], (j - 3 if j >= 3 else {0: last - 3, 1: last, 2: last - 1}[j] - MT)

        ld_mod1, ld_selqk = sem("ld_mod1"), sem("ld_sel_qk")
        (ld_x, ld_consts, ld_w0, ld_w13, ld_w2, ld_mod, ld_wo1, ld_rest, ld_early) = (
            sem(n) for n in ("ld_x", "ld_constants", "ld_attn0", "ld_w13", "ld_w2raw", "ld_mod", "ld_wo1raw",
                             "ld_rest", "ld_moe_early"))
        ld_late = [sem(f"ld_moe_late{i}") for i in range(len(LOTS) - 1)]
        gates_stored, out_stored = sem("gates_stored"), sem("out_stored")
        dve_setup, pool_setup, act_setup = sem("dve_setup"), sem("pool_setup"), sem("act_setup")
        (cs_ready, mod_ps, mod_sb, modT_ps, modc_ready, gr_ready, w2_ps, w2_ping, w2_done, w2_split, w13_split,
         wo1_done, wo1_ps, consts_ready, late_high, early_done) = (sem(n) for n in (
            "cond_ready", "mod_in_psum", "mod_in_sbuf", "modT_in_psum", "mod_cols_ready", "gate_rows_ready",
            "w2_in_psum", "w2_evacuated", "w2_ready", "w2_split", "w13_split", "wo1_ready", "wo1_in_psum", "consts_ready",
            "late_high", "early_done"))
        late_low = [sem("late_low_dve"), sem("late_low_pool")]

        def names(layer, which):
            return {n: sem(f"{n}_{layer}{which}") for n in (
                "gate_in", "mv", "rstd", "xn", "xnT", "hT", "hT_split", "x_done")}

        L = [dict(attn=names(0, "a"), ffn=names(0, "f")), dict(attn=names(1, "a"), ffn=names(1, "f"))]
        s = {n: sem(n) for n in (
            "q_ps", "k_ps", "v_ps", "rope_done", "qk_rot", "qk_high", "qk_split", "v_done", "kst_ps", "kst_done", "qst_ps",
            "qst_act", "s_ps", "max_done", "nm_split", "nmT_ps", "nmT_done",
            "st_ps", "exp_done", "masked", "pv_ps", "o_done", "oT_ps", "ctx_done", "ctxT_ps", "ctxT_done",
            "wo_ps", "wo_read",
            "gu0_ps", "tanh0", "hid0", "high0", "low0", "down0_used", "ffn0_read",
            "gu1_ps", "cb_ps", "tanh1", "act1", "gated1", "hid1", "high1", "low1", "down1_used", "ffn1_read",
            "kv1_ps", "kv1_done", "v1T_ps", "v1_done", "s1_ps", "nmb1", "exp1", "p1_norm", "pT1_ps", "pT1_done",
            "o1_ps", "o1_done", "wo1_ps", "wo1_read",
            "lg_ps", "lmax", "lexp", "csplit", "cT_ps", "cT_done")}
        ch = {k: sem("steps_" + k) for k in ("dve_a0", "dve_f0", "dve_a1", "dve_r1", "dve_na", "dve_nf", "pool_a", "pool_f")}
        rows_in = [sem(f"rows_in{c}") for c in range(2)]
        mod_cols_in = [[sem(f"mod_cols_in_{l}{w}") for w in "af"] for l in range(2)]
        turns = {e: sem("turns_" + e) for e in ("dve", "pe", "pool")}

        def xtile(b, tt):
            if isinstance(b, int):
                return XA[:, b * TT + tt, :]
            return XA[:, bass.ds(b * TT + tt, 1), :].rearrange("p a d -> p (a d)")

        def xboth(b):
            return XA[:, b * TT:(b + 1) * TT, :] if isinstance(b, int) else XA[:, bass.ds(b * TT, TT), :]

        def layer0_turns(eng, turn):
            turn(0, None, 1)
            turn(1, 0, 2)
            with eng.Fori(2, NB - 1) as i:
                turn(i, i - 1, i + 1)
            turn(NB - 1, NB - 2, None)

        def before(jf):
            return None if jf is None or (isinstance(jf, int) and jf == 0) else jf - 1

        PE0 = {2: [("gu", 1)], 3: [("gu", 2)], 4: [("down", 0)], 5: [("down", 1)], 6: [("gu", 3)],
               7: [("gu", 4)], 8: [("down", 2)], 9: [("gu", 5)], 10: [("down", 3)], 11: [("down", 4)], 12: [("gu", 6)]}
        DVE0 = {2: 0, 3: 1, 4: 2, 7: 3}
        DVE0_CTX = {0: 5, 3: 6}
        ACT0_CTX = {1: [("high", 4), ("tanh", 5)], 2: [("high", 5)], 4: [("tanh", 6)], 5: [("high", 6)]}
        POOL0_CTX = {1: 4, 3: 5, 6: 6}

        def layer1_turns(eng, turn):
            turn(1, 0, None)
            with eng.Fori(2, NB) as i:
                turn(i, i - 1, i - 2)
            turn(None, NB - 1, NB - 2)

        STEPS_PE = {2: "xnT", 4: "kv", 6: "scores", 10: "probsT", 12: "ctx", 14: "wo", 18: "xnT2", 20: "logits"}
        STEPS_ACT = {3: "modulate", 5: "kv", 7: "v", 8: "exp", 11: "probsT", 13: "ctx", 19: "modulate2", 21: "route"}
        STEPS_DVE = {0: "mean", 1: "norm", 7: "max", 9: "softmax", 15: "wo", 16: "mean2", 17: "norm2", 21: "max2",
                     22: "route"}
        STEPS_POOL = {0: "rstd", 16: "rstd2"}

        def late_at(jf, j):
            return j if isinstance(jf, int) and jf == 0 and j < LATE else None

        block = ctx.enter_context(nc.Block())

        @block.sync
        def _(sp):
            sp.dma_start(CT[:, :, :, :], cT).then_inc(ld_x, 16)
            sp.dma_start(XA[:, 0:TT, :], x[0:T, :].rearrange("(n p) d -> p n d", p=P)).then_inc(ld_x, 16)
            sp.dma_start(WMOD[:, 0, :, :], wmod[:, 0, :, :]).then_inc(ld_mod, 16)
            sp.dma_start(CON[:, :], consts[:, 0:C_ALL]).then_inc(ld_consts, 16)
            sp.dma_start(IDT[:, :], consts[:, C_ID:C_ID + P]).then_inc(ld_consts, 16)
            sp.dma_start(W2RAW, w2).then_inc(ld_w2, 16)
            sp.dma_start(WK[:, :, :, :], wk).then_inc(ld_w0, 16)
            sp.dma_start(WV[:, :, :], wv).then_inc(ld_w0, 16)
            sp.dma_start(WQ[:, :, :, :], wq).then_inc(ld_w0, 16)
            sp.dma_start(SELQK, consts[:, S_Q:S_ALL]).then_inc(ld_selqk, 16)
            sp.dma_start(WMOD[:, 1, :, :], wmod[:, 1, :, :]).then_inc(ld_mod1, 16)
            sp.dma_start(W13RAW[:, :, :, :], w13).then_inc(ld_w13, 16)
            sp.dma_start(WO[:, :, :], wo).then_inc(ld_rest, 16)
            sp.dma_start(XA[:, TT:NB * TT, :], x[T:NB * T, :].rearrange("(n p) d -> p n d", p=P)).then_inc(ld_rest, 16)
            sp.dma_start(WK1[:, :, :], wk1).then_inc(ld_rest, 16)
            sp.dma_start(WV1[:, :, :], wv1).then_inc(ld_rest, 16)
            sp.dma_start(BC1[:, :], bcol1).then_inc(ld_rest, 16)
            sp.dma_start(BO1[:, :], spread(bo1.rearrange("(a d) -> a d", a=1), 0, P)).then_inc(ld_rest, 16)
            sp.dma_start(GW[:, :, :], gate).then_inc(ld_rest, 16)

            def store_gates(l):
                sp.wait_ge(gr_ready, l + 1)
                sp.dma_start(gate_rows[l], GR[:, :, :]).then_inc(gates_stored, 16)
                sp.wait_ge(gates_stored, 16 * (l + 1))

            store_gates(0)

            def gate_row(layer, side, b):
                n = L[layer]["attn" if side == 0 else "ffn"]
                wait(sp, n["x_done"], b, 1, 0)
                src = gate_rows[layer, b:b + 1, side, :] if isinstance(b, int) else \
                    gate_rows[layer, bass.ds(b, 1), side, :]
                sp.dma_start(GB_[side][:, :], spread(src, 0, P)).then_inc(n["gate_in"], 16)

            def turn0(ia, jf, nxt):
                if ia is not None:
                    gate_row(0, 0, ia)
                    if isinstance(ia, int) and ia == 0:
                        store_gates(1)
                    if isinstance(ia, int) and ia == 1:
                        sp.wait_ge(wo1_done, 1)
                        sp.wait_ge(w2_done, 1)
                        sp.wait_ge(act_setup, 2)
                        sp.dma_start(RAW_A[:, :, :], moe[:, 0:EARLY, :]).then_inc(ld_early, 16)
                    for c in range(2):
                        wait(sp, s["nmT_done"], ia, 2, c + 1)
                        for hl in range(2):
                            row = 3 * DH + hl
                            sp.dma_start(
                                QST[row:P:32, c, :, :].rearrange("g r t -> g (r t)").bitcast(F32),
                                NMT[16 * hl:16 * hl + 16, c, :]).then_inc(rows_in[c], 16)
                        if isinstance(ia, int) and ia == 0 and c == 0:
                            sp.wait_ge(mod_ps, 6)
                            sp.dma_start(WO1RAW, wo1).then_inc(ld_wo1, 16)
                if jf is not None:
                    gate_row(0, 1, jf)

            def turn1(ia, jf, prev):
                if ia is not None:
                    gate_row(1, 0, ia)
                if prev is not None:
                    store(prev)
                if jf is not None:
                    gate_row(1, 1, jf)

            def store(b):
                wait(sp, L[1]["ffn"]["x_done"], b, 1, 1)
                dst = out[b * T:(b + 1) * T, :] if isinstance(b, int) else out[bass.ds(b * T, T), :]
                sp.dma_start(dst.rearrange("(n p) d -> p n d", p=P), xboth(b)).then_inc(out_stored, 16)

            layer0_turns(sp, turn0)
            gate_row(0, 1, NB - 1)
            sp.wait_ge(L[0]["attn"]["x_done"], NB)
            gate_row(1, 0, 0)
            for n, lot in enumerate(ld_late):
                lo, hi = LOTS[n], LOTS[n + 1]
                sp.dma_start(RAW_B[:, lo:hi, :], moe[:, EARLY + lo:EARLY + hi, :]).then_inc(lot, 16)
                if n == 1:
                    sp.dma_start(SELC[:, :], selrows.bitcast(BF16)).then_inc(lot, 16)
            sp.wait_ge(L[0]["ffn"]["x_done"], NB)
            layer1_turns(sp, turn1)
            store(NB - 1)
            sp.wait_ge(out_stored, 16 * NB)

        @block.gpsimd
        def _(po):
            n_ = [0]

            def step(ins):
                n_[0] += 1
                ins.then_inc(pool_setup, 1)
                po.wait_ge(pool_setup, n_[0])

            step(po.memset(HALF[:, :], -0.5))

            norm_steps = {(l, w): Steps(ch[f"pool_{w[0]}"], 1, l * NB) for l in (0, 1) for w in ("attn", "ffn")}

            def norm(layer, which, b):
                side = 0 if which == "attn" else 1
                m = L[layer][which]
                st = norm_steps[layer, which]
                st.start(b)
                wait(po, m["mv"], b, 1, 1)
                wait(po, m["xn"], b, 1, 0)
                stand(po, turns["pool"])
                st(po, po.tensor_scalar(VE[side][:, :], MV[side][:, :, 1], EPS, None, ALU.add))
                po.tensor_tensor(RS[side][:, :], VE[side][:, :], HALF[:, :], ALU.pow).then_inc(m["rstd"], 1)

            def low_tile(j, b, per, high, low):
                i, _ = slot(j, per)
                wait(po, s[high], b, per, j + 1)
                po.tensor_tensor(HL[i][:, :], HB[i][:, :], HH[i][:, :].bitcast(F32), ALU.subtract)\
                    .then_inc(s[low], 1)

            def setup_splits():
                po.wait_ge(w2_split, 1)
                po.tensor_tensor(W2LO[:, :, :], W2F[:, :, :], W2HI[:, :, :].bitcast(F32), ALU.subtract)\
                    .then_inc(w2_split, 1)
                po.wait_ge(w13_split, 1)
                po.tensor_tensor(W13L[:, :, :, :], W13RAW[:, :, :, :], W13H[:, :, :, :].bitcast(F32), ALU.subtract)\
                    .then_inc(w13_split, 1)

            def early(b):
                hi, raw, lo = (w[:, b, :] if isinstance(b, int) else
                               w[:, bass.ds(b, 1), :].rearrange("p a n -> p (a n)") for w in (WHI_A, RAW_A, WLO_A))
                if isinstance(b, int) and b == 0:
                    po.wait_ge(ld_early, 16)
                po.tensor_copy(hi, raw).then_inc(early_done, 1)
                wait(po, early_done, b, 2, 1)
                stand(po, turns["pool"])
                po.tensor_tensor(lo, raw, hi.bitcast(F32), ALU.subtract).then_inc(early_done, 1)

            def turn0(ia, jf, nxt):
                def tile(j):
                    if jf is not None:
                        low_tile(j, jf, HT, "high0", "low0")

                if jf is not None:
                    norm(0, "ffn", jf)
                if ia is not None:
                    if isinstance(ia, int) and ia == 0:
                        setup_splits()
                    for j in range(3):
                        tile(j)
                    if not (isinstance(ia, int) and ia == 0):
                        early(ia - 1)
                    tile(3)
                    for g in range(KV):
                        pa = PR[g % 2][:, 0:4 * T].rearrange("p (r t) -> p r t", r=REP)[:, :, 0:P]
                        pb = PR[g % 2][:, 4 * T:6 * T].rearrange("p (r t) -> p r t", r=REP)
                        for n, pr in enumerate((pa, pb)):
                            wait(po, s["exp_done"], ia, 2 * KV, 2 * g + n + 1)
                            stand(po, turns["pool"])
                            po.affine_select(out=pr, in_=pr, compare_op=ALU.is_ge, fill=0.0, base=0,
                                             pattern=[[0, REP], [1, P]], channel_multiplier=-1).then_inc(s["masked"], 1)
                        if g in POOL0_CTX:
                            tile(POOL0_CTX[g])
                        if g == 2 and nxt is not None:
                            norm(0, "attn", nxt)
                    tile(7)

            norm(0, "attn", 0)
            layer0_turns(po, turn0)
            norm(0, "ffn", NB - 1)
            for i in range(3 * HT):
                if STEPS_POOL.get(i) == "rstd":
                    norm(1, "attn", 0)
                if STEPS_POOL.get(i) == "rstd2":
                    norm(1, "ffn", 0)
                if i % 3 == 2:
                    low_tile(i // 3, NB - 1, HT, "high0", "low0")
            early(NB - 1)

            def turn1(ia, jf, prev):
                for j in range(MT - 1):
                    if jf is not None:
                        low_tile(j, jf, MT, "high1", "low1")
                    if ia is not None and STEPS_POOL.get(j) == "rstd":
                        norm(1, "attn", ia)
                    if ia is not None and STEPS_POOL.get(j) == "rstd2":
                        norm(1, "ffn", ia)
                    n = late_at(jf, j)
                    if n is not None and n % 2 == 1:
                        po.wait_ge(late_high, n + 1)
                        po.tensor_tensor(WLO_B[:, n, :], RAW_B[:, n, :], WHI_B[:, n, :].bitcast(F32), ALU.subtract)\
                            .then_inc(late_low[1], 1)
                if jf is not None:
                    low_tile(MT - 1, jf, MT, "high1", "low1")

            layer1_turns(po, turn1)

        @block.scalar
        def _(act):
            act.wait_ge(ld_x, 32)
            nc.scalar.activation(CS[:, :, :, :], CT[:, :, :, :], ACT.Tanh, scale=0.5).then_inc(act_setup, 1)
            act.wait_ge(w2_ps, 1)
            nc.scalar.activation(W2PING.rearrange("p a d -> p (a d)"), PS[:, 4:8, :].rearrange("p b n -> p (b n)"),
                                 ACT.Copy, scale=1.0 / 64).then_inc(w2_ping, 1)

            def high_weights():
                act.wait_ge(ld_selqk, 16)
                nc.scalar.activation(SELQ[:, :, :, :], SELQK[:, 0:S_K - S_Q].rearrange("p (r h n) -> p r h n", r=REP, h=2),
                                     ACT.Copy)
                nc.scalar.activation(SELK[:, :, :, :], SELQK[:, S_K - S_Q:S_ALL - S_Q].rearrange("p (c h n) -> p c h n", c=2, h=2),
                                     ACT.Copy).then_inc(act_setup, 1)
                act.wait_ge(w2_done, 1)
                nc.scalar.activation(W2HI[:, :, :], W2F[:, :, :], ACT.Copy).then_inc(w2_split, 1)


            def split_hT(layer, b):
                m = L[layer]["ffn"]
                wait(act, m["hT"], b, 1, 1)
                nc.scalar.activation(HFH[:, :, :], HTT[1][:, :, :], ACT.Copy).then_inc(m["hT_split"], 1)

            def tanh0(b, j):
                wait(act, s["gu0_ps"], b, HT, j + 1)
                i, before = slot(j, HT)
                wait(act, s["low0"], b, HT, before + 1)
                nc.scalar.activation(HB[i][:, :], GUP[j % 2][:, 0:T], ACT.Tanh, scale=0.5).then_inc(s["tanh0"], 1)

            def high_tile(j, b, per, hid, used, high):
                wait(act, s[hid], b, per, j + 1)
                i, before = slot(j, per)
                wait(act, s[used], b, per, before + 1)
                nc.scalar.activation(HH[i][:, :], HB[i][:, :], ACT.Copy).then_inc(s[high], 1)

            def modulate(layer, which, b, bank):
                side = 0 if which == "attn" else 1
                m = L[layer][which]
                wait(act, mod_cols_in[layer][side], b, 1, 1)
                wait(act, m["xnT"], b, 1, 1)
                if which == "ffn":
                    wait(act, m["hT_split"], b, 2, 0)
                for k in range(KC):
                    ins = nc.scalar.activation(HTT[side][:, k, :], bank[:, k * T:(k + 1) * T], ACT.Identity,
                                               scale=MB_[side][:, 2 + k:3 + k], bias=MB_[side][:, k:k + 1])
                ins.then_inc(m["hT"], 1)

            def high_qk(b, c):
                rows = P if c < 2 else 64
                wait(act, s["qk_rot"], b, 3, {2: 1, 0: 2, 1: 3}[c])
                nc.scalar.activation(QH[0:rows, c, :], QR[0:rows, c, :], ACT.Copy).then_inc(s["qk_high"], 1)

            def start0(b):
                high_qk(b, 2)
                wait(act, s["v_ps"], b, 1, 1)
                nc.scalar.activation(VA[:, :, :, 0:DH], B_V[:, 0:2 * 64].rearrange("p (t g d) -> p t g d", t=TT, g=KV),
                                     ACT.Copy).then_inc(s["v_done"], 1)

            def turn0(ia, jf, nxt):
                b = ia

                def tanh(j):
                    if jf is not None:
                        tanh0(jf, j)

                def high(j):
                    if jf is not None:
                        high_tile(j, jf, HT, "hid0", "down0_used", "high0")

                def evac_qst(m):
                    wait(act, s["qst_ps"], b, 4, m + 1)
                    half = slice(0, 2) if m % 2 == 0 else slice(2, 4)
                    nc.scalar.activation(QST[:, m // 2, half, :].rearrange("p r t -> p (r t)"), B_QST[m],
                                         ACT.Copy).then_inc(s["qst_act"], 1)

                def evac_nmT(c):
                    wait(act, s["nmT_ps"], b, 2, c + 1)
                    wait(act, rows_in[c], b, 32, 0)
                    nc.scalar.activation(NMT[:, c, :], B_NMT[0:32, 0:T], ACT.Copy).then_inc(s["nmT_done"], 1)

                if ia is not None:
                    high_qk(b, 0)
                    wait(act, s["kst_ps"], b, 1, 1)
                    nc.scalar.activation(KST[:, :, :].rearrange("p c t -> p (c t)"), B_KST, ACT.Identity,
                                         bias=ones24).then_inc(s["kst_done"], 1)
                if jf is not None:
                    modulate(0, "ffn", jf, GUP[1])
                    split_hT(0, jf)
                if ia is not None:
                    high_qk(b, 1)
                    evac_qst(0)
                    evac_qst(1)
                    if isinstance(b, int) and b == 0:
                        act.wait_ge(ld_w13, 16)
                        nc.scalar.activation(W13H[:, :, :, :], W13RAW[:, :, :, :], ACT.Copy).then_inc(w13_split, 1)
                    tanh(0)
                    evac_qst(2)
                    tanh(1)
                    high(0)
                    evac_qst(3)
                    tanh(2)
                    high(1)
                    high(2)
                    evac_nmT(0)
                    tanh(3)
                    if isinstance(b, int) and b == 0:
                        act.wait_ge(gates_stored, 32)
                        act.wait_ge(consts_ready, 1)
                    for g in range(KV):
                        wait(act, s["pv_ps"], b, KV, g - 1)
                        wait(act, s["st_ps"], b, 2 * KV, 2 * g + 1)
                        nc.scalar.activation(PR[g % 2][:, 0:4 * T], SPA, ACT.Exp, scale=SC0).then_inc(s["exp_done"], 1)
                        if g == 0:
                            high(3)
                            tanh(4)
                        wait(act, s["st_ps"], b, 2 * KV, 2 * g + 2)
                        nc.scalar.activation(PR[g % 2][:, 4 * T:6 * T], SPB, ACT.Exp, scale=SC0).then_inc(s["exp_done"], 1)
                        if g == 0:
                            evac_nmT(1)
                        for what, j in ACT0_CTX.get(g, ()):
                            (tanh if what == "tanh" else high)(j)
                    if nxt is not None:
                        modulate(0, "attn", nxt, B_XNT)
                    tanh(7)
                    wait(act, s["ctxT_ps"], b, 1, 1)
                    nc.scalar.activation(CXT.rearrange("p k t -> p (k t)"), B_CTXT, ACT.Copy)\
                        .then_inc(s["ctxT_done"], 1)
                    if isinstance(b, int) and b == 0:
                        act.wait_ge(wo1_ps, 1)
                        nc.scalar.activation(WO1[:, :], FO[:, 0:D], ACT.Copy).then_inc(wo1_done, 1)
                    high(7)
                    if nxt is not None:
                        start0(nxt)

            modulate(0, "attn", 0, B_XNT)
            high_weights()
            act.wait_ge(consts_ready, 1)
            start0(0)
            layer0_turns(act, turn0)


            def tanh1(b, j):
                bank, _ = bank1(j)
                wait(act, s["gu1_ps"], b, MT, j + 1)
                i, before = slot(j, MT)
                wait(act, s["low1"], b, MT, before + 1)
                nc.scalar.activation(HB[i][:, :], bank[:, 0:T], ACT.Tanh, scale=0.5).then_inc(s["tanh1"], 1)

            def chain(what, b):
                if what == "modulate":
                    modulate(1, "attn", b, ring[0])
                if what == "modulate2":
                    modulate(1, "ffn", b, ring[1])
                if what == "kv":
                    wait(act, s["kv1_ps"], b, 1, 1)
                    nc.scalar.activation(KT1, ring[1][:, 0:T], ACT.Identity, bias=BC1[:, 0:1]).then_inc(s["kv1_done"], 1)
                    nc.scalar.activation(VT1, ring[1][:, T:2 * T], ACT.Identity, bias=BC1[:, 1:2]).then_inc(s["kv1_done"], 1)
                if what == "v":
                    wait(act, s["v1T_ps"], b, 1, 1)
                    nc.scalar.activation(V1.rearrange("p i d -> p (i d)"), ring[2][:, 0:T], ACT.Copy).then_inc(s["v1_done"], 1)
                if what == "exp":
                    wait(act, s["nmb1"], b, 1, 1)
                    for tt in range(TT):
                        nc.scalar.activation(P1[:, tt, :], ring[0][:, tt * T:(tt + 1) * T], ACT.Exp, scale=SC1,
                                             bias=NMB1[:, tt:tt + 1], accum_out=DEN1[:, tt:tt + 1]).then_inc(s["exp1"], 1)
                if what == "probsT":
                    wait(act, s["pT1_ps"], b, 1, 1)
                    nc.scalar.activation(PT1[:, :, :].rearrange("p i t -> p (i t)"), ring[2], ACT.Copy).then_inc(s["pT1_done"], 1)
                if what == "ctx":
                    wait(act, s["o1_ps"], b, 1, 1)
                    nc.scalar.activation(OT1, ring[1][:, 0:T], ACT.Copy).then_inc(s["o1_done"], 1)
                if what == "route":
                    wait(act, s["lmax"], b, 1, 1)
                    for tt in range(TT):
                        nc.scalar.activation(SE[:, tt, :], ring[2][:, tt * EXP:(tt + 1) * EXP], ACT.Exp, bias=LMX[:, tt:tt + 1],
                                             accum_out=ZZ[:, tt:tt + 1]).then_inc(s["lexp"], 1)

            modulate(0, "ffn", NB - 1, GUP[1])
            split_hT(0, NB - 1)
            tanh0(NB - 1, 0)
            for i in range(3 * HT):
                j = i // 3
                if i % 3 == 1 and j + 1 < HT:
                    tanh0(NB - 1, j + 1)
                if i % 3 == 2:
                    high_tile(j, NB - 1, HT, "hid0", "down0_used", "high0")
                chain(STEPS_ACT.get(i), 0)
            act.wait_ge(s["gu0_ps"], NB * HT)
            split_hT(1, 0)
            act.wait_ge(L[0]["ffn"]["x_done"], NB)

            def turn1(ia, jf, prev):
                if jf is not None:
                    tanh1(jf, 0)
                    wait(act, s["cT_ps"], jf, 1, 1)
                    if prev is not None:
                        wait(act, s["cb_ps"], prev, MT, MT)
                    nc.scalar.activation(CTT[:, :], ring[0].bitcast(BF16)[0:3 * NC, 0:T], ACT.Copy).then_inc(s["cT_done"], 1)
                for j in range(MT - 1):
                    if jf is not None:
                        tanh1(jf, j + 1)
                        if j == MT - 2 and ia is not None:
                            wait(act, s["gu1_ps"], jf, MT, MT)
                            split_hT(1, ia)
                        high_tile(j, jf, MT, "hid1", "down1_used", "high1")
                    if ia is not None:
                        chain(STEPS_ACT.get(j), ia)
                    n = late_at(jf, j)
                    if n is not None:
                        lot = max(i for i in range(len(ld_late)) if LOTS[i] <= n)
                        act.wait_ge(ld_late[lot], 32 if lot == 1 else 16)
                        nc.scalar.activation(WHI_B[:, n, :], RAW_B[:, n, :], ACT.Copy).then_inc(late_high, 1)
                if jf is not None:
                    high_tile(MT - 1, jf, MT, "hid1", "down1_used", "high1")

            layer1_turns(act, turn1)

        @block.vector
        def _(dve):
            n_ = [0]

            def step(ins):
                n_[0] += 1
                ins.then_inc(dve_setup, 1)
                dve.wait_ge(dve_setup, n_[0])

            dve.wait_ge(act_setup, 1)
            step(dve.scalar_tensor_tensor(CS[:, :, :, :].rearrange("p l k b -> p (l k b)"),
                                          CS[:, :, :, :].rearrange("p l k b -> p (l k b)"), 1.0,
                                          CT[:, :, :, :].rearrange("p l k b -> p (l k b)"), ALU.add, ALU.mult))
            dve.tensor_scalar(CS[:, :, :, :], CS[:, :, :, :], 0.5, None, ALU.mult).then_inc(cs_ready, 1)

            norm_steps = {(l, w): Steps(ch[f"dve_n{w[0]}"], 1, l * NB) for l in (0, 1) for w in ("attn", "ffn")}

            def mean(layer, which, b):
                side = 0 if which == "attn" else 1
                m = L[layer][which]
                st = norm_steps[layer, which]
                st.start(b)
                if not (layer == 0 and which == "attn" and isinstance(b, int) and b == 0):
                    shifts(layer, which, b)
                if which == "ffn":
                    wait(dve, L[layer]["attn"]["x_done"], b, 1, 1)
                elif layer == 1:
                    wait(dve, L[0]["ffn"]["x_done"], b, 1, 1)
                stand(dve, turns["dve"])
                for tt in range(TT):
                    ins = dve.bn_stats(ST[side][:, tt, :], xtile(b, tt))
                st(dve, ins)
                stand(dve, turns["dve"])
                dve.bn_aggr(MV[side][:, 0, :], ST[side][:, 0, :])
                dve.bn_aggr(MV[side][:, 1, :], ST[side][:, 1, :]).then_inc(m["mv"], 1)

            def norm(layer, which, b):
                side = 0 if which == "attn" else 1
                m = L[layer][which]
                wait(dve, m["mv"], b, 1, 1)
                wait(dve, m["rstd"], b, 1, 1)
                wait(dve, m["xnT"], b, 1, 0)
                for tt in range(TT):
                    ins = dve.tensor_scalar(XN[side][:, tt, :], xtile(b, tt), MV[side][:, tt, 0:1],
                                            RS[side][:, tt:tt + 1], ALU.subtract, ALU.mult)
                ins.then_inc(m["xn"], 1)

            def low_hT(layer, b):
                m = L[layer]["ffn"]
                wait(dve, m["hT_split"], b, 2, 1)
                dve.tensor_tensor(HFL[:, :, :], HTT[1][:, :, :], HFH[:, :, :].bitcast(F32), ALU.subtract)\
                    .then_inc(m["hT_split"], 1)

            def shifts(layer, which, b):
                side = 0 if which == "attn" else 1
                mc = MODC[:, layer, b:b + 1, 4 * side:4 * side + 4] if isinstance(b, int) else \
                    MODC[:, layer, bass.ds(b, 1), 4 * side:4 * side + 4]
                wait(dve, L[layer][which]["hT"], b, 1, 0)
                dve.tensor_copy(MB_[side][:, :], mc.rearrange("p a c -> p (a c)")).then_inc(mod_cols_in[layer][side], 1)

            def residual(layer, which, b, ps, Y, st, filled, per, read, bias=None):
                m = L[layer][which]
                g = spread(GB_[0 if which == "attn" else 1][:, :].rearrange("p (a d) -> p a d", a=1), 1, TT)
                wait(dve, s[filled], b, per, per)
                wait(dve, m["gate_in"], b, 16, 16)
                src = ps.rearrange("p (t d) -> p t d", t=TT)
                if bias is not None:
                    dve.tensor_tensor(Y, src, spread(bias[:, :].rearrange("p (a d) -> p a d", a=1), 1, TT),
                                      ALU.add).then_inc(s[read], 1)
                    wait(dve, s[read], b, 1, 1)
                    st(dve, dve.tensor_tensor(Y, Y, g, ALU.mult))
                else:
                    dve.tensor_tensor(Y, src, g, ALU.mult).then_inc(s[read], 1)
                    wait(dve, s[read], b, 1, 1)
                dve.tensor_tensor(xboth(b), xboth(b), Y, ALU.add).then_inc(m["x_done"], 1)

            def ffn_residual(layer, b, Y, used, per, read, half):
                m = L[layer]["ffn"]
                if half != 1:
                    wait(dve, s[used], b, per, per)
                    wait(dve, m["gate_in"], b, 16, 16)
                    dve.tensor_tensor(Y, FO.rearrange("p (t d) -> p t d", t=TT),
                                      spread(GB_[1][:, :].rearrange("p (a d) -> p a d", a=1), 1, TT), ALU.mult)\
                        .then_inc(s[read], 1)
                if half != 0:
                    wait(dve, s[read], b, 1, 1)
                    dve.tensor_tensor(xboth(b), xboth(b), Y, ALU.add).then_inc(m["x_done"], 1)

            def mod_rows(l, c):
                dve.wait_ge(mod_ps, 3 * l + c + 1)
                if l == 1 and c == 0:
                    dve.wait_ge(modT_ps, 1)
                dve.tensor_copy(MODR[:, c * 512:(c + 1) * 512], B_MOD[l][c][0:NB, :]).then_inc(mod_sb, 1)

            def mod_cols(l):
                dve.wait_ge(mod_sb, 3 * l + 3)
                dve.wait_ge(modT_ps, l + 1)
                mt = B_MODT[l][:, 0:64].rearrange("p (a s k b) -> p a s k b", a=2, s=2, k=KC)
                mc = MODC[:, l, :, :].rearrange("p b (a s k) -> p a s k b", a=2, s=2)
                for a in range(2):
                    dve.tensor_copy(mc[:, a, 0, :, :], mt[:, a, 0, :, :])
                    ins = dve.tensor_scalar(mc[:, a, 1, :, :], mt[:, a, 1, :, :], 1.0, None, ALU.add)
                ins.then_inc(modc_ready, 1)
                if l == 0:
                    dve.wait_ge(modc_ready, 1)
                    shifts(0, "attn", 0)

            def gates(l):
                g = MODR[:, :].rearrange("p (a c d) -> p a c d", a=2, c=3)[:, :, 2, :]
                step(dve.scalar_tensor_tensor(GT[:, :, :], g, -1.0, g, ALU.mult, ALU.max))
                step(dve.tensor_scalar(GT[:, :, :], GT[:, :, :], 0.25, None, ALU.max))
                if l == 1:
                    dve.wait_ge(gates_stored, 16)
                step(dve.tensor_scalar(GR[:, :, :], g, 0.0, 2.0, ALU.is_ge, ALU.mult))
                step(dve.tensor_scalar(GR[:, :, :], GR[:, :, :], -1.0, None, ALU.add))
                dve.tensor_tensor(GR[:, :, :], GR[:, :, :], GT[:, :, :], ALU.mult).then_inc(gr_ready, 1)

            dve.wait_ge(ld_x, 32)
            mean(0, "attn", 0)
            norm(0, "attn", 0)
            for c in range(3):
                mod_rows(0, c)
            mod_cols(0)
            dve.wait_ge(ld_consts, 32)
            dve.tensor_copy(mask_b[:, :], CON[:, C_MASK:C_MASK + P])
            dve.tensor_copy(IDB[:, :], ident)
            step(dve.memset(VA[:, :, :, :], 0.0))
            dve.memset(VA[:, :, :, DH:DH + 1], 1.0).then_inc(consts_ready, 1)
            dve.wait_ge(w2_ping, 1)
            for h, src, dst in ((1, W2PING, W2RAW), (2, W2RAW, W2PING), (4, W2PING, W2F[:, :, :])):
                v = src.rearrange("p (n s h) d -> p n s (h d)", s=2, h=h)
                o = dst.rearrange("p (n s h) d -> p n s (h d)", s=2, h=h)
                dve.tensor_tensor(o[:, :, 0, :], v[:, :, 0, :], v[:, :, 1, :], ALU.add)
                ins = dve.tensor_tensor(o[:, :, 1, :], v[:, :, 0, :], v[:, :, 1, :], ALU.subtract)
                if h < 4:
                    step(ins)
                else:
                    ins.then_inc(w2_done, 1)

            a0 = Steps(ch["dve_a0"], 2 + 4)
            f0 = Steps(ch["dve_f0"], HT)

            def rotate(b, c):
                rows, n = (P if c < 2 else 64), {2: 1, 0: 2, 1: 3}[c]
                ps = (B_Q[c] if c < 2 else B_K)[0:rows, :]
                if c < 2:
                    wait(dve, s["q_ps"], b, 2, c + 1)
                else:
                    wait(dve, s["k_ps"], b, 1, 1)
                wait(dve, s["qk_rot"], b, 3, n - 1)
                dve.tensor_tensor(RT[0:rows, 0, :], ps[:, 0:T], cosT[0:rows, :], ALU.mult)
                dve.tensor_tensor(RT[0:rows, 1, :], ps[:, T:2 * T], sinT[0:rows, :], ALU.mult).then_inc(s["rope_done"], 1)
                wait(dve, s["rope_done"], b, 3, n)
                dve.tensor_tensor(QR[0:rows, c, :], RT[0:rows, 0, :], RT[0:rows, 1, :], ALU.add).then_inc(s["qk_rot"], 1)

            def low_qk(b, c):
                rows = P if c < 2 else 64
                wait(dve, s["qk_high"], b, 3, {2: 1, 0: 2, 1: 3}[c])
                dve.tensor_tensor(QL[0:rows, c, :], QR[0:rows, c, :], QH[0:rows, c, :].bitcast(F32),
                                  ALU.subtract).then_inc(s["qk_split"], 1)

            def start0(b):
                rotate(b, 2)
                low_qk(b, 2)

            def hidden0(b, j):
                wait(dve, s["tanh0"], b, HT, j + 1)
                hid = HB[slot(j, HT)[0]][:, :]
                f0(dve, dve.scalar_tensor_tensor(hid, hid, 1.0, GUP[j % 2][:, 0:T], ALU.add, ALU.mult))
                dve.tensor_tensor(hid, hid, GUP[j % 2][:, T:2 * T], ALU.mult).then_inc(s["hid0"], 1)

            def residual0(b, half=None):
                ffn_residual(0, b, RT[:, :, :], "down0_used", HT, "ffn0_read", half)

            def turn0(ia, jf, nxt):
                b, prev = ia, before(jf)

                def tile(j):
                    if jf is not None:
                        hidden0(jf, j)

                def maxima(g):
                    c, gg = g // 4, g % 4
                    for u in range(3):
                        n = 3 * g + u
                        wait(dve, s["s_ps"], b, 3 * KV, n + 1)
                        to = NM[:, 0, c, gg, :] if u == 0 else NM[:, 1, c, gg, 2 * u - 2:2 * u]
                        dve.tensor_reduce(to, B_MAX[n % 4].rearrange("p (r t) -> p r t", r=REP if u == 0 else 2),
                                          AX.X, ALU.max, negate=True).then_inc(s["max_done"], 1)

                def split_maxima(c):
                    wait(dve, s["max_done"], b, 3 * KV, 12 * c + 12)
                    wait(dve, s["nmT_ps"], b, 2, c)
                    nm = NM[:, :, c, :, :]
                    a0(dve, dve.tensor_copy(NMS[:, :, c, 0, :, :], nm))
                    dve.tensor_tensor(NMS[:, :, c, 1, :, :], nm, NMS[:, :, c, 0, :, :].bitcast(F32), ALU.subtract)\
                        .then_inc(s["nm_split"], 1)

                if jf is not None:
                    f0.start(jf)
                    mean(0, "ffn", jf)
                if ia is not None:
                    a0.start(b)
                    rotate(b, 0)
                    if jf is not None:
                        norm(0, "ffn", jf)
                    low_qk(b, 0)
                    rotate(b, 1)
                    if jf is not None:
                        low_hT(0, jf)
                    low_qk(b, 1)
                    if isinstance(b, int) and b == 0:
                        gates(0)
                    for g in range(KV):
                        maxima(g)
                        if isinstance(b, int) and b == 0:
                            if g < 3:
                                mod_rows(1, g)
                            if g == 3:
                                mod_cols(1)
                                gates(1)
                        if g == 3:
                            split_maxima(0)
                        if g == KV - 1:
                            split_maxima(1)
                        if g in DVE0:
                            tile(DVE0[g])
                        if g == 2 and prev is not None:
                            residual0(prev, 0)
                    if isinstance(b, int) and b == 0:
                        dve.wait_ge(w2_split, 2)
                    tile(4)
                    if prev is not None:
                        residual0(prev, 1)

                    def contexts(n):
                        tt, q = n % 2, n // 2
                        wait(dve, s["oT_ps"], b, 4, n + 1)
                        v = B_OT[n].rearrange("p (g r e) -> p g r e", g=4, r=REP)
                        rd = RD[:, tt, 4 * q:4 * q + 4, :]
                        a0(dve, dve.reciprocal(rd, v[:, :, :, DH]))
                        for g in range(4):
                            ins = dve.tensor_tensor(
                                CX[:, tt, (4 * q + g) * 32:(4 * q + g + 1) * 32].rearrange("p (r d) -> p r d", r=REP),
                                v[:, g, :, 0:DH],
                                spread(rd[:, g, :].rearrange("p (r o) -> p r o", o=1), 2, DH), ALU.mult)
                        ins.then_inc(s["ctx_done"], 1)

                    for g in range(KV):
                        if g == KV - 1:
                            contexts(0)
                            contexts(1)
                        wait(dve, s["pv_ps"], b, KV, g + 1)
                        dve.tensor_copy(OS[:, g, :], CTX[g % 2][:, 0:T]).then_inc(s["o_done"], 1)
                        if g in DVE0_CTX:
                            tile(DVE0_CTX[g])
                        if g == 1 and nxt is not None:
                            if isinstance(nxt, int) and nxt == 1:
                                dve.wait_ge(ld_rest, 112)
                            mean(0, "attn", nxt)
                        if g == 5 and nxt is not None:
                            norm(0, "attn", nxt)
                    contexts(2)
                    contexts(3)
                    tile(7)
                    if nxt is not None:
                        if prev is not None:
                            wait(dve, L[0]["ffn"]["x_done"], prev, 1, 1)
                        start0(nxt)
                    residual(0, "attn", b, B_WO, XN[0][:, :, :], None, "wo_ps", 1, "wo_read")

            start0(0)
            layer0_turns(dve, turn0)

            a1 = Steps(ch["dve_a1"], 3)
            r1 = Steps(ch["dve_r1"], 14)
            step(dve.memset(S18[:, :, :], -1.0))
            step(dve.memset(CW[:, :, :], 0.5))

            def gated1(b, j):
                if j < MT:
                    bank, _ = bank1(j)
                    wait(dve, s["tanh1"], b, MT, j + 1)
                    hid = HB[slot(j, MT)[0]][:, :]
                    dve.scalar_tensor_tensor(hid, hid, 1.0, bank[:, 0:T], ALU.add, ALU.mult)\
                        .then_inc(s["act1"], 1)
                if j > 0:
                    wait(dve, s["gated1"], b, MT, j)
                    wait(dve, s["cb_ps"], b, MT, j)
                    last = HB[slot(j - 1, MT)[0]][:, :]
                    dve.tensor_tensor(last, last, CB[:, 0:T], ALU.mult)\
                        .then_inc(s["hid1"], 1)
                if j < MT:
                    wait(dve, s["act1"], b, MT, j + 1)
                    dve.tensor_tensor(hid, hid, bank[:, T:2 * T], ALU.mult)\
                        .then_inc(s["gated1"], 1)

            def max2(b):
                wait(dve, s["lg_ps"], b, 1, 1)
                dve.tensor_reduce(LMX[:, :], ring[2][:, 0:TT * EXP].rearrange("p (t e) -> p t e", t=TT), AX.X, ALU.max,
                                  negate=True).then_inc(s["lmax"], 1)

            def route(b, st):
                st.start(b)
                wait(dve, s["lexp"], b, TT, TT)
                st(dve, dve.reciprocal(RZ[:, :], ZZ[:, :]))
                for tt in range(TT):
                    ins = dve.tensor_scalar(S18[:, tt, 0:EXP], SE[:, tt, :], RZ[:, tt:tt + 1], None, ALU.mult)
                st(dve, ins)
                stand(dve, turns["dve"])
                for tt in range(TT):
                    ins = dve.max(M8[:, tt, :], S18[:, tt, 0:EXP])
                st(dve, ins)

            def route2(b, st):
                st(dve, dve.memset(M8[:, :, TOPK:8], -1.0))
                stand(dve, turns["dve"])
                for tt in range(TT):
                    ins = dve.match_replace(RP[:, tt, :], M8[:, tt, :], S18[:, tt, :], 0.0)
                st(dve, ins)
                st(dve, dve.tensor_tensor(CW[:, :, 0:EXP], S18[:, :, 0:EXP], RP[:, :, 0:EXP], ALU.subtract))
                st(dve, dve.tensor_reduce(WS[:, :], CW[:, :, 0:EXP], AX.X, ALU.add))
                st(dve, dve.tensor_scalar(WS[:, :], WS[:, :], 1e-20, None, ALU.add))
                st(dve, dve.reciprocal(WS[:, :], WS[:, :]))
                for tt in range(TT):
                    ins = dve.tensor_scalar(CW[:, tt, 0:EXP], CW[:, tt, 0:EXP], WS[:, tt:tt + 1], 0.5, ALU.mult, ALU.mult)
                st(dve, ins)
                wait(dve, s["cT_ps"], b, 1, 0)
                st(dve, dve.tensor_copy(CSP[:, :, 0, :], CW[:, :, :]))
                st(dve, dve.tensor_tensor(CW2[:, :, :], CW[:, :, :], CSP[:, :, 0, :], ALU.subtract))
                st(dve, dve.tensor_copy(CSP[:, :, 1, :], CW2[:, :, :]))
                st(dve, dve.tensor_tensor(CW2[:, :, :], CW2[:, :, :], CSP[:, :, 1, :], ALU.subtract))
                dve.tensor_copy(CSP[:, :, 2, :], CW2[:, :, :]).then_inc(s["csplit"], 1)

            def chain(what, b):
                if what == "mean":
                    a1.start(b)
                    mean(1, "attn", b)
                if what == "norm":
                    norm(1, "attn", b)
                if what == "max":
                    wait(dve, s["s1_ps"], b, 1, 1)
                    a1(dve, dve.tensor_reduce(NM1, ring[0].rearrange("p (t i) -> p t i", t=TT), AX.X, ALU.max, negate=True))
                    dve.tensor_scalar(NMB1, NM1, SC1, None, ALU.mult).then_inc(s["nmb1"], 1)
                if what == "softmax":
                    wait(dve, s["exp1"], b, TT, TT)
                    a1(dve, dve.reciprocal(RDN1, DEN1))
                    for tt in range(TT):
                        ins = dve.tensor_scalar(P1[:, tt, :], P1[:, tt, :], RDN1[:, tt:tt + 1], None, ALU.mult)
                    ins.then_inc(s["p1_norm"], 1)
                if what == "wo":
                    residual(1, "attn", b, ring[0], XN[0][:, :, :], a1, "wo1_ps", 1, "wo1_read", bias=BO1)
                if what == "mean2":
                    mean(1, "ffn", b)
                if what == "norm2":
                    norm(1, "ffn", b)
                if what == "max2":
                    max2(b)
                if what == "route":
                    route(b, r1)

            def residual1(b, half=None):
                ffn_residual(1, b, XN[1][:, :, :], "down1_used", MT, "ffn1_read", half)

            f0.start(NB - 1)
            mean(0, "ffn", NB - 1)
            norm(0, "ffn", NB - 1)
            residual0(NB - 2)
            low_hT(0, NB - 1)
            for i in range(3 * HT):
                if i % 3 == 1:
                    hidden0(NB - 1, i // 3)
                chain(STEPS_DVE.get(i), 0)
            low_hT(1, 0)
            route2(0, r1)
            residual0(NB - 1)

            def turn1(ia, jf, prev):
                if jf is not None:
                    gated1(jf, 0)
                for j in range(MT - 1):
                    if jf is not None:
                        gated1(jf, j + 1)
                    if prev is not None and j < 2:
                        residual1(prev, j)
                    if ia is not None:
                        chain(STEPS_DVE.get(j), ia)
                    n = late_at(jf, j)
                    if n is not None and n % 2 == 0:
                        dve.wait_ge(late_high, n + 1)
                        dve.tensor_tensor(WLO_B[:, n, :], RAW_B[:, n, :], WHI_B[:, n, :].bitcast(F32), ALU.subtract)\
                            .then_inc(late_low[0], 1)
                if ia is not None:
                    low_hT(1, ia)
                if jf is not None:
                    gated1(jf, MT)
                if ia is not None:
                    route2(ia, r1)

            layer1_turns(dve, turn1)
            residual1(NB - 1)

        @block.tensor
        def _(pe):
            mm = nc.tensor.matmul

            def xnT(layer, which, b, bank):
                side = 0 if which == "attn" else 1
                m = L[layer][which]
                wait(pe, m["xn"], b, 1, 1)
                for k in range(KC):
                    for tt in range(TT):
                        ins = nc.tensor.transpose(bank[:, k * T + tt * P:k * T + (tt + 1) * P],
                                                  XN[side][:, tt, k * P:(k + 1) * P], ident)
                ins.then_inc(m["xnT"], 1)

            def product3(out, terms, low_ready=None):
                first = True
                for mi, wi in ((0, 0), (0, 1), (1, 0)):
                    if mi == 1 and low_ready is not None:
                        low_ready()
                    for n, (w, m) in enumerate(terms):
                        last = mi == 1 and n == len(terms) - 1
                        ins = mm(out, w[wi], m[mi], start=first, stop=last)
                        first = False
                return ins

            def mod_rows(l, c):
                for k in range(KC):
                    ins = mm(B_MOD[l][c][0:NB, :], CS[:, l, k, :], WMOD[:, l, k, c * 512:(c + 1) * 512],
                             start=(k == 0), stop=(k == KC - 1))
                ins.then_inc(mod_ps, 1)

            def mod_cols(l):
                pe.wait_ge(mod_sb, 3 * l + 3)
                for a in range(2):
                    for sc in range(2):
                        for k in range(KC):
                            col = (3 * a + sc) * D + k * P
                            at = ((a * 2 + sc) * KC + k) * NB
                            ins = nc.tensor.transpose(B_MODT[l][:, at:at + NB], MODR[:, col:col + P], ident[0:NB, 0:NB])
                ins.then_inc(modT_ps, 1)

            pe.wait_ge(cs_ready, 1)
            pe.wait_ge(ld_mod, 16)
            for c in range(3):
                mod_rows(0, c)
            pe.wait_ge(ld_consts, 32)
            mod_cols(0)
            xnT(0, "attn", 0, B_XNT)
            pe.wait_ge(ld_w2, 16)
            for a in range(HT):
                ins = mm(PS[:, 4 + a // 2, (a % 2) * D:(a % 2 + 1) * D], had, W2RAW[:, a, :], start=True, stop=True)
            ins.then_inc(w2_ps, 1)
            pe.wait_ge(ld_w0, 48)
            pe.wait_ge(w2_ping, 1)

            def gu0(b, j):
                if j == 0:
                    wait(pe, L[0]["ffn"]["hT_split"], b, 2, 1)
                    low = lambda: wait(pe, L[0]["ffn"]["hT_split"], b, 2, 2)
                else:
                    low = None
                wait(pe, s["hid0"], b, HT, j - 1)
                for h in range(2):
                    ins = product3(GUP[j % 2][:, h * T:(h + 1) * T],
                                   [((W13H[:, k, h, j * P:(j + 1) * P], W13L[:, k, h, j * P:(j + 1) * P]),
                                     (HFH[:, k, :], HFL[:, k, :])) for k in range(KC)], low)
                ins.then_inc(s["gu0_ps"], 1)

            def down(b, j, low, used, read, per, W):
                wait(pe, s[low], b, per, j + 1)
                if j == 0:
                    wait(pe, s[read], b, 1, 0)
                    if per == HT and isinstance(b, int) and b == 0:
                        pe.wait_ge(wo1_done, 1)
                for tt in range(TT):
                    for n, (hid, w) in enumerate(((HH, W[0]), (HH, W[1]), (HL, W[0]))):
                        ins = mm(FO[:, tt * D:(tt + 1) * D], hid[slot(j, per)[0]][:, tt * P:(tt + 1) * P], w,
                                 start=(j == 0 and tt == 0 and n == 0), stop=(j == per - 1 and n == 2),
                                 skip_group_check=True)
                ins.then_inc(s[used], 1)

            def proj_q(b, c):
                for h in range(2):
                    for k in range(KC):
                        ins = mm(B_Q[c][:, h * T:(h + 1) * T], WQ[:, k, h, c * P:(c + 1) * P], HTT[0][:, k, :],
                                 start=(k == 0), stop=(k == KC - 1))
                ins.then_inc(s["q_ps"], 1)

            def proj_k(b):
                wait(pe, L[0]["attn"]["hT"], b, 1, 1)
                for h in range(2):
                    for k in range(KC):
                        ins = mm(B_K[0:64, h * T:(h + 1) * T], WK[:, k, h, :], HTT[0][:, k, :],
                                 start=(k == 0), stop=(k == KC - 1))
                ins.then_inc(s["k_ps"], 1)

            def proj_v(b):
                if isinstance(b, int) and b == 0:
                    pe.wait_ge(modc_ready, 1)
                for tt in range(TT):
                    for k in range(KC):
                        ins = mm(B_V[:, tt * 64:(tt + 1) * 64], HTT[0][:, k, tt * P:(tt + 1) * P], WV[:, k, :],
                                 start=(k == 0), stop=(k == KC - 1))
                ins.then_inc(s["v_ps"], 1)

            def down0(b, j):
                down(b, j, "low0", "down0_used", "ffn0_read", HT, (W2HI[:, j, :], W2LO[:, j, :]))

            def turn0(ia, jf, nxt):
                b, prev = ia, before(jf)

                def parts(n):
                    if jf is not None:
                        for what, j in PE0.get(n, ()):
                            (gu0 if what == "gu" else down0)(jf, j)

                if isinstance(jf, int) and jf == 0:
                    pe.wait_ge(w13_split, 2)
                    pe.wait_ge(w2_split, 2)
                if ia is not None:
                    proj_q(b, 0)
                    proj_q(b, 1)
                    wait(pe, s["qk_split"], b, 3, 1)
                    if isinstance(b, int) and b == 0:
                        pe.wait_ge(act_setup, 2)
                        pe.wait_ge(consts_ready, 1)
                    for c in range(2):
                        for hl, src in enumerate((QH, QL)):
                            ins = mm(B_KST[:, c * T:(c + 1) * T], SELK[0:64, c, hl, :], src[0:64, 2, :],
                                     start=(hl == 0), stop=(hl == 1))
                    ins.then_inc(s["kst_ps"], 1)

                    def q_stack(m):
                        wait(pe, s["qk_split"], b, 3, 2 if m < 2 else 3)
                        if m == 0:
                            wait(pe, s["v_done"], b, 1, 1)
                        if m > 1:
                            wait(pe, s["qst_act"], b, 4, m)
                        for r2 in range(2):
                            for hl, src in enumerate((QH, QL)):
                                ins = mm(B_QST[m][:, r2 * T:(r2 + 1) * T], SELQ[:, 2 * (m % 2) + r2, hl, :],
                                         src[:, m // 2, :], start=(hl == 0), stop=(hl == 1))
                        ins.then_inc(s["qst_ps"], 1)

                    if prev is not None:
                        down0(prev, HT - 3)
                        down0(prev, HT - 2)
                    if jf is not None:
                        wait(pe, s["hid0"], jf, HT, 0)
                        xnT(0, "ffn", jf, GUP[1])
                    if prev is not None:
                        down0(prev, HT - 1)
                    q_stack(0)
                    q_stack(1)
                    if jf is not None:
                        gu0(jf, 0)
                    mk = mask_b[:, :].rearrange("p (a s) -> p a s", a=1)

                    def scores(g):
                        c, R = g // 4, slice(32 * (g % 4), 32 * (g % 4) + 3 * DH)
                        if g % 4 == 0:
                            wait(pe, s["qst_act"], b, 4, 2 + 2 * c)
                        for u in range(3):
                            n = 3 * g + u
                            if n == 0:
                                wait(pe, s["kst_done"], b, 1, 1)
                            elif n == 2:
                                wait(pe, s["wo_read"], b, 1, 0)
                            elif n == 3:
                                wait(pe, s["rope_done"], b, 3, 3)
                            elif n > 3:
                                wait(pe, s["max_done"], b, 3 * KV, n - 3)
                            bank = B_MAX[n % 4]
                            if u == 0:
                                mm(bank.rearrange("p (r t) -> p r t", r=REP), IDB[:, :], spread(mk, 1, REP), start=True,
                                   stop=False, skip_group_check=True)
                                for r in range(REP):
                                    ins = mm(bank[:, r * P:(r + 1) * P], QST[R, c, r, 0:P], KST[R, c, 0:P], start=False,
                                             stop=True, skip_group_check=True)
                            else:
                                mm(bank.rearrange("p (r t) -> p r t", r=2)[:, :, P:T], IDB[:, :], spread(mk, 1, 2),
                                   start=True, stop=False, skip_group_check=True)
                                for r in range(2):
                                    ins = mm(bank[:, r * T:(r + 1) * T], QST[R, c, 2 * u - 2 + r, P:T], KST[R, c, :],
                                             start=False, stop=True, skip_group_check=True)
                            ins.then_inc(s["s_ps"], 1)

                    def maxT(c):
                        wait(pe, s["nm_split"], b, 2, c + 1)
                        if c == 0:
                            wait(pe, s["qst_act"], b, 4, 4)
                        else:
                            wait(pe, s["nmT_done"], b, 2, 1)
                        stand(pe, turns["pe"])
                        for tt in range(TT):
                            ins = nc.tensor.transpose(B_NMT[0:32, tt * P:(tt + 1) * P],
                                                      NMS[:, tt, c, :, :, :].rearrange("p h g r -> p (h g r)").bitcast(F32), ident)
                        ins.then_inc(s["nmT_ps"], 1)

                    for g in range(KV):
                        scores(g)
                        parts(g)
                        if isinstance(b, int) and b == 0:
                            if g == 0:
                                pe.wait_ge(ld_mod1, 16)
                            if g < 3:
                                mod_rows(1, g)
                            if g == 3:
                                mod_cols(1)
                        if g == 1:
                            q_stack(2)
                        if g == 2:
                            q_stack(3)
                        if g == 5:
                            maxT(0)

                    def pv(g):
                        wait(pe, s["masked"], b, 2 * KV, 2 * g + 2)
                        wait(pe, s["o_done"], b, KV, g - 1)
                        if g == 1:
                            wait(pe, s["nmT_done"], b, 2, 2)
                        o, pr = CTX[g % 2][:, 0:T], PR[g % 2]
                        for r in range(REP):
                            mm(o[32 * r:32 * r + 32, :], VA[:, 0, g, :], pr[:, r * T:(r + 1) * T], start=True, stop=False,
                               skip_group_check=True)
                        for r in range(REP):
                            ins = mm(o[32 * r:32 * r + 32, P:T], VA[:, 1, g, :], pr[:, 4 * T + r * P:4 * T + (r + 1) * P],
                                     start=False, stop=True, skip_group_check=True)
                        ins.then_inc(s["pv_ps"], 1)

                    for g in range(KV):
                        c, R = g // 4, slice(32 * (g % 4), 32 * (g % 4) + 3 * DH + 2)
                        if g == 0:
                            wait(pe, s["max_done"], b, 3 * KV, 3 * KV)
                        if g % 4 == 0:
                            wait(pe, rows_in[c], b, 32, 32)
                        wait(pe, s["exp_done"], b, 2 * KV, 2 * g - 1 if g else 0)
                        for i in range(2):
                            ins = mm(SPA[:, i * 512:(i + 1) * 512], KST[R, c, 0:P], QST[R, c, 2 * i:2 * i + 2, :],
                                     start=True, stop=True)
                        ins.then_inc(s["st_ps"], 1)
                        parts(KV + g)
                        wait(pe, s["exp_done"], b, 2 * KV, 2 * g)
                        mm(SPB, KST[R, c, P:T], QST[R, c, :, P:T], start=True, stop=True).then_inc(s["st_ps"], 1)
                        if g == 0:
                            maxT(1)
                        if g:
                            pv(g - 1)
                        if isinstance(b, int) and b == 0 and g >= KV // 2:
                            if g == KV // 2:
                                pe.wait_ge(ld_wo1, 16)
                            for h in range((g - KV // 2) * 4, (g - KV // 2) * 4 + 4):
                                ins = mm(FO[:, 0:D], ident, WO1RAW[:, h, :], start=(h == 0), stop=(h == HEADS1 - 1))
                            if h == HEADS1 - 1:
                                ins.then_inc(wo1_ps, 1)
                    if nxt is not None:
                        wait(pe, s["exp_done"], b, 2 * KV, 2 * KV - 1)
                        xnT(0, "attn", nxt, B_XNT)

                    def ctx_back(n):
                        tt, q = n % 2, n // 2
                        wait(pe, s["o_done"], b, KV, 4 * q + 4)
                        wait(pe, s["exp_done"], b, 2 * KV, 2 * KV)
                        for g in range(4):
                            ins = nc.tensor.transpose(B_OT[n][:, g * P:(g + 1) * P], OS[:, 4 * q + g, tt * P:(tt + 1) * P], ident)
                        ins.then_inc(s["oT_ps"], 1)

                    ctx_back(0)
                    ctx_back(1)
                    pv(KV - 1)
                    if jf is not None:
                        gu0(jf, HT - 1)
                    ctx_back(2)
                    ctx_back(3)
                    if nxt is not None:
                        if jf is not None:
                            wait(pe, s["hid0"], jf, HT, HT - 1)
                        proj_k(nxt)
                    wait(pe, s["ctx_done"], b, 4, 4)
                    for k in range(KC):
                        for tt in range(TT):
                            ins = nc.tensor.transpose(B_CTXT[:, k * T + tt * P:k * T + (tt + 1) * P],
                                                      CX[:, tt, k * P:(k + 1) * P], ident)
                    ins.then_inc(s["ctxT_ps"], 1)
                    if nxt is not None:
                        proj_v(nxt)
                    if isinstance(b, int) and b == 0:
                        pe.wait_ge(ld_rest, 112)
                    wait(pe, s["ctxT_done"], b, 1, 1)
                    for tt in range(TT):
                        for k in range(KC):
                            ins = mm(B_WO[:, tt * D:(tt + 1) * D], CXT[:, k, tt * P:(tt + 1) * P], WO[:, k, :],
                                     start=(k == 0), stop=(k == KC - 1))
                    ins.then_inc(s["wo_ps"], 1)

            proj_k(0)
            proj_v(0)
            layer0_turns(pe, turn0)

            def gu1(b, j):
                bank, before = bank1(j)
                wait(pe, s["gated1"], b, MT, before + 1)
                low = None
                if j == 0:
                    wait(pe, L[1]["ffn"]["hT_split"], b, 2, 1)
                    low = lambda: wait(pe, L[1]["ffn"]["hT_split"], b, 2, 2)
                if isinstance(b, int) and b == 0:
                    if j >= EARLY:
                        n = j - EARLY
                        pe.wait_ge(late_low[n % 2], n // 2 + 1)
                    else:
                        pe.wait_ge(early_done, 2 * j + 2)
                for h in range(2):
                    ins = product3(bank[:, h * T:(h + 1) * T],
                                   [(moe_tile(j, k, h, P), (HFH[:, k, :], HFL[:, k, :])) for k in range(KC)], low)
                ins.then_inc(s["gu1_ps"], 1)

            def cb(b, j):
                wait(pe, s["hid1"], b, MT, j)
                mm(CB[:, 0:T], SELC[:, j * P:(j + 1) * P], CTT[:, :], start=True, stop=True).then_inc(s["cb_ps"], 1)

            def down1(b, j):
                down(b, j, "low1", "down1_used", "ffn1_read", MT, moe_down(j, P))

            def chain(what, b):
                H = HTT[0]
                if what == "xnT":
                    wait(pe, s["wo1_read"], b, 1, 0)
                    xnT(1, "attn", b, ring[0])
                if what == "kv":
                    wait(pe, L[1]["attn"]["hT"], b, 1, 1)
                    wait(pe, L[1]["ffn"]["hT"], b, 1, 0)
                    for w, W in enumerate((WK1, WV1)):
                        for k in range(KC):
                            ins = mm(ring[1][:, w * T:(w + 1) * T], W[:, k, :], H[:, k, :], start=(k == 0), stop=(k == KC - 1))
                    ins.then_inc(s["kv1_ps"], 1)
                if what == "scores":
                    wait(pe, s["kv1_done"], b, 2, 2)
                    wait(pe, s["lexp"], b, TT, 0)
                    for i in range(TT):
                        ins = nc.tensor.transpose(ring[2][:, i * P:(i + 1) * P], VT1[:, i * P:(i + 1) * P], ident)
                    ins.then_inc(s["v1T_ps"], 1)
                    for tt in range(TT):
                        ins = mm(ring[0][:, tt * T:(tt + 1) * T], VT1[:, tt * P:(tt + 1) * P], KT1, start=True, stop=True)
                    ins.then_inc(s["s1_ps"], 1)
                if what == "probsT":
                    wait(pe, s["p1_norm"], b, 1, 1)
                    wait(pe, s["v1_done"], b, 1, 1)
                    for i in range(TT):
                        for tt in range(TT):
                            ins = nc.tensor.transpose(ring[2][:, i * T + tt * P:i * T + (tt + 1) * P],
                                                      P1[:, tt, i * P:(i + 1) * P], ident)
                    ins.then_inc(s["pT1_ps"], 1)
                if what == "ctx":
                    wait(pe, s["pT1_done"], b, 1, 1)
                    for i in range(TT):
                        ins = mm(ring[1][:, 0:T], V1[:, i, :], PT1[:, i, :], start=(i == 0), stop=(i == TT - 1))
                    ins.then_inc(s["o1_ps"], 1)
                if what == "wo":
                    wait(pe, s["o1_done"], b, 1, 1)
                    for tt in range(TT):
                        ins = mm(ring[0][:, tt * D:(tt + 1) * D], OT1[:, tt * P:(tt + 1) * P], WO1[:, :], start=True, stop=True)
                    ins.then_inc(s["wo1_ps"], 1)
                if what == "xnT2":
                    xnT(1, "ffn", b, ring[1])
                if what == "logits":
                    wait(pe, L[1]["ffn"]["hT"], b, 1, 1)
                    for tt in range(TT):
                        for k in range(KC):
                            ins = mm(ring[2][:, tt * EXP:(tt + 1) * EXP], HTT[1][:, k, tt * P:(tt + 1) * P], GW[:, k, :],
                                     start=(k == 0), stop=(k == KC - 1))
                    ins.then_inc(s["lg_ps"], 1)

            pe.wait_ge(wo1_done, 1)
            down0(NB - 2, HT - 3)
            down0(NB - 2, HT - 2)
            down0(NB - 2, HT - 1)
            xnT(0, "ffn", NB - 1, GUP[1])
            gu0(NB - 1, 0)
            pe.wait_ge(s["wo_read"], NB)
            for i in range(3 * HT):
                j = i // 3
                if i % 3 == 0 and j + 1 < HT:
                    gu0(NB - 1, j + 1)
                if i % 3 == 1 and j > 0:
                    down0(NB - 1, j - 1)
                chain(STEPS_PE.get(i), 0)
            down0(NB - 1, HT - 1)
            pe.wait_ge(ld_late[1], 32)

            def turn1(ia, jf, prev):
                if jf is not None:
                    gu1(jf, 0)
                if prev is not None:
                    down1(prev, MT - 2)
                    down1(prev, MT - 1)
                if jf is not None:
                    gu1(jf, 1)
                    wait(pe, s["csplit"], jf, 1, 1)
                    wait(pe, s["wo1_read"], jf, 1, 1)
                    stand(pe, turns["pe"])
                    for tt in range(TT):
                        ins = nc.tensor.transpose(ring[0].bitcast(BF16)[0:3 * NC, tt * P:(tt + 1) * P],
                                                  CSP[:, tt, :, :].rearrange("p h e -> p (h e)"), IDB[:, :])
                    ins.then_inc(s["cT_ps"], 1)
                    wait(pe, s["cT_done"], jf, 1, 1)
                    cb(jf, 0)
                for j in range(MT - 1):
                    if jf is not None:
                        if j + 2 < MT:
                            gu1(jf, j + 2)
                        if j > 0:
                            down1(jf, j - 1)
                        cb(jf, j + 1)
                    if ia is not None:
                        chain(STEPS_PE.get(j), ia)

            layer1_turns(pe, turn1)
            down1(NB - 1, MT - 2)
            down1(NB - 1, MT - 1)


def kernel(**inputs):
    import concourse.bacc as bacc
    from concourse.bass_utils import run_bass_kernel_spmd

    nc = bacc.Bacc("TRN2", target_bir_lowering=False, num_devices=1)
    a = {k: np.asarray(v) for k, v in inputs.items()}

    def swapped(w):
        w = w.reshape(D, -1, 2, DH // 2)
        return w[:, :, ::-1, :].reshape(D, -1)

    def half(which):
        rows = a["L1_ffn_w13"][:, which * INNER:(which + 1) * INNER, :].reshape(EXP * INNER, D)
        return np.concatenate([rows, a["L1_ffn_sw13"][which * SHARED:(which + 1) * SHARED]])

    def rows(*parts):
        w = np.stack(parts)
        return w.reshape(len(parts), -1, P, w.shape[-1]).transpose(2, 1, 0, 3)

    def one(w):
        return rows(w)[:, :, 0, :]

    def tiles(w):
        return np.concatenate([w, np.zeros((MT * P - MOE, D), w.dtype)]).reshape(MT, P, D)

    def halves(which):
        return tiles(half(which)).transpose(0, 2, 1).reshape(MT, KC, P, P).transpose(2, 0, 1, 3)

    down = tiles(np.concatenate([a["L1_ffn_w2"].transpose(0, 2, 1).reshape(EXP * INNER, D), a["L1_ffn_sw2"].T]))
    arrays = {
        "x": a["L0_attn_x"].reshape(NB * T, D),
        "consts": shape_constants(),
        "selrows": expert_rows(),
        "cT": rows(a["L0_c"].T, a["L1_c"].T).transpose(0, 2, 1, 3),
        "wmod": rows(a["L0_wmod"], a["L1_wmod"]).transpose(0, 2, 1, 3),
        "wq": rows(a["L0_attn_Wq"], swapped(a["L0_attn_Wq"])),
        "wk": rows(a["L0_attn_Wk"], swapped(a["L0_attn_Wk"])),
        "wv": one(a["L0_attn_Wv"]),
        "wo": one(a["L0_attn_Wo"]),
        "w13": rows(a["L0_ffn_W1"].T, a["L0_ffn_W3"].T),
        "w2": one(a["L0_ffn_W2"].T),
        "wk1": one(a["L1_attn_Wk"]),
        "wv1": one(a["L1_attn_Wv"]),
        "bcol1": np.stack([a["L1_attn_bk"], a["L1_attn_bv"]], axis=1),
        "wo1": one(a["L1_attn_Wo"]),
        "bo1": a["L1_attn_bo"],
        "gate": one(a["L1_ffn_gate_w"].T),
        "moe": np.concatenate([halves(0).reshape(P, MT, KC * P), halves(1).reshape(P, MT, KC * P),
                               down.transpose(1, 0, 2)], axis=2),
    }
    arrays = {f"in_{k}": np.ascontiguousarray(v) for k, v in arrays.items()}
    args = [nc.dram_tensor(k, v.shape, mybir.dt.from_np(v.dtype), kind="ExternalInput").ap() for k, v in arrays.items()]
    gate_rows = nc.dram_tensor("gate_rows", (2, NB, 2, D), F32, kind="Internal").ap()
    out = nc.dram_tensor("out_x", (NB * T, D), F32, kind="ExternalOutput").ap()
    adaln_two_layers(nc, *args, gate_rows, out)
    r = run_bass_kernel_spmd(nc, [arrays], core_ids=[0])
    return r.results[0]["out_x"].reshape(NB, T, D)
```
